# Optimizing a Trainium2 kernel written in Bass

```python
import numpy as np
import jax
import jax.numpy as jnp

def _softmax(x, axis=-1):
    return jax.nn.softmax(x, axis=axis)

def _gelu(x):
    return jax.nn.gelu(x, approximate=True)

def _silu(x):
    return jax.nn.silu(x)

def _sigmoid(x):
    return jax.nn.sigmoid(x)

def _layernorm(x, axis=-1, eps=1e-05):
    m = jnp.mean(x, axis=axis, keepdims=True)
    v = jnp.var(x, axis=axis, keepdims=True)
    return (x - m) / jnp.sqrt(v + eps)

def _scatter_add(tgt, idx, src, axis=0):
    return tgt.at[idx].add(src)

def _segment_sum(src, seg, n):
    return jax.ops.segment_sum(src, seg, n)
kernel_name = 'mk_recurrent_d2_jaxref_r4_c12e85'

def setup_inputs(seed: int=0):
    np.random.seed(seed)
    _w = jnp.asarray

    def _L0_attn_setup():
        import jax, jax.numpy as jnp
        import numpy as np
        B, S, E, H = (2, 512, 256, 8)
        DH = E // H
        F = DH // 2
        key = jax.random.key(seed)
        ks = jax.random.split(key, 7)
        sc = E ** (-0.5)
        return {'x': jax.random.normal(ks[0], (B, S, E), dtype=jnp.float32), 'Wq': jax.random.normal(ks[1], (E, E), dtype=jnp.float32) * sc, 'Wk': jax.random.normal(ks[2], (E, E), dtype=jnp.float32) * sc, 'Wv': jax.random.normal(ks[3], (E, E), dtype=jnp.float32) * sc, 'norm_w': jnp.ones((H, DH), dtype=jnp.float32), 'Wo': jax.random.normal(ks[4], (E, E), dtype=jnp.float32) * sc, 'bo': jnp.zeros((E,), dtype=jnp.float32), 'diff_weight': jnp.float32(0.2)}
    _L0_attn_in = _L0_attn_setup()

    def _L0_ffn_setup():
        import jax, jax.numpy as jnp
        import numpy as np
        E = 8
        TOP_K = 2
        R = 16
        ALPHA = 32.0
        SCALING = ALPHA / R
        key = jax.random.key(seed)
        k1, k2, k3, k4 = jax.random.split(key, 4)
        B, T, D_IN, D_OUT = (4, 1024, 256, 256)
        x = jax.random.normal(k1, (B, T, D_IN), dtype=jnp.float32)
        w_route = jax.random.normal(k2, (E, D_IN), dtype=jnp.float32) * 0.02
        compress = jax.random.normal(k3, (R, D_IN), dtype=jnp.float32) * 0.02
        routed = jax.random.normal(k4, (E, D_OUT, R), dtype=jnp.float32) * 0.02
        return {'x': x, 'w_route': w_route, 'compress': compress, 'routed': routed}
    _L0_ffn_in = _L0_ffn_setup()

    def _L1_attn_setup():
        import jax, jax.numpy as jnp
        import numpy as np
        EMBED_DIM = 256
        N_HEADS = 16
        KV_SIZE = 64
        CLIP_DIST = 10
        SLEN = 256
        BSZ = 8
        key = jax.random.key(seed)
        ks = jax.random.split(key, 7)
        s = 0.02
        inputs = jax.random.normal(ks[0], (SLEN, BSZ, EMBED_DIM), dtype=jnp.float32)
        W_in = jax.random.normal(ks[1], (3 * N_HEADS * KV_SIZE, EMBED_DIM), dtype=jnp.float32) * s
        b_in = jnp.zeros((3 * N_HEADS * KV_SIZE,), dtype=jnp.float32)
        k_dist_emb = jax.random.normal(ks[2], (CLIP_DIST + 1, KV_SIZE), dtype=jnp.float32) * s
        v_dist_emb = jax.random.normal(ks[3], (CLIP_DIST + 1, KV_SIZE), dtype=jnp.float32) * s
        W_out = jax.random.normal(ks[4], (EMBED_DIM, N_HEADS * KV_SIZE), dtype=jnp.float32) * s
        b_out = jnp.zeros((EMBED_DIM,), dtype=jnp.float32)
        return {'inputs': inputs, 'W_in': W_in, 'b_in': b_in, 'k_dist_emb': k_dist_emb, 'v_dist_emb': v_dist_emb, 'W_out': W_out, 'b_out': b_out}
    _L1_attn_in = _L1_attn_setup()

    def _L1_ffn_setup():
        import jax, jax.numpy as jnp
        import numpy as np
        INPUT_SIZE = 256
        OUTPUT_SIZE = 256
        key = jax.random.key(seed)
        kx, kt, kp, ktn, kpn = jax.random.split(key, 5)
        x = jax.random.normal(kx, (8, 512, INPUT_SIZE), dtype=jnp.float32)
        theta = jax.random.normal(kt, (INPUT_SIZE, OUTPUT_SIZE), dtype=jnp.float32) * 0.02
        phi = jax.random.normal(kp, (INPUT_SIZE, OUTPUT_SIZE), dtype=jnp.float32) * 0.02
        theta_noise = jax.random.normal(ktn, (INPUT_SIZE, OUTPUT_SIZE), dtype=jnp.float32) * 0.01
        phi_noise = jax.random.normal(kpn, (INPUT_SIZE, OUTPUT_SIZE), dtype=jnp.float32) * 0.01
        return {'x': x, 'theta': theta, 'phi': phi, 'theta_noise': theta_noise, 'phi_noise': phi_noise}
    _L1_ffn_in = _L1_ffn_setup()
    _d = {'L0_attn_x': _L0_attn_in['x'], 'L0_attn_Wq': _L0_attn_in['Wq'], 'L0_attn_Wk': _L0_attn_in['Wk'], 'L0_attn_Wv': _L0_attn_in['Wv'], 'L0_attn_norm_w': _L0_attn_in['norm_w'], 'L0_attn_Wo': _L0_attn_in['Wo'], 'L0_attn_bo': _L0_attn_in['bo'], 'L0_attn_diff_weight': _L0_attn_in['diff_weight'], 'L0_ffn_w_route': _L0_ffn_in['w_route'], 'L0_ffn_compress': _L0_ffn_in['compress'], 'L0_ffn_routed': _L0_ffn_in['routed'], 'L1_attn_W_in': _L1_attn_in['W_in'], 'L1_attn_b_in': _L1_attn_in['b_in'], 'L1_attn_k_dist_emb': _L1_attn_in['k_dist_emb'], 'L1_attn_v_dist_emb': _L1_attn_in['v_dist_emb'], 'L1_attn_W_out': _L1_attn_in['W_out'], 'L1_attn_b_out': _L1_attn_in['b_out'], 'L1_ffn_theta': _L1_ffn_in['theta'], 'L1_ffn_phi': _L1_ffn_in['phi'], 'L1_ffn_theta_noise': _L1_ffn_in['theta_noise'], 'L1_ffn_phi_noise': _L1_ffn_in['phi_noise']}
    _x0 = _d['L0_attn_x']
    _d['L0_attn_x'] = jax.random.normal(jax.random.fold_in(jax.random.key(seed), 1), (8, 512, 256), dtype=_x0.dtype)
    del _x0
    return _d

def reference(L0_attn_x, L0_attn_Wq, L0_attn_Wk, L0_attn_Wv, L0_attn_norm_w, L0_attn_Wo, L0_attn_bo, L0_attn_diff_weight, L0_ffn_w_route, L0_ffn_compress, L0_ffn_routed, L1_attn_W_in, L1_attn_b_in, L1_attn_k_dist_emb, L1_attn_v_dist_emb, L1_attn_W_out, L1_attn_b_out, L1_ffn_theta, L1_ffn_phi, L1_ffn_theta_noise, L1_ffn_phi_noise):

    def _L0_attn_ref(x, Wq, Wk, Wv, norm_w, Wo, bo, diff_weight):
        import jax, jax.numpy as jnp
        import numpy as np
        B, S, E, H = (2, 512, 256, 8)
        DH = E // H
        F = DH // 2
        b, s, e = x.shape
        qs = (x @ Wq.T).reshape(b, s, H, 2, F)
        ks_ = (x @ Wk.T).reshape(b, s, H, 2, F)
        vs = (x @ Wv.T).reshape(b, s, H, DH)
        scale = F ** (-0.5)
        scores = jnp.einsum('bqhif,bkhif->ibhqk', qs, ks_) * scale
        atts = jax.nn.softmax(scores, axis=-1)
        att = atts[0] - diff_weight * atts[1]
        o = jnp.einsum('bhqk,bkhe->bqhe', att, vs)
        eps = jnp.finfo(o.dtype).eps
        rms = jax.lax.rsqrt(jnp.mean(o * o, axis=(-2, -1), keepdims=True) + eps)
        normed = (o * rms * norm_w).reshape(b, s, e)
        return (normed @ Wo.T + bo) * (1.0 - diff_weight)

    def _L0_ffn_ref(x, w_route, compress, routed):
        import jax, jax.numpy as jnp
        import numpy as np
        E = 8
        TOP_K = 2
        R = 16
        ALPHA = 32.0
        SCALING = ALPHA / R
        logits = jnp.einsum('btd,ed->bte', x, w_route)
        topk_vals, topk_idx = jax.lax.top_k(logits, TOP_K)
        topk_w = jax.nn.softmax(topk_vals, axis=-1)
        gate = jnp.sum(jax.nn.one_hot(topk_idx, E, dtype=x.dtype) * topk_w[..., None], axis=-2)
        ce = jnp.einsum('btd,rd->btr', x, compress)
        out = SCALING * jnp.einsum('btr,bte,eor->bto', ce, gate, routed)
        return out

    def _L1_attn_ref(inputs, W_in, b_in, k_dist_emb, v_dist_emb, W_out, b_out):
        import jax, jax.numpy as jnp
        import numpy as np
        EMBED_DIM = 256
        N_HEADS = 16
        KV_SIZE = 64
        CLIP_DIST = 10
        SLEN = 256
        BSZ = 8
        slen, bsz, _ = inputs.shape
        h, d = (N_HEADS, KV_SIZE)
        qkv = inputs @ W_in.T + b_in
        qkv = qkv.reshape(slen, bsz, 3, h, d).transpose(2, 1, 3, 0, 4)
        q, k, v = (qkv[0], qkv[1], qkv[2])
        q = q * d ** (-0.5)
        idx = jnp.arange(slen)
        dist = jnp.minimum(jnp.abs(idx[None, :] - idx[:, None]), CLIP_DIST)
        k_dist = k_dist_emb[dist]
        v_dist = v_dist_emb[dist]
        attn = jnp.einsum('bhsd,bhtd->bhst', q, k) + jnp.einsum('bhsd,std->bhst', q, k_dist)
        attn = jax.nn.softmax(attn, axis=-1)
        out = jnp.einsum('bhst,bhtd->bhsd', attn, v) + jnp.einsum('bhst,std->bhsd', attn, v_dist)
        out = out.transpose(2, 0, 1, 3).reshape(slen, bsz, h * d)
        return out @ W_out.T + b_out

    def _L1_ffn_ref(x, theta, phi, theta_noise, phi_noise):
        import jax, jax.numpy as jnp
        import numpy as np
        INPUT_SIZE = 256
        OUTPUT_SIZE = 256
        real = jnp.einsum('bti,io->bto', x, jnp.cos(theta + theta_noise))
        imag = jnp.einsum('bti,io->bto', x, jnp.sin(phi + phi_noise))
        return jnp.sqrt(real * real + imag * imag)
    x = L0_attn_x
    xn = _layernorm(x, axis=-1)
    s = _L0_attn_ref(xn, L0_attn_Wq, L0_attn_Wk, L0_attn_Wv, L0_attn_norm_w, L0_attn_Wo, L0_attn_bo, L0_attn_diff_weight)
    g = _silu(_L0_ffn_ref(xn, L0_ffn_w_route, L0_ffn_compress, L0_ffn_routed))
    x = x + s * g
    xn = _layernorm(x, axis=-1)
    s = _L1_attn_ref(xn, L1_attn_W_in, L1_attn_b_in, L1_attn_k_dist_emb, L1_attn_v_dist_emb, L1_attn_W_out, L1_attn_b_out)
    g = _silu(_L1_ffn_ref(xn, L1_ffn_theta, L1_ffn_phi, L1_ffn_theta_noise, L1_ffn_phi_noise))
    x = x + s * g
    return x

_drawn_inputs = setup_inputs


def setup_inputs(seed=0):
    import zlib

    import numpy as np

    out = dict(_drawn_inputs(seed))
    spreads = {'L0_attn_norm_w': (1.0, 0.6),
     'L0_attn_bo': (0.0, 0.8),
     'L1_attn_b_in': (0.0, 0.51),
     'L1_attn_b_out': (0.0, 0.353)}
    factors = {'L0_attn_Wq': 4.081,
     'L0_attn_Wk': 4.051,
     'L0_attn_Wv': 3.733,
     'L0_attn_Wo': 3.772,
     'L0_ffn_w_route': 4.321,
     'L0_ffn_compress': 3.791,
     'L0_ffn_routed': 3.744,
     'L1_attn_W_in': 3.323,
     'L1_attn_k_dist_emb': 8.0,
     'L1_attn_v_dist_emb': 8.0,
     'L1_ffn_theta': 8.0,
     'L1_ffn_phi': 2.74,
     'L1_ffn_theta_noise': 8.0,
     'L1_ffn_phi_noise': 4.345}
    for name, (base, spread) in spreads.items():
        noise = np.random.default_rng([zlib.crc32(name.encode()), seed]).standard_normal(out[name].shape)
        drawn = base * np.exp(spread * noise) if base else spread * noise
        out[name] = jnp.asarray(drawn.astype(out[name].dtype))
    for name, factor in factors.items():
        out[name] = (out[name] * factor).astype(out[name].dtype)
    return out
```

```python
from contextlib import ExitStack

import numpy as np

import concourse.bass as bass
from concourse import mybir

F32 = mybir.dt.float32
F32R = mybir.dt.float32r
I32 = mybir.dt.int32
ALU = mybir.AluOpType
ACT = mybir.ActivationFunctionType
X = mybir.AxisListType.X

P = 128
B, S, E = 8, 512, 256
KC = E // P
QT = S // P
LN_EPS = 1e-5

H0 = 8
DH0 = E // H0
F0 = DH0 // 2
HG = 4
HALF = 4
UNITS = 16
NE, R = 8, 16
WCAT = E + NE + R
STACK = 4 * F0
MROW = 96
MROWS = 2 * HG
LEAD = 24
LAG = 2
SCALE0 = float(F0) ** -0.5
EPS32 = float(np.finfo(np.float32).eps)

H1 = 16
D1 = 64
HP = H1 // 2
NREL = 8
NS = 64
NT1 = S // NS
TOK = NS * B
TT = TOK // P
BLK = 32
NBLK = TOK // BLK
NEG = -1e30


class Semaphores:
    pass


def wait(eng, sem, value):
    if not (isinstance(value, int) and value <= 0):
        eng.wait_ge(sem, value)


def stand_alone(eng, passed):
    eng.sem_inc(passed, 1)


def over_batches(eng, body, before=1):
    for b in range(before):
        body(b)
    with eng.Fori(before, B - 1) as b:
        body(b)
    body(B - 1)


def layer0_jobs(b):
    nxt = not (isinstance(b, int) and b >= B - 1)
    prv = not (isinstance(b, int) and b < 1)
    jobs = [((0, 1), "PROJ", 4 * b + 3, 0), ((0, 9), "M", 4 * b + 1, 0)]
    if nxt:
        jobs += [((0, 11), "XT", b + 1, 0), ((0, 13), "XT", b + 1, 1)]
    if prv:
        jobs += [((0, 15), "TD", b - 1, 0), ((1, 1), "TA", b - 1, 0), ((1, 3), "TA", b - 1, 1),
                 ((1, 5), "TA", b - 1, 2), ((1, 7), "TA", b - 1, 3)]
    jobs += [((1, 9), "M", 4 * b + 2, 0)]
    if nxt:
        jobs += [((1, 11), "PROJ", 4 * b + 4, 0), ((1, 13), "V", b + 1, 0), ((2, 1), "PROJ", 4 * b + 5, 0)]
    if prv:
        jobs += [((2, 3), "OT", b - 1, 0), ((2, 5), "OT", b - 1, 1), ((2, 7), "ZT", b - 1, 0)]
    jobs += [((2, 9), "M", 4 * b + 3, 0)]
    if prv:
        jobs += [((2, 11), "WF", b - 1, 0), ((2, 13), "WF", b - 1, 1)]
    if nxt:
        jobs += [((2, 15), "V", b + 1, 1), ((3, 1), "PROJ", 4 * b + 6, 0)]
    if prv:
        jobs += [((3, 3), "WF", b - 1, 2), ((3, 5), "WF", b - 1, 3)]
    if nxt:
        jobs += [((3, 7), "V", b + 1, 2), ((3, 9), "M", 4 * b + 4, 0), ((3, 11), "V", b + 1, 3)]
    return jobs


FIRST_JOBS = [("XT", 0, 0), ("XT", 0, 1), ("PROJ", 0, 0), ("PROJ", 1, 0), ("PROJ", 2, 0),
              ("V", 0, 0), ("V", 0, 1), ("V", 0, 2), ("V", 0, 3), ("M", 0, 0)]
LAST_JOBS = [("TD", B - 1, 0)] + [("TA", B - 1, t) for t in range(QT)] + [("OT", B - 1, 0), ("OT", B - 1, 1),
             ("ZT", B - 1, 0)] + [("WF", B - 1, t) for t in range(QT)]


def layer0(nc, io, x1_dram):
    with ExitStack() as ctx:
        def sb(name, shape, dt=F32):
            return ctx.enter_context(nc.sbuf_tensor(name, shape, dt))

        def bank(name):
            return ctx.enter_context(nc.psum_tensor(name, [P, 512], F32))

        def sem(name):
            return ctx.enter_context(nc.semaphore(name))

        ident = sb("ident0", [P, P])
        wqk_h, wqk_l = sb("wqk_h", [P, KC, HALF, P], F32R), sb("wqk_l", [P, KC, HALF, P], F32R)
        wcat = sb("wcat", [P, KC, WCAT])
        wo = sb("wo", [P, KC, E])
        normw = sb("normw", [P, KC])
        routed = sb("routed", [P, E])
        bo = sb("bo", [P, E])
        dw = sb("dw", [P, 1])
        one_dw, neg_dw = sb("one_dw", [P, 1]), sb("neg_dw", [P, 1])
        rank8 = sb("rank8", [P, NE])
        pick = sb("pick", [P, HALF, BLK])
        mhalf = sb("mhalf", [P, QT])
        xb = sb("xb", [P, QT, E])
        stat, mv = sb("stat", [P, QT, 6]), sb("mv", [P, QT, 2])
        veps, rstd = sb("veps", [P, QT]), sb("rstd", [P, QT])
        xn = sb("xn", [P, QT, E])
        xt = sb("xt", [P, KC, S])
        xt_h, xt_l = sb("xt_h", [P, KC, S], F32R), sb("xt_l", [P, KC, S], F32R)
        qk_h, qk_l = sb("qk_h", [P, S], F32R), sb("qk_l", [P, S], F32R)
        qst = [sb(f"qst{i}", [P, HG, S], F32R) for i in range(HALF)]
        kst = [sb(f"kst{i}", [P, HG, S], F32R) for i in range(HALF)]
        vnew = sb("vnew", [P, QT, WCAT])
        v = sb("v", [P, QT, E])
        lc = sb("lc", [P, QT, NE + R])
        negmax = sb("negmax", [P, 2, QT, HG])
        msplit = sb("msplit", [P, QT, 2, HG], F32R)
        mrow = sb("mrow", [P, S], F32R)
        probs = sb("probs", [P, 4, HG, S])
        pairs = sb("pairs", [P, 2, HG, S])
        wqk = pairs[:, 0, 0:2, :].rearrange("p a (k n) -> p a k n", k=HALF)
        which = probs[:, 0, :, :]
        at = sb("at", [P, HALF, S])
        dt_ = sb("dt", [P, S])
        rec = sb("rec", [P, QT, HALF, HG])
        an = sb("an", [P, HALF, HG, DH0])
        o = sb("o", [P, QT, E])
        ss, ms, rms = sb("ss", [P, QT]), sb("ms", [P, QT]), sb("rms", [P, QT])
        ot = sb("ot", [P, KC, S])
        gt = sb("gt", [P, 8, QT, NE])
        gs = sb("gs", [P, 8, QT])
        z, zt = sb("z", [P, QT, NE, R]), sb("zt", [P, S])
        th, s_, g_ = sb("th", [P, QT, E]), sb("s_", [P, QT, E]), sb("g_", [P, QT, E])
        xr, x1o = sb("xr", [P, QT, E]), sb("x1o", [P, 2, E])

        s_bank = [bank("s_bank0"), bank("s_bank1")]
        t_bank = [bank("t_bank0"), bank("t_bank1")]
        a_bank = [bank("a_bank0"), bank("a_bank1")]
        d_bank = bank("d_bank")
        misc = bank("misc0")

        park = nc.dram_tensor("park", [2, P, S], F32).ap()

        m = Semaphores()
        m.w_load = sem("w_load0")
        m.wsplit = sem("wsplit0")
        m.x_load = sem("x_load0")
        m.stats = sem("stats0")
        m.aggr = sem("aggr0")
        m.veps_ok = sem("veps_ok0")
        m.rstd_ok = sem("rstd_ok0")
        m.xn_ok = sem("xn_ok0")
        m.xt_psum = sem("xt_psum0")
        m.xt_high = sem("xt_high0")
        m.xt_low = sem("xt_low0")
        m.proj_psum = sem("proj_psum0")
        m.qk_high = sem("qk_high0")
        m.qk_low = sem("qk_low0")
        m.parked = sem("parked0")
        m.stacked = sem("stacked0")
        m.v_psum = sem("v_psum0")
        m.vnew_ok = sem("vnew_ok0")
        m.v_ok = sem("v_ok0")
        m.lc_ok = sem("lc_ok0")
        m.s_done = sem("s_done0")
        m.max_done = sem("max_done0")
        m.m_high = sem("m_high0")
        m.m_low = sem("m_low0")
        m.m_psum = sem("m_psum0")
        m.m_evac = sem("m_evac0")
        m.m_placed = sem("m_placed0")
        m.t_done = sem("t_done0")
        m.exp_done = sem("exp_done0")
        m.pair_ok = sem("pair_ok0")
        m.a_done = sem("a_done0")
        m.d_done = sem("d_done0")
        m.a_evac = sem("a_evac0")
        m.d_evac = sem("d_evac0")
        m.td_psum = sem("td_psum0")
        m.recip_ok = sem("recip_ok0")
        m.rec_ok = sem("rec_ok0")
        m.ta_psum = sem("ta_psum0")
        m.an_ok = sem("an_ok0")
        m.o_ok = sem("o_ok0")
        m.ss_ok = sem("ss_ok0")
        m.ms_ok = sem("ms_ok0")
        m.rms_ok = sem("rms_ok0")
        m.ot_psum = sem("ot_psum0")
        m.ot_evac = sem("ot_evac0")
        m.prod_ok = sem("prod_ok0")
        m.zeros = sem("zeros0")
        m.mhalf_ok = sem("mhalf_ok0")
        m.which_ok = sem("which_ok0")
        m.fold = sem("fold0")
        m.gate = sem("gate0")
        m.gate_d = sem("gate_d0")
        m.gate_e = sem("gate_e0")
        m.z_ok = sem("z_ok0")
        m.zt_psum = sem("zt_psum0")
        m.zt_evac = sem("zt_evac0")
        m.wf_psum = sem("wf_psum0")
        m.tanh_ok = sem("tanh_ok0")
        m.s_ok = sem("s_ok0")
        m.wf_gate = sem("wf_gate0")
        m.sg_ok = sem("sg_ok0")
        m.xr_load = sem("xr_load0")
        m.x1_ok = sem("x1_ok0")
        m.x1_stored_even = sem("x1_stored_even0")
        m.x1_stored_odd = sem("x1_stored_odd0")
        m.sp_passed = sem("sp_passed0")
        m.dve_passed = sem("dve_passed0")
        m.pool_passed = sem("pool_passed0")
        m.x1_stored = (m.x1_stored_even, m.x1_stored_odd)

        def drained(kind, i, k):
            return {"XT": (m.xt_low, KC * i + k + 1), "PROJ": (m.qk_low, i + 1), "V": (m.vnew_ok, QT * i + k + 1),
                    "M": (m.m_evac, i + 1), "TD": (m.recip_ok, i + 1), "TA": (m.an_ok, QT * i + k + 1),
                    "OT": (m.ot_evac, KC * i + k + 1), "ZT": (m.zt_evac, i + 1),
                    "WF": (m.wf_gate, QT * i + k + 1)}[kind]

        LOADS = 11
        block = ctx.enter_context(nc.Block())

        @block.sync
        def _(sp):
            sp.dma_start(xb[:, :, :], io["x"][0].rearrange("(t p) c -> p t c", p=P)).then_inc(m.x_load, 16)
            for dst, src in (
                    (ident[:, :], io["ident"]), (wqk, io["wqk"].rearrange("(k p) h n -> p k h n", p=P)),
                    (wcat[:, :, :], io["wcat"].rearrange("(k p) n -> p k n", p=P)),
                    (wo[:, :, :], io["wo"].rearrange("(k p) n -> p k n", p=P)),
                    (normw[:, :], io["normw"]), (routed[:, :], io["routed"]),
                    (bo[:, :], io["bo"].partition_broadcast(P)), (dw[:, :], io["dw"].partition_broadcast(P)),
                    (rank8[:, :], io["rank8"].partition_broadcast(P)), (pick[:, :, :], io["pick"]),
                    (which[MROW:MROW + MROWS], io["which"])):
                sp.dma_start(dst, src).then_inc(m.w_load, 16)

            def park_parts(i):
                sp.wait_ge(m.qk_high, i + 1)
                stand_alone(sp, m.sp_passed)
                wait(sp, m.stacked, 128 * i)
                sp.dma_start(park[0], qk_h[:, :].bitcast(F32)).then_inc(m.parked, 16)
                sp.wait_ge(m.qk_low, i + 1)
                sp.dma_start(park[1], qk_l[:, :].bitcast(F32)).then_inc(m.parked, 16)

            def fill_stacks(i, slot):
                sp.wait_ge(m.parked, 32 * i + 32)
                for r in range(4):
                    for side, stack, part in ((0, qst, r // 2), (1, kst, r % 2)):
                        src = park[part, 64 * side:64 * side + 64, :].rearrange("(h f) q -> f h q", f=F0)
                        sp.dma_start(stack[slot][F0 * r:F0 * r + F0, :, :].bitcast(F32), src).then_inc(m.stacked, 16)

            def place_max(i, slot):
                sp.wait_ge(m.m_evac, i + 1)
                sp.dma_start(qst[slot][MROW:MROW + MROWS, :, :].bitcast(F32),
                             mrow[MROW:MROW + MROWS, :].bitcast(F32).unsqueeze(1).to_broadcast([MROWS, HG, S])
                             ).then_inc(m.m_placed, 16)

            def load_x(b):
                wait(sp, m.xn_ok, b)
                stand_alone(sp, m.sp_passed)
                sp.dma_start(xb[:, :, :], io["x"][b].rearrange("(t p) c -> p t c", p=P)).then_inc(m.x_load, 16)

            def load_residual(b):
                wait(sp, m.x1_ok, QT * b)
                stand_alone(sp, m.sp_passed)
                sp.dma_start(xr[:, :, :], io["x"][b].rearrange("(t p) c -> p t c", p=P)).then_inc(m.xr_load, 16)

            def store_x1(b, t):
                sp.wait_ge(m.x1_ok, QT * b + t + 1)
                stand_alone(sp, m.sp_passed)
                sp.dma_start(x1_dram[t * P:(t + 1) * P, b, :], x1o[:, t % 2, :]).then_inc(m.x1_stored[t % 2], 16)

            for i in range(3):
                park_parts(i)
                fill_stacks(i, i)
            place_max(0, 0)

            def body(b):
                for hf, v_, kind, i, k in slots(b):
                    if kind == "START" and hf == 0:
                        if not (isinstance(b, int) and b >= B - 1):
                            load_x(b + 1)
                        if not (isinstance(b, int) and b < 1):
                            load_residual(b - 1)
                    if kind == "PROJ":
                        park_parts(i)
                        fill_stacks(i, k)
                    if kind == "M":
                        place_max(i, k)
                    if kind == "WF":
                        store_x1(i, k)

            def slots(b):
                out = [(0, -1, "START", 0, 0)]
                for (hf, v_), kind, i, k in layer0_jobs(b):
                    if kind == "PROJ":
                        k = (3, 0, 1, 2)[hf]
                    if kind == "M":
                        k = (1, 2, 3, 0)[hf]
                    out.append((hf, v_, kind, i, k))
                return out

            over_batches(sp, body, 2)
            load_residual(B - 1)
            for t in range(QT):
                store_x1(B - 1, t)
            for stored in m.x1_stored:
                sp.wait_ge(stored, 16 * B * QT // 2)

        @block.tensor
        def _(pe):
            pe.wait_ge(m.wsplit, 2)
            pe.wait_ge(m.zeros, 2 * HALF)
            pe.wait_ge(m.which_ok, HALF)
            pe.wait_ge(m.fold, 5)

            def job(kind, i, k):
                if kind == "XT":
                    pe.wait_ge(m.xn_ok, i + 1)
                    for t in range(QT):
                        mm = pe.transpose(misc[:, t * P:(t + 1) * P], xn[:, t, k * P:(k + 1) * P], ident[:, :])
                    mm.then_inc(m.xt_psum, 1)
                if kind == "PROJ":
                    hf = k
                    n = 0
                    for kc in range(KC):
                        for w, x in ((wqk_h, xt_h), (wqk_h, xt_l), (wqk_l, xt_h)):
                            mm = pe.matmul(misc[:, :], w[:, kc, hf, :], x[:, kc, :], start=(n == 0), stop=(n == 5))
                            n += 1
                    mm.then_inc(m.proj_psum, 1)
                if kind == "V":
                    for kc in range(KC):
                        mm = pe.matmul(misc[:, 0:WCAT], xt[:, kc, k * P:(k + 1) * P], wcat[:, kc, :],
                                       start=(kc == 0), stop=(kc == KC - 1))
                    mm.then_inc(m.v_psum, 1)
                if kind == "M":
                    pe.wait_ge(m.m_low, i + 1)
                    for c in range(QT):
                        mm = pe.matmul(misc[MROW:MROW + MROWS, c * P:(c + 1) * P],
                                       msplit[:, c, :, :].bitcast(F32).rearrange("p a h -> p (a h)"),
                                       ident[:, :], start=True, stop=True)
                    mm.then_inc(m.m_psum, 1)
                if kind == "TD":
                    pe.wait_ge(m.d_evac, i + 1)
                    for t in range(QT):
                        mm = pe.transpose(misc[:, t * P:(t + 1) * P], dt_[:, t * P:(t + 1) * P], ident[:, :])
                    mm.then_inc(m.td_psum, 1)
                if kind == "TA":
                    pe.wait_ge(m.a_evac, HALF * (i + 1))
                    for hf in range(HALF):
                        mm = pe.transpose(misc[:, hf * P:(hf + 1) * P], at[:, hf, k * P:(k + 1) * P], ident[:, :])
                    mm.then_inc(m.ta_psum, 1)
                if kind == "OT":
                    pe.wait_ge(m.o_ok, QT * (i + 1))
                    for t in range(QT):
                        mm = pe.transpose(misc[:, t * P:(t + 1) * P], o[:, t, k * P:(k + 1) * P], ident[:, :])
                    mm.then_inc(m.ot_psum, 1)
                if kind == "ZT":
                    pe.wait_ge(m.z_ok, i + 1)
                    for t in range(QT):
                        mm = pe.transpose(misc[:, t * P:(t + 1) * P], z[:, t, :, :].rearrange("p e r -> p (e r)"),
                                          ident[:, :])
                    mm.then_inc(m.zt_psum, 1)
                if kind == "WF":
                    for kc in range(KC):
                        pe.matmul(misc[:, 0:E], ot[:, kc, k * P:(k + 1) * P], wo[:, kc, :],
                                  start=(kc == 0), stop=(kc == KC - 1))
                    pe.matmul(misc[:, E:2 * E], zt[:, k * P:(k + 1) * P], routed[:, :],
                              start=True, stop=True).then_inc(m.wf_psum, 1)

            def score_max(n, w, slot, i):
                if w == 0:
                    pe.wait_ge(m.stacked, 128 * (i + 1))
                wait(pe, m.max_done, n - 1)
                j, c = w // 4, w % 4
                pe.matmul(s_bank[w % 2][:, :], qst[slot][0:MROW, j, c * P:(c + 1) * P], kst[slot][0:MROW, j, :],
                          start=True, stop=True).then_inc(m.s_done, 1)

            def score_exp(g, w, slot, i):
                if w == 0:
                    pe.wait_ge(m.m_placed, 16 * (i + 1))
                wait(pe, m.exp_done, g - 1)
                c, j = w // 4, w % 4
                pe.matmul(t_bank[w % 2][:, :], kst[slot][0:MROW + MROWS, j, c * P:(c + 1) * P],
                          qst[slot][0:MROW + MROWS, j, :], start=True, stop=True).then_inc(m.t_done, 1)

            def value_step(b, hf, c):
                y = HALF * b + hf
                hg = hf // 2
                if c == 0:
                    wait(pe, m.a_evac, y - 1)
                    if hf == 0:
                        pe.wait_ge(m.v_ok, b + 1)
                pe.wait_ge(m.exp_done, UNITS * y + 4 * c + 4)
                for h in range(HG):
                    mm = pe.matmul(a_bank[hf % 2][BLK * h:BLK * h + BLK, :],
                                   v[:, c, hg * P + h * DH0:hg * P + (h + 1) * DH0], probs[:, c, h, :],
                                   start=(c == 0), stop=(c == 3))
                mm.then_inc(m.a_done, 1)
                if c % 2:
                    if hf == 0 and c == 1:
                        wait(pe, m.d_evac, b)
                    pe.wait_ge(m.pair_ok, 2 * y + c // 2 + 1)
                    for h in range(HG):
                        mm = pe.matmul(d_bank[BLK * h:BLK * h + BLK, :], pick[:, hf, :], pairs[:, c // 2, h, :],
                                       start=(hf == 0 and c == 1), stop=(hf == 3 and c == 3))
                    mm.then_inc(m.d_done, 1)

            prev = None

            def side(kind, i, k):
                nonlocal prev
                if prev is not None:
                    wait(pe, *drained(*prev))
                job(kind, i, k)
                prev = (kind, i, 0 if kind in ("PROJ", "M") else k)

            for kind, i, k in FIRST_JOBS[:-1]:
                side(kind, i, i if kind == "PROJ" else k)
            for n in range(LEAD):
                score_max(n, n % UNITS, n // UNITS, n // UNITS)
            side(*FIRST_JOBS[-1])

            def body(b):
                nonlocal prev
                last = isinstance(b, int) and b >= B - 1
                if not isinstance(b, int):
                    _, kind, i, k = layer0_jobs(b - 1)[-1]
                    prev = (kind, i, k)
                jobs = layer0_jobs(b)
                for hf in range(HALF):
                    for w in range(UNITS):
                        g = HALF * UNITS * b + UNITS * hf + w
                        score_exp(g, w, hf, HALF * b + hf)
                        ahead = hf * UNITS + w + LEAD
                        if not (last and ahead >= HALF * UNITS):
                            score_max(g + LEAD, ahead % UNITS, ahead // UNITS % HALF, HALF * b + ahead // UNITS)
                        if w % 4 == 3:
                            step = 4 * hf + w // 4 - LAG
                            if step >= 0:
                                value_step(b, step // 4, step % 4)
                            elif not (isinstance(b, int) and b < 1):
                                value_step(b - 1, (step + 16) // 4, (step + 16) % 4)
                        for (jh, jw), kind, i, k in jobs:
                            if (jh, jw) == (hf, w):
                                side(kind, i, (3, 0, 1, 2)[hf] if kind == "PROJ" else k)

            over_batches(pe, body, 2)
            for step in range(16 - LAG, 16):
                value_step(B - 1, step // 4, step % 4)
            for kind, i, k in LAST_JOBS:
                side(kind, i, k)

        @block.scalar
        def _(act):
            act.wait_ge(m.w_load, 16 * LOADS)
            act.activation(wqk_h[:, :, :, :], wqk, ACT.Copy).then_inc(m.wsplit, 1)

            def exp_tile(b, hf, w):
                g = HALF * UNITS * b + UNITS * hf + w
                act.wait_ge(m.t_done, g + 1)
                c, j = w // 4, w % 4
                if j == 0:
                    wait(act, m.a_done, 4 * (HALF * b + hf - 1) + c + 1)
                    wait(act, m.pair_ok, 2 * (HALF * b + hf - 1) + c // 2 + 1)
                act.activation(probs[:, c, j, :], t_bank[w % 2][:, :], ACT.Exp, scale=SCALE0).then_inc(m.exp_done, 1)

            def side(kind, i, k):
                if kind == "XT":
                    act.wait_ge(m.xt_psum, KC * i + k + 1)
                    if k == 0:
                        wait(act, m.proj_psum, 4 * i)
                        wait(act, m.v_psum, QT * i)
                    act.activation(xt[:, k, :], misc[:, :], ACT.Copy)
                    act.activation(xt_h[:, k, :], misc[:, :], ACT.Copy).then_inc(m.xt_high, 1)
                if kind == "PROJ":
                    act.wait_ge(m.proj_psum, i + 1)
                    wait(act, m.parked, 32 * i)
                    act.activation(qk_h[:, :], misc[:, :], ACT.Copy).then_inc(m.qk_high, 1)
                if kind == "V":
                    act.wait_ge(m.v_psum, QT * i + k + 1)
                    wait(act, m.lc_ok, i)
                    act.activation(vnew[:, k, :], misc[:, 0:WCAT], ACT.Copy).then_inc(m.vnew_ok, 1)
                if kind == "M":
                    act.wait_ge(m.m_psum, i + 1)
                    wait(act, m.m_placed, 16 * i)
                    act.activation(mrow[MROW:MROW + MROWS, :], misc[MROW:MROW + MROWS, :], ACT.Copy).then_inc(m.m_evac, 1)
                if kind == "DEV":
                    act.wait_ge(m.d_done, 8 * i + 8)
                    wait(act, m.td_psum, i)
                    act.activation(dt_[:, :], d_bank[:, :], ACT.Copy).then_inc(m.d_evac, 1)
                if kind == "SQ":
                    act.wait_ge(m.o_ok, QT * i + k + 1)
                    if k == 0:
                        wait(act, m.ms_ok, i)
                        wait(act, m.wf_gate, QT * i)
                    act.activation(th[:, k, :], o[:, k, :], ACT.Square, accum_out=ss[:, k:k + 1]).then_inc(m.ss_ok, 1)
                if kind == "OT":
                    act.wait_ge(m.ot_psum, KC * i + k + 1)
                    wait(act, m.wf_psum, QT * i)
                    act.activation(ot[:, k, :], misc[:, :], ACT.Copy).then_inc(m.ot_evac, 1)
                if kind == "ZT":
                    act.wait_ge(m.zt_psum, i + 1)
                    act.activation(zt[:, :], misc[:, :], ACT.Copy).then_inc(m.zt_evac, 1)
                if kind == "WF":
                    act.wait_ge(m.wf_psum, QT * i + k + 1)
                    if k == 0:
                        act.wait_ge(m.ss_ok, QT * (i + 1))
                    act.activation(th[:, k, :], misc[:, E:2 * E], ACT.Tanh).then_inc(m.tanh_ok, 1)
                if kind == "GEXP":
                    act.wait_ge(m.gate_d, i + 1)
                    act.activation(gs[:, 5, :], gs[:, 4, :], ACT.Exp).then_inc(m.gate_e, 1)

            for kind, i, k in FIRST_JOBS:
                side(kind, i, k)

            def body(b):
                first = isinstance(b, int) and b < 1
                jobs = layer0_jobs(b)
                for hf in range(HALF):
                    for w in range(UNITS):
                        exp_tile(b, hf, w)
                        if w == 8:
                            if hf:
                                act.wait_ge(m.a_done, 4 * (HALF * b + hf))
                                if hf == 1:
                                    wait(act, m.ta_psum, QT * b)
                                act.activation(at[:, hf - 1, :], a_bank[(hf - 1) % 2][:, :], ACT.Copy).then_inc(m.a_evac, 1)
                            elif not first:
                                act.wait_ge(m.a_done, 16 * b)
                                act.activation(at[:, 3, :], a_bank[1][:, :], ACT.Copy).then_inc(m.a_evac, 1)
                                side("DEV", b - 1, 0)
                        if hf == 3 and w == 10:
                            side("GEXP", b, 0)
                        for (jh, jw), kind, i, k in jobs:
                            if (jh, jw) == (hf, w):
                                side(kind, i, k)
                        if not first and hf == 1 and w in (3, 5, 7, 9):
                            side("SQ", b - 1, (w - 3) // 2)

            over_batches(act, body, 2)
            act.wait_ge(m.a_done, 16 * B)
            act.activation(at[:, 3, :], a_bank[1][:, :], ACT.Copy).then_inc(m.a_evac, 1)
            side("DEV", B - 1, 0)
            for kind, i, k in LAST_JOBS:
                side(kind, i, k)
                if kind == "TA":
                    side("SQ", i, k)

        @block.vector
        def _(dve):
            for i in range(HALF):
                dve.memset(qst[i][STACK:MROW, :, :].bitcast(F32), 0.0).then_inc(m.zeros, 1)
                dve.memset(kst[i][STACK:MROW, :, :].bitcast(F32), 0.0).then_inc(m.zeros, 1)
            dve.memset(mhalf[:, :], -0.5).then_inc(m.mhalf_ok, 1)

            def norm_stats(b):
                dve.wait_ge(m.x_load, 16 * (b + 1))
                for t in range(QT):
                    dve.bn_stats(stat[:, t, :], xb[:, t, :]).then_inc(m.stats, 1)
                dve.wait_ge(m.stats, QT * (b + 1))
                wait(dve, m.veps_ok, b)
                stand_alone(dve, m.dve_passed)
                for t in range(QT):
                    dve.bn_aggr(mv[:, t, :], stat[:, t, :]).then_inc(m.aggr, 1)

            def normalise(b):
                dve.wait_ge(m.rstd_ok, b + 1)
                wait(dve, m.xt_psum, KC * b)
                for t in range(QT):
                    ins = dve.tensor_scalar(xn[:, t, :], xb[:, t, :], mv[:, t, 0:1], rstd[:, t:t + 1],
                                            ALU.subtract, ALU.mult)
                ins.then_inc(m.xn_ok, 1)

            norm_stats(0)
            dve.wait_ge(m.w_load, 16 * LOADS)
            dve.wait_ge(m.wsplit, 1)
            dve.tensor_tensor(wqk_l[:, :, :, :], wqk, wqk_h[:, :, :, :].bitcast(F32),
                              ALU.subtract).then_inc(m.wsplit, 1)
            for i in range(HALF):
                dve.tensor_copy(kst[i][MROW:MROW + MROWS, :, :], which[MROW:MROW + MROWS]).then_inc(m.which_ok, 1)
            normalise(0)
            dve.tensor_scalar(one_dw[:, :], dw[:, :], -1.0, 1.0, ALU.mult, ALU.add).then_inc(m.fold, 1)
            dve.tensor_scalar(neg_dw[:, :], dw[:, :], -1.0, None, ALU.mult).then_inc(m.fold, 1)
            dve.wait_ge(m.fold, 2)
            for kc in range(KC):
                dve.tensor_scalar(wo[:, kc, :], wo[:, kc, :], normw[:, kc:kc + 1], one_dw[:, 0:1], ALU.mult,
                                  ALU.mult).then_inc(m.fold, 1)
            dve.tensor_scalar(bo[:, :], bo[:, :], one_dw[:, 0:1], None, ALU.mult).then_inc(m.fold, 1)

            def max_tile(n, w, i_par):
                dve.wait_ge(m.s_done, n + 1)
                j, c = w // 4, w % 4
                dve.tensor_reduce(negmax[:, i_par, c, j:j + 1], s_bank[w % 2][:, :], X, ALU.max,
                                  negate=True).then_inc(m.max_done, 1)

            def side(kind, i, k):
                if kind == "XT":
                    dve.wait_ge(m.xt_high, KC * i + k + 1)
                    dve.tensor_tensor(xt_l[:, k, :], misc[:, :], xt_h[:, k, :].bitcast(F32),
                                      ALU.subtract).then_inc(m.xt_low, 1)
                if kind == "PROJ":
                    dve.wait_ge(m.qk_high, i + 1)
                    wait(dve, m.parked, 32 * i)
                    dve.tensor_tensor(qk_l[:, :], misc[:, :], qk_h[:, :].bitcast(F32), ALU.subtract).then_inc(m.qk_low, 1)
                if kind == "MS":
                    dve.wait_ge(m.max_done, UNITS * (i + 1))
                    wait(dve, m.m_psum, i)
                    dve.tensor_copy(msplit[:, :, 0, :], negmax[:, k, :, :]).then_inc(m.m_high, 1)
                    dve.wait_ge(m.m_high, i + 1)
                    dve.tensor_tensor(msplit[:, :, 1, :], negmax[:, k, :, :], msplit[:, :, 0, :].bitcast(F32),
                                      ALU.subtract).then_inc(m.m_low, 1)
                if kind == "VCOPY":
                    dve.wait_ge(m.vnew_ok, QT * (i + 1))
                    wait(dve, m.a_done, 16 * i)
                    dve.tensor_copy(v[:, :, :], vnew[:, :, 0:E]).then_inc(m.v_ok, 1)
                    dve.tensor_copy(lc[:, :, :], vnew[:, :, E:WCAT]).then_inc(m.lc_ok, 1)
                if kind == "TD":
                    dve.wait_ge(m.td_psum, i + 1)
                    dve.reciprocal(rec[:, :, :, :].rearrange("p t s h -> p t h s"),
                                   misc[:, :].rearrange("p (t h s) -> p t h s", t=QT, h=HG)[:, :, :, 0:HALF]
                                   ).then_inc(m.recip_ok, 1)
                    dve.wait_ge(m.recip_ok, i + 1)
                    for hg in range(2):
                        one = rec[:, :, 2 * hg + 1, :]
                        ins = dve.tensor_scalar(one, one, neg_dw[:, 0:1], None, ALU.mult)
                    ins.then_inc(m.rec_ok, 1)
                if kind == "TA":
                    dve.wait_ge(m.rec_ok, i + 1)
                    dve.wait_ge(m.ta_psum, QT * i + k + 1)
                    wait(dve, m.o_ok, QT * i + k)
                    if k == 0:
                        wait(dve, m.ot_psum, KC * i)
                        wait(dve, m.ss_ok, QT * i)
                    dve.tensor_tensor(an[:, :, :, :], misc[:, :].rearrange("p (s h e) -> p s h e", s=HALF, h=HG),
                                      rec[:, k, :, :].unsqueeze(3).to_broadcast([P, HALF, HG, DH0]),
                                      ALU.mult).then_inc(m.an_ok, 1)
                    dve.wait_ge(m.an_ok, QT * i + k + 1)
                    maps = an[:, :, :, :].rearrange("p (g i) h e -> p g i (h e)", g=2)
                    dve.tensor_tensor(o[:, k, :].rearrange("p (g n) -> p g n", g=2), maps[:, :, 0, :],
                                      maps[:, :, 1, :], ALU.add).then_inc(m.o_ok, 1)
                if kind == "WF":
                    dve.wait_ge(m.tanh_ok, QT * i + k + 1)
                    dve.wait_ge(m.rms_ok, i + 1)
                    wait(dve, m.x1_ok, QT * (i - 1) + k + 1)
                    dve.scalar_tensor_tensor(s_[:, k, :], misc[:, 0:E], rms[:, k:k + 1], bo[:, :],
                                             op0=ALU.mult, op1=ALU.add).then_inc(m.s_ok, 1)
                    dve.scalar_tensor_tensor(g_[:, k, :], th[:, k, :], 1.0, misc[:, E:2 * E],
                                             op0=ALU.add, op1=ALU.mult).then_inc(m.wf_gate, 1)

            GATES = 17

            def wide(k):
                return gs[:, k, :].unsqueeze(2).to_broadcast([P, QT, NE])

            def gate(b):
                lg = lc[:, :, 0:NE]
                w8 = rank8[:, :].unsqueeze(1).to_broadcast([P, QT, NE])
                n = GATES * b
                dve.wait_ge(m.lc_ok, b + 1)
                wait(dve, m.zt_psum, b)
                for src, top, num, hot in ((lg, 0, 1, 1), (gt[:, 2, :, :], 2, 3, 3)):
                    dve.tensor_reduce(gs[:, top, :], src, X, ALU.max).then_inc(m.gate, 1)
                    dve.wait_ge(m.gate, n + 1)
                    dve.tensor_tensor(gt[:, 0, :, :], src, wide(top), ALU.is_equal).then_inc(m.gate, 1)
                    dve.wait_ge(m.gate, n + 2)
                    dve.tensor_tensor(gt[:, 0, :, :], gt[:, 0, :, :], w8, ALU.mult).then_inc(m.gate, 1)
                    dve.wait_ge(m.gate, n + 3)
                    dve.tensor_reduce(gs[:, num, :], gt[:, 0, :, :], X, ALU.max).then_inc(m.gate, 1)
                    dve.wait_ge(m.gate, n + 4)
                    dve.tensor_tensor(gt[:, hot, :, :], gt[:, 0, :, :], wide(num), ALU.is_equal).then_inc(m.gate, 1)
                    dve.wait_ge(m.gate, n + 5)
                    n = n + 5
                    if top == 0:
                        dve.scalar_tensor_tensor(gt[:, 2, :, :], gt[:, 1, :, :], -3e38, lg,
                                                 op0=ALU.mult, op1=ALU.add).then_inc(m.gate, 1)
                        dve.wait_ge(m.gate, n + 1)
                        n = n + 1
                dve.tensor_tensor(gs[:, 4, :], gs[:, 2, :], gs[:, 0, :], ALU.subtract).then_inc(m.gate_d, 1)

            def gate_end(b):
                n = GATES * b + 11
                dve.wait_ge(m.gate_e, b + 1)
                dve.tensor_scalar(gs[:, 6, :], gs[:, 5, :], 1.0, None, ALU.add).then_inc(m.gate, 1)
                dve.wait_ge(m.gate, n + 1)
                dve.reciprocal(gs[:, 7, :], gs[:, 6, :]).then_inc(m.gate, 1)
                dve.wait_ge(m.gate, n + 2)
                dve.tensor_tensor(gs[:, 6, :], gs[:, 5, :], gs[:, 7, :], ALU.mult).then_inc(m.gate, 1)
                dve.tensor_tensor(gt[:, 4, :, :], gt[:, 1, :, :], wide(7), ALU.mult).then_inc(m.gate, 1)
                dve.wait_ge(m.gate, n + 4)
                dve.tensor_tensor(gt[:, 5, :, :], gt[:, 3, :, :], wide(6), ALU.mult).then_inc(m.gate, 1)
                dve.wait_ge(m.gate, n + 5)
                dve.tensor_tensor(gt[:, 6, :, :], gt[:, 4, :, :], gt[:, 5, :, :], ALU.add).then_inc(m.gate, 1)
                dve.wait_ge(m.gate, n + 6)
                for t in range(QT):
                    ins = dve.tensor_tensor(z[:, t, :, :], gt[:, 6, t, :].unsqueeze(2).to_broadcast([P, NE, R]),
                                            lc[:, t, NE:NE + R].unsqueeze(1).to_broadcast([P, NE, R]), ALU.mult)
                ins.then_inc(m.z_ok, 1)

            for kind, i, k in FIRST_JOBS[:-1]:
                side(kind, i, k)
            side("VCOPY", 0, 0)
            for n in range(LEAD):
                max_tile(n, n % UNITS, n // UNITS % 2)
                if n == UNITS - 1:
                    side("MS", 0, 0)

            def body(b):
                first = isinstance(b, int) and b < 1
                last = isinstance(b, int) and b >= B - 1
                jobs = layer0_jobs(b)
                for hf in range(HALF):
                    for w in range(UNITS):
                        ahead = hf * UNITS + w + LEAD
                        if not (last and ahead >= HALF * UNITS):
                            max_tile(HALF * UNITS * b + ahead, ahead % UNITS, ahead // UNITS % 2)
                        if w == 7 and not (last and hf == 3):
                            side("MS", HALF * b + hf + 1, (hf + 1) % 2)
                        if (hf, w) == (0, 1) and not last:
                            norm_stats(b + 1)
                        if (hf, w) == (0, 6) and not last:
                            normalise(b + 1)
                        if (hf, w) == (0, 8) and not first:
                            side("VCOPY", b, 0)
                        if (hf, w) == (3, 8):
                            gate(b)
                        if (hf, w) == (3, 12):
                            gate_end(b)
                        for (jh, jw), kind, i, k in jobs:
                            if (jh, jw) == (hf, w):
                                side(kind, i, k)

            over_batches(dve, body, 2)
            for kind, i, k in LAST_JOBS:
                side(kind, i, k)

        @block.gpsimd
        def _(pool):
            def rstd_of(b):
                pool.wait_ge(m.aggr, QT * (b + 1))
                wait(pool, m.xn_ok, b)
                stand_alone(pool, m.pool_passed)
                pool.tensor_scalar(veps[:, :], mv[:, :, 1], LN_EPS, None, ALU.add).then_inc(m.veps_ok, 1)
                pool.wait_ge(m.veps_ok, b + 1)
                pool.tensor_tensor(rstd[:, :], veps[:, :], mhalf[:, :], ALU.pow).then_inc(m.rstd_ok, 1)

            def pair_sum(b, hf, c2):
                y = HALF * b + hf
                pool.wait_ge(m.exp_done, UNITS * y + 8 * (c2 + 1))
                wait(pool, m.d_done, 2 * y + c2 - 1)
                pool.tensor_tensor(pairs[:, c2, :, :], probs[:, 2 * c2, :, :], probs[:, 2 * c2 + 1, :, :],
                                   ALU.add).then_inc(m.pair_ok, 1)

            def rms_of(b):
                pool.wait_ge(m.ss_ok, QT * (b + 1))
                wait(pool, m.wf_gate, QT * b)
                stand_alone(pool, m.pool_passed)
                pool.tensor_scalar(ms[:, :], ss[:, :], 1.0 / E, EPS32, ALU.mult, ALU.add).then_inc(m.ms_ok, 1)
                pool.wait_ge(m.ms_ok, b + 1)
                pool.tensor_tensor(rms[:, :], ms[:, :], mhalf[:, :], ALU.pow).then_inc(m.rms_ok, 1)

            def residual(b, k):
                pool.wait_ge(m.wf_gate, QT * b + k + 1)
                pool.tensor_tensor(g_[:, k, :], s_[:, k, :], g_[:, k, :], ALU.mult).then_inc(m.prod_ok, 1)
                pool.wait_ge(m.prod_ok, QT * b + k + 1)
                if k == 0:
                    pool.wait_ge(m.xr_load, 16 * (b + 1))
                wait(pool, m.x1_stored[k % 2], 16 * (QT // 2 * b + k // 2))
                pool.tensor_tensor(x1o[:, k % 2, :], xr[:, k, :], g_[:, k, :], ALU.add).then_inc(m.x1_ok, 1)

            pool.wait_ge(m.mhalf_ok, 1)
            pool.wait_ge(m.x_load, 16)
            rstd_of(0)

            def body(b):
                first = isinstance(b, int) and b < 1
                last = isinstance(b, int) and b >= B - 1
                if not last:
                    rstd_of(b + 1)
                pair_sum(b, 0, 0)
                pair_sum(b, 0, 1)
                pair_sum(b, 1, 0)
                if not first:
                    rms_of(b - 1)
                pair_sum(b, 1, 1)
                pair_sum(b, 2, 0)
                if not first:
                    residual(b - 1, 0)
                    residual(b - 1, 1)
                pair_sum(b, 2, 1)
                if not first:
                    residual(b - 1, 2)
                    residual(b - 1, 3)
                pair_sum(b, 3, 0)
                pair_sum(b, 3, 1)

            over_batches(pool, body, 2)
            rms_of(B - 1)
            for k in range(QT):
                residual(B - 1, k)


def layer1_steps():
    steps = [("V", k) for k in range(2 * TT)] + [("Q", 0), ("K", 0)]
    for hp in range(HP):
        if hp + 1 < HP:
            steps += [("Q", hp + 1), ("K", hp + 1)]
        steps += [("S", hp)]
        if hp < TT:
            steps += [("F", hp)]
        if hp >= 2:
            steps += [("AV", hp - 2)]
    return steps + [("AV", HP - 2), ("AV", HP - 1)]


TWO_PI = (6.28125, 0.0019350051879882812, 3.019916050561733e-07)
ROUND = 1.5 * 2.0 ** 23
PI_BELOW = 3.1415925


def layer1(nc, io, x1_dram, out):
    with ExitStack() as ctx:
        def sb(name, shape, dt=F32):
            return ctx.enter_context(nc.sbuf_tensor(name, shape, dt))

        def banks(name, n=1):
            return ctx.enter_context(nc.psum_tensor(name, [P, n, 512], F32))

        def sem(name):
            return ctx.enter_context(nc.semaphore(name))

        W3 = 3 * H1 * D1
        win_h, win_l = sb("win_h", [P, KC, W3], F32R), sb("win_l", [P, KC, W3], F32R)
        cs_h, cs_l = sb("cs_h", [P, KC, 2 * E], F32R), sb("cs_l", [P, KC, 2 * E], F32R)
        wout = sb("wout", [P, HP, E])
        gk = sb("gk", [P, KC, H1, NREL])
        ud = sb("ud", [P, E])
        beta = sb("beta", [P, H1, NREL])
        bqk, bv, bout = sb("bqk", [P, 2 * HP]), sb("bv", [P, H1 * D1]), sb("bout", [P, E])
        ident = sb("ident1", [P, P])
        apart = sb("apart", [P, BLK])
        own = sb("own", [P, NREL])
        kdx = sb("kdx", [P, 2, NREL])
        mhalf, halfpi = sb("mhalf1", [P, TT]), sb("halfpi", [P, 1])
        work = sb("work", [P, KC * W3])
        v = work[:, 0:TT * H1 * D1].rearrange("p (t n) -> p t n", t=TT)
        rm = work[:, TT * H1 * D1:].rearrange("p (t h k) -> p t h k", t=TT, h=H1)
        xb, xn, xr = sb("xb1", [P, TT, E]), sb("xn1", [P, TT, E]), sb("xr1", [P, TT, E])
        stat, mv = sb("stat1", [P, TT, 6]), sb("mv1", [P, TT, 2])
        veps, rstd = sb("veps1", [P, TT]), sb("rstd1", [P, TT])
        xt = sb("xt1", [P, KC, TOK])
        xt_h, xt_l = sb("xt_h1", [P, KC, TOK], F32R), sb("xt_l1", [P, KC, TOK], F32R)
        qt, kt = sb("qt", [P, 2, TOK]), sb("kt", [P, 2, TOK])
        sc, ex = sb("sc", [P, 2, 2, TT, BLK]), sb("ex", [P, 2, 2, TT, BLK])
        mx, sm, rc = sb("mx", [P, 2, 2, TT]), sb("sm", [P, 2, 2, TT]), sb("rc", [P, 2, 2, TT])
        ec = sb("ec", [P, 2, 2, TT, NREL])
        pt = [sb(f"pt{i}", [P, 2, TT, P]) for i in range(2)]
        ot = sb("ot1", [P, HP, TOK])
        r15, rt = sb("r15", [P, TT, H1, 2 * NREL - 1]), sb("rt", [P, TT, H1, NREL])
        p15, pc = sb("p15", [P, TT, H1, 2 * NREL - 1]), sb("pc", [P, TT, H1, NREL])
        pd = sb("pd", [P, TT, H1, NREL])
        pdt = sb("pdt", [P, TOK])
        sq = sb("sq", [P, 2, 2 * E])
        q2, th = sb("q2", [P, TT, E]), sb("th1", [P, TT, E])
        so = sb("so", [P, 2, E])
        wqn = ot[:, 0:4, :].rearrange("p a b -> p (a b)").rearrange("p (h c) -> p h c", h=HP)
        vdx = ot[:, 4:6, :].rearrange("p a b -> p (a b)").rearrange("p (h c) -> p h c", h=HP)
        kdb = ot[:, 6, 0:HP * 2 * NREL].rearrange("p (h c) -> p h c", h=HP)
        ones = ot[:, 7, 0:P]
        ang = [t[:, 0:KC, :] for t in (xb, xn)]
        noise = [t[:, 0:KC, :] for t in (q2, th)]
        turns = [xb[:, KC:2 * KC, :], xn[:, KC:2 * KC, :]]
        cs = xr[:, :, :].rearrange("p (k a) n -> p k (a n)", k=KC)

        pr = banks("pr", 2)
        s_ps = banks("s_ps", 2)
        o_ps = banks("o_ps", 2)
        misc = banks("misc1")[:, 0, :]
        fin = banks("fin")[:, 0, :]

        m = Semaphores()
        m.w_load = sem("w_load1")
        m.w_high = sem("w_high1")
        m.w_low = sem("w_low1")
        m.b_load = sem("b_load1")
        m.theta_load = sem("theta_load1")
        m.trig = sem("trig1")
        m.sin_ok = sem("sin_ok1")
        m.cs_high = sem("cs_high1")
        m.cs_low = sem("cs_low1")
        m.zero_pt = sem("zero_pt1")
        m.consts_ok = sem("consts_ok1")
        m.kdb_ok = sem("kdb_ok1")
        m.g_psum = sem("g_psum1")
        m.g_ok = sem("g_ok1")
        m.x_load = sem("x_load1")
        m.stats = sem("stats1")
        m.aggr = sem("aggr1")
        m.veps_ok = sem("veps_ok1")
        m.rstd_ok = sem("rstd_ok1")
        m.xn_ok = sem("xn_ok1")
        m.xt_psum = sem("xt_psum1")
        m.xt_high = sem("xt_high1")
        m.xt_low = sem("xt_low1")
        m.r_psum = sem("r_psum1")
        m.r_evac = sem("r_evac1")
        m.r_flip = sem("r_flip1")
        m.r_sum = sem("r_sum1")
        m.rm_ok = sem("rm_ok1")
        m.v_psum = sem("v_psum1")
        m.v_ok = sem("v_ok1")
        m.qk_psum = sem("qk_psum1")
        m.qk_ok = sem("qk_ok1")
        m.s_psum = sem("s_psum1")
        m.sc_ok = sem("sc_ok1")
        m.mx_ok = sem("mx_ok1")
        m.sub_ok = sem("sub_ok1")
        m.ex_ok = sem("ex_ok1")
        m.ec_ok = sem("ec_ok1")
        m.sm_ok = sem("sm_ok1")
        m.rc_ok = sem("rc_ok1")
        m.pc_ok = sem("pc_ok1")
        m.p_ok = sem("p_ok1")
        m.pt_ok = sem("pt_ok1")
        m.o_psum = sem("o_psum1")
        m.ot_ok = sem("ot_ok1")
        m.f_psum = sem("f_psum1")
        m.sq_ok = sem("sq_ok1")
        m.q2_ok = sem("q2_ok1")
        m.sqrt_ok = sem("sqrt_ok1")
        m.tanh_ok = sem("tanh_ok1")
        m.gate_ok = sem("gate_ok1")
        m.p15_zero = sem("p15_zero1")
        m.p15_sum = sem("p15_sum1")
        m.pd_ok = sem("pd_ok1")
        m.pd_psum = sem("pd_psum1")
        m.pdt_ok = sem("pdt_ok1")
        m.w_psum = sem("w_psum1")
        m.so_ok = sem("so_ok1")
        m.sg_ok = sem("sg_ok1")
        m.xr_load = sem("xr_load1")
        m.x2_ok = sem("x2_ok1")
        m.stored_even = sem("stored_even1")
        m.stored_odd = sem("stored_odd1")
        m.sp_passed = sem("sp_passed1")
        m.dve_passed = sem("dve_passed1")
        m.pool_passed = sem("pool_passed1")
        m.pe_passed = sem("pe_passed1")
        m.stored = (m.stored_even, m.stored_odd)

        def drained(kind, i, k):
            return {"V": (m.v_ok, 2 * TT * i + k + 1), "Q": (m.qk_ok, 2 * HP * i + 2 * k + 1),
                    "K": (m.qk_ok, 2 * HP * i + 2 * k + 2), "F": (m.sq_ok, TT * i + k + 1),
                    "W": (m.so_ok, TT * i + k + 1), "R": (m.r_evac, i + 1), "XT": (m.xt_low, KC * i + k + 1),
                    "PD": (m.pdt_ok, i + 1)}[kind]

        steps = layer1_steps()
        through_pr = [x for x in steps if x[0] in "VQKF"] + [("W", 1), ("W", 2)]
        assert len(through_pr) % 2 == 0
        BLOADS, TLOADS = 11, 4

        block = ctx.enter_context(nc.Block())

        @block.sync
        def _(sp):
            sp.dma_start(work[:, :].rearrange("p (k n) -> p k n", k=KC),
                         io["win"].rearrange("(k p) n -> p k n", p=P)).then_inc(m.w_load, 16)
            for dst, name in ((ang[0], "theta"), (ang[1], "phi"), (noise[0], "theta_noise"), (noise[1], "phi_noise")):
                sp.dma_start(dst, io[name].rearrange("(k p) n -> p k n", p=P)).then_inc(m.theta_load, 16)
            for dst, src in (
                    (wqn, io["wqn"].rearrange("(h p) c -> p h c", p=P)), (vdx, io["vdx"]), (kdx[:, :, :], io["kdx"]),
                    (wout[:, :, :], io["wout"].rearrange("(h p) c -> p h c", p=P)), (bqk[:, :], io["bqk"]),
                    (bv[:, :], io["bv"].partition_broadcast(P)), (bout[:, :], io["bout"].partition_broadcast(P)),
                    (ident[:, :], io["ident"]), (apart[:, :], io["apart"]), (own[:, :], io["own"]),
                    (ones, io["ones"])):
                sp.dma_start(dst, src).then_inc(m.b_load, 16)

            def rows(i):
                return x1_dram.rearrange("n s c -> (n s) c").rearrange("(i t p) c -> i p t c", t=TT, p=P)[i]

            def load_x(i):
                wait(sp, m.xn_ok, i)
                stand_alone(sp, m.sp_passed)
                sp.dma_start(xb[:, :, :], rows(i)).then_inc(m.x_load, 16)

            sp.wait_ge(m.sin_ok, 2)
            load_x(0)
            sp.wait_ge(m.cs_low, 1)

            def body(i):
                wait(sp, m.x2_ok, TT * i)
                stand_alone(sp, m.sp_passed)
                sp.dma_start(xr[:, :, :], rows(i)).then_inc(m.xr_load, 16)
                if not (isinstance(i, int) and i >= NT1 - 1):
                    load_x(i + 1)
                o_rows = out.rearrange("n s c -> (n s) c").rearrange("(i t p) c -> i t p c", t=TT, p=P)
                for t in range(TT):
                    sp.wait_ge(m.x2_ok, TT * i + t + 1)
                    stand_alone(sp, m.sp_passed)
                    sp.dma_start(o_rows[i, t], so[:, t % 2, :]).then_inc(m.stored[t % 2], 16)

            over_batches(sp, body)
            for stored in m.stored:
                sp.wait_ge(stored, 16 * NT1 * TT // 2)

        @block.tensor
        def _(pe):
            pe.wait_ge(m.b_load, 16 * BLOADS)
            for hp in range(HP):
                for kc in range(KC):
                    pe.matmul(misc[:, kc * P + 2 * NREL * hp:kc * P + 2 * NREL * (hp + 1)],
                              wqn[:, hp, kc * P:(kc + 1) * P], kdx[:, :, :].rearrange("p a b -> p (a b)"),
                              start=True, stop=True)
            for hp in range(HP):
                mm = pe.matmul(fin[:, 0:E], vdx[:, hp, :], wout[:, hp, :], start=(hp == 0), stop=(hp == HP - 1))
            pe.wait_ge(m.kdb_ok, HP)
            for hp in range(HP):
                mm = pe.matmul(o_ps[:, 0, 2 * NREL * hp:2 * NREL * (hp + 1)], ones, kdb[:, hp, :],
                               start=True, stop=True)
            mm.then_inc(m.g_psum, 1)
            pe.wait_ge(m.g_ok, 3)
            pe.wait_ge(m.w_low, 1)
            pe.wait_ge(m.cs_low, 1)
            pe.wait_ge(m.zero_pt, 2)

            prev_misc = [None]

            def misc_free():
                if prev_misc[0] is not None:
                    wait(pe, *drained(*prev_misc[0]))

            def three(dst, w_h, w_l, x_h, x_l, inc):
                n = 0
                for kc in range(KC):
                    for a, b in ((w_h, x_h), (w_h, x_l), (w_l, x_h)):
                        mm = pe.matmul(dst, a(kc), b(kc), start=(n == 0), stop=(n == 3 * KC - 1))
                        n += 1
                mm.then_inc(inc, 1)

            def transposes(i):
                pe.wait_ge(m.xn_ok, i + 1)
                for kc in range(KC):
                    misc_free()
                    for t in range(TT):
                        mm = pe.transpose(misc[:, t * P:(t + 1) * P], xn[:, t, kc * P:(kc + 1) * P], ident[:, :])
                    mm.then_inc(m.xt_psum, 1)
                    prev_misc[0] = ("XT", i, kc)

            def free_pr(i, kind, k):
                n = through_pr.index((kind, k))
                if n >= 2:
                    wait(pe, *drained(through_pr[n - 2][0], i, through_pr[n - 2][1]))
                elif not (isinstance(i, int) and i < 1):
                    wait(pe, *drained(through_pr[n - 2][0], i - 1, through_pr[n - 2][1]))
                return pr[:, n % 2, :]

            transposes(0)

            def body(i):
                last = isinstance(i, int) and i >= NT1 - 1
                if not isinstance(i, int):
                    prev_misc[0] = ("PD", i - 1, 0)
                misc_free()
                pe.wait_ge(m.xt_low, KC * (i + 1))
                for t in range(TT):
                    for kc in range(KC):
                        mm = pe.matmul(misc[:, t * P:(t + 1) * P], xt[:, kc, t * P:(t + 1) * P],
                                       gk[:, kc, :, :].rearrange("p h r -> p (h r)"), start=(kc == 0), stop=(kc == KC - 1))
                mm.then_inc(m.r_psum, 1)
                prev_misc[0] = ("R", i, 0)

                for kind, k in steps:
                    if kind == "V":
                        t, half = k // 2, k % 2
                        c = 2 * H1 * D1 + 512 * half
                        three(free_pr(i, kind, k),
                              lambda kc: xt_h[:, kc, t * P:(t + 1) * P], lambda kc: xt_l[:, kc, t * P:(t + 1) * P],
                              lambda kc: win_h[:, kc, c:c + 512], lambda kc: win_l[:, kc, c:c + 512], m.v_psum)
                    if kind in ("Q", "K"):
                        c = H1 * D1 * (kind == "K") + P * k
                        three(free_pr(i, kind, k),
                              lambda kc: win_h[:, kc, c:c + P], lambda kc: win_l[:, kc, c:c + P],
                              lambda kc: xt_h[:, kc, :], lambda kc: xt_l[:, kc, :], m.qk_psum)
                    if kind == "F":
                        three(free_pr(i, kind, k),
                              lambda kc: xt_h[:, kc, k * P:(k + 1) * P], lambda kc: xt_l[:, kc, k * P:(k + 1) * P],
                              lambda kc: cs_h[:, kc, :], lambda kc: cs_l[:, kc, :], m.f_psum)
                    if kind == "S":
                        pe.wait_ge(m.qk_ok, 2 * HP * i + 2 * k + 2)
                        wait(pe, m.sc_ok, HP * i + k)
                        stand_alone(pe, m.pe_passed)
                        for blk in range(NBLK):
                            q, t = blk % 4, blk // 4
                            for h in range(2):
                                mm = pe.matmul(s_ps[BLK * q:BLK * (q + 1), h, BLK * t:BLK * (t + 1)],
                                               qt[D1 * h:D1 * (h + 1), k % 2, BLK * blk:BLK * (blk + 1)],
                                               kt[D1 * h:D1 * (h + 1), k % 2, BLK * blk:BLK * (blk + 1)],
                                               start=True, stop=True)
                        mm.then_inc(m.s_psum, 1)
                    if kind == "AV":
                        pe.wait_ge(m.pt_ok, 4 * (HP * i + k + 1))
                        if k == 0:
                            pe.wait_ge(m.v_ok, 2 * TT * (i + 1))
                            wait(pe, m.so_ok, TT * i)
                        wait(pe, m.ot_ok, HP * i + k - 1)
                        for t in range(TT):
                            for h in range(2):
                                c = D1 * (2 * k + h)
                                mm = pe.matmul(o_ps[D1 * h:D1 * (h + 1), k % 2, P * t:P * (t + 1)],
                                               v[:, t, c:c + D1], pt[k % 2][:, h, t, :], start=True, stop=True)
                        mm.then_inc(m.o_psum, 1)

                def w_bank(t):
                    return (fin, pr[:, through_pr.index(("W", 1)) % 2, :], pr[:, through_pr.index(("W", 2)) % 2, :],
                            o_ps[:, 0, :])[t]

                pe.wait_ge(m.ot_ok, HP * (i + 1))
                for t in range(TT):
                    if t == 0:
                        wait(pe, m.so_ok, TT * i)
                    if t in (1, 2):
                        free_pr(i, "W", t)
                    for hp in range(HP):
                        pe.matmul(w_bank(t)[:, 0:E], ot[:, hp, t * P:(t + 1) * P], wout[:, hp, :],
                                  start=(hp == 0), stop=False)
                if not last:
                    transposes(i + 1)
                pe.wait_ge(m.pd_ok, 2 * (i + 1))
                misc_free()
                for t in range(TT):
                    mm = pe.transpose(misc[:, t * P:(t + 1) * P], pd[:, t, :, :].rearrange("p h r -> p (h r)"), ident[:, :])
                mm.then_inc(m.pd_psum, 1)
                prev_misc[0] = ("PD", i, 0)
                pe.wait_ge(m.pdt_ok, i + 1)
                for t in range(TT):
                    pe.matmul(w_bank(t)[:, 0:E], pdt[:, t * P:(t + 1) * P], ud[:, :],
                              start=False, stop=True).then_inc(m.w_psum, 1)

            over_batches(pe, body)

        @block.scalar
        def _(act):
            act.wait_ge(m.w_load, 16)
            act.activation(win_h[:, :, :].rearrange("p k n -> p (k n)"), work[:, :], ACT.Copy).then_inc(m.w_high, 1)
            act.wait_ge(m.trig, 8)
            act.activation(cs[:, :, 0:E], turns[0], ACT.Sin, scale=-1.0, bias=halfpi[:, 0:1]).then_inc(m.sin_ok, 1)
            act.wait_ge(m.trig, 15)
            act.activation(cs[:, :, E:2 * E], ang[1], ACT.Sin).then_inc(m.sin_ok, 1)
            act.wait_ge(m.sin_ok, 2)
            act.activation(cs_h[:, :, :], cs, ACT.Copy).then_inc(m.cs_high, 1)
            act.wait_ge(m.g_psum, 1)
            act.activation(gk[:, :, :, :].rearrange("p k h r -> p (k h r)"), misc[:, 0:KC * P], ACT.Copy).then_inc(m.g_ok, 1)
            act.activation(ud[:, :], fin[:, 0:E], ACT.Copy).then_inc(m.g_ok, 1)
            act.activation(beta[:, :, :].rearrange("p h r -> p (h r)"), o_ps[:, 0, 0:P], ACT.Copy).then_inc(m.g_ok, 1)

            def transposed(i):
                for kc in range(KC):
                    act.wait_ge(m.xt_psum, KC * i + kc + 1)
                    if kc == 0:
                        wait(act, m.qk_psum, 2 * HP * i)
                        wait(act, m.f_psum, TT * i)
                        wait(act, m.v_psum, 2 * TT * i)
                        wait(act, m.r_psum, i)
                    act.activation(xt[:, kc, :], misc[:, :], ACT.Copy)
                    act.activation(xt_h[:, kc, :], misc[:, :], ACT.Copy).then_inc(m.xt_high, 1)

            transposed(0)

            def exp_pair(i, k):
                act.wait_ge(m.sub_ok, HP * i + k + 1)
                wait(act, m.p_ok, HP * i + k - 1)
                act.activation(ex[:, k % 2, :, :, :], sc[:, k % 2, :, :, :], ACT.Exp, scale=D1 ** -0.5).then_inc(m.ex_ok, 1)

            def body(i):
                last = isinstance(i, int) and i >= NT1 - 1
                for kind, k in steps:
                    if kind in ("Q", "K"):
                        side = int(kind == "K")
                        n = 2 * HP * i + 2 * k + side
                        act.wait_ge(m.qk_psum, n + 1)
                        wait(act, m.s_psum, HP * i + k - 1)
                        bank = pr[:, through_pr.index((kind, k)) % 2, :]
                        act.activation((qt, kt)[side][:, k % 2, :], bank, ACT.Identity,
                                       bias=bqk[:, HP * side + k:HP * side + k + 1]).then_inc(m.qk_ok, 1)
                    if kind == "F":
                        act.wait_ge(m.f_psum, TT * i + k + 1)
                        wait(act, m.q2_ok, TT * i + k - 1)
                        act.activation(sq[:, k % 2, :], pr[:, through_pr.index((kind, k)) % 2, :],
                                       ACT.Square).then_inc(m.sq_ok, 1)
                    if kind == "S" and k >= 1:
                        exp_pair(i, k - 1)
                    if kind == "AV":
                        if k == HP - 2:
                            exp_pair(i, HP - 1)
                        act.wait_ge(m.o_psum, HP * i + k + 1)
                        if k == 0:
                            wait(act, m.w_psum, TT * i)
                        act.activation(ot[:, k, :], o_ps[:, k % 2, :], ACT.Copy).then_inc(m.ot_ok, 1)
                act.wait_ge(m.q2_ok, TT * (i + 1))
                wait(act, m.gate_ok, i)
                act.activation(q2[:, :, :], q2[:, :, :], ACT.Sqrt).then_inc(m.sqrt_ok, 1)
                act.wait_ge(m.sqrt_ok, i + 1)
                act.activation(th[:, :, :], q2[:, :, :], ACT.Tanh, scale=0.5).then_inc(m.tanh_ok, 1)
                if not last:
                    transposed(i + 1)
                act.wait_ge(m.pd_psum, i + 1)
                act.activation(pdt[:, :], misc[:, :], ACT.Copy).then_inc(m.pdt_ok, 1)

            over_batches(act, body)

        @block.vector
        def _(dve):
            for i in range(2):
                dve.memset(pt[i][:, :, :, :], 0.0).then_inc(m.zero_pt, 1)
            dve.memset(mhalf[:, :], -0.5).then_inc(m.consts_ok, 1)
            dve.memset(halfpi[:, :], float(np.pi / 2)).then_inc(m.consts_ok, 1)
            dve.wait_ge(m.theta_load, 16 * TLOADS)
            dve.wait_ge(m.consts_ok, 2)
            n = 0
            for a in range(2):
                ops = [lambda: dve.tensor_tensor(ang[a], ang[a], noise[a], ALU.add),
                       lambda: dve.tensor_scalar(turns[a], ang[a], float(1 / (2 * np.pi)), ROUND, ALU.mult, ALU.add),
                       lambda: dve.tensor_scalar(turns[a], turns[a], ROUND, None, ALU.subtract)]
                ops += [(lambda c: lambda: dve.scalar_tensor_tensor(ang[a], turns[a], -c, ang[a], op0=ALU.mult, op1=ALU.add))(c)
                        for c in TWO_PI]
                ops += [lambda: dve.tensor_scalar(ang[a], ang[a], PI_BELOW, -PI_BELOW, ALU.min, ALU.max)]
                if a == 0:
                    ops += [lambda: dve.scalar_tensor_tensor(turns[0], ang[0], -1.0, ang[0], op0=ALU.mult, op1=ALU.max)]
                for op in ops:
                    op().then_inc(m.trig, 1)
                    n += 1
                    dve.wait_ge(m.trig, n)
            dve.wait_ge(m.w_high, 1)
            dve.tensor_tensor(win_l[:, :, :].rearrange("p k n -> p (k n)"), work[:, :],
                              win_h[:, :, :].rearrange("p k n -> p (k n)").bitcast(F32), ALU.subtract).then_inc(m.w_low, 1)
            dve.wait_ge(m.b_load, 16 * BLOADS)
            for hp in range(HP):
                dve.tensor_scalar(kdb[:, hp, :], kdx[:, :, :].rearrange("p a b -> p (a b)"), bqk[:, hp:hp + 1], None,
                                  ALU.mult).then_inc(m.kdb_ok, 1)
            dve.wait_ge(m.cs_high, 1)
            dve.tensor_tensor(cs_l[:, :, :], cs, cs_h[:, :, :].bitcast(F32), ALU.subtract).then_inc(m.cs_low, 1)
            dve.wait_ge(m.w_low, 1)
            dve.wait_ge(m.g_ok, 3)

            def norm_stats(i):
                dve.wait_ge(m.x_load, 16 * (i + 1))
                for t in range(TT):
                    dve.bn_stats(stat[:, t, :], xb[:, t, :]).then_inc(m.stats, 1)
                dve.wait_ge(m.stats, TT * (i + 1))
                wait(dve, m.veps_ok, i)
                stand_alone(dve, m.dve_passed)
                for t in range(TT):
                    dve.bn_aggr(mv[:, t, :], stat[:, t, :]).then_inc(m.aggr, 1)

            def normalise(i):
                dve.wait_ge(m.rstd_ok, i + 1)
                wait(dve, m.xt_psum, KC * i)
                for t in range(TT):
                    ins = dve.tensor_scalar(xn[:, t, :], xb[:, t, :], mv[:, t, 0:1], rstd[:, t:t + 1],
                                            ALU.subtract, ALU.mult)
                ins.then_inc(m.xn_ok, 1)

            def low_parts(i):
                for kc in range(KC):
                    dve.wait_ge(m.xt_high, KC * i + kc + 1)
                    dve.tensor_tensor(xt_l[:, kc, :], misc[:, :], xt_h[:, kc, :].bitcast(F32),
                                      ALU.subtract).then_inc(m.xt_low, 1)

            def key_distances(i):
                dve.wait_ge(m.r_psum, i + 1)
                wait(dve, m.r_sum, NREL * i)
                dve.tensor_tensor(r15[:, :, :, NREL - 1:], misc[:, :].rearrange("p (t h r) -> p t h r", t=TT, h=H1),
                                  beta[:, :, :].unsqueeze(1).to_broadcast([P, TT, H1, NREL]), ALU.add).then_inc(m.r_evac, 1)
                dve.wait_ge(m.r_evac, i + 1)
                dve.tensor_copy(r15[:, :, :, 0:NREL - 1], r15[:, :, :, 2 * NREL - 2:NREL - 1:-1]).then_inc(m.r_flip, 1)

            def own_keys(i, s):
                src = r15[:, :, :, NREL - 1 - s:2 * NREL - 1 - s]
                if s == 0:
                    dve.wait_ge(m.r_flip, i + 1)
                    wait(dve, m.rm_ok, TT * i)
                    dve.tensor_scalar(rt[:, :, :, :], src, own[:, 0:1], None, ALU.mult).then_inc(m.r_sum, 1)
                else:
                    dve.wait_ge(m.r_sum, NREL * i + s)
                    dve.scalar_tensor_tensor(rt[:, :, :, :], src, own[:, s:s + 1], rt[:, :, :, :],
                                             op0=ALU.mult, op1=ALU.add).then_inc(m.r_sum, 1)

            def scores(i, k):
                n = HP * i + k
                dve.wait_ge(m.s_psum, n + 1)
                wait(dve, m.ex_ok, n - 1)
                if k == 0:
                    dve.wait_ge(m.rm_ok, TT * (i + 1))
                a = sc[:, k % 2, :, :, :]
                dve.tensor_tensor(a, s_ps[:, :, 0:TT * BLK].rearrange("p h (t k) -> p h t k", t=TT),
                                  rm[:, :, 2 * k:2 * k + 2, :].rearrange("p t h k -> p h t k"), ALU.add).then_inc(m.sc_ok, 1)
                dve.wait_ge(m.sc_ok, n + 1)
                dve.tensor_reduce(mx[:, k % 2, :, :], a, X, ALU.max).then_inc(m.mx_ok, 1)
                dve.wait_ge(m.mx_ok, n + 1)
                dve.tensor_tensor(a, a, mx[:, k % 2, :, :].unsqueeze(3).to_broadcast([P, 2, TT, BLK]),
                                  ALU.subtract).then_inc(m.sub_ok, 1)

            def probabilities(i, k):
                n = HP * i + k
                e = ex[:, k % 2, :, :, :]
                dve.wait_ge(m.ex_ok, n + 1)
                wait(dve, m.pc_ok, n - 1)
                dve.tensor_reduce(ec[:, k % 2, :, :, :].rearrange("p h t s -> p (h t) s"),
                                  e.rearrange("p h t (n s) -> p (h t) s n", n=4), X, ALU.add).then_inc(m.ec_ok, 1)
                dve.wait_ge(m.ec_ok, n + 1)
                dve.tensor_reduce(sm[:, k % 2, :, :], ec[:, k % 2, :, :, :], X, ALU.add).then_inc(m.sm_ok, 1)
                dve.wait_ge(m.sm_ok, n + 1)
                dve.reciprocal(rc[:, k % 2, :, :], sm[:, k % 2, :, :]).then_inc(m.rc_ok, 1)
                dve.wait_ge(m.rc_ok, n + 1)
                if k == 0:
                    wait(dve, m.p15_sum, NREL * i)
                dve.tensor_tensor(pc[:, :, 2 * k:2 * k + 2, :].rearrange("p t h s -> p h t s"), ec[:, k % 2, :, :, :],
                                  rc[:, k % 2, :, :].unsqueeze(3).to_broadcast([P, 2, TT, NREL]), ALU.mult).then_inc(m.pc_ok, 1)
                wait(dve, m.pt_ok, 4 * (n - 1))
                dve.tensor_tensor(e, e, rc[:, k % 2, :, :].unsqueeze(3).to_broadcast([P, 2, TT, BLK]),
                                  ALU.mult).then_inc(m.p_ok, 1)
                dve.wait_ge(m.p_ok, n + 1)
                wait(dve, m.o_psum, n - 1)
                for q in range(4):
                    rows = slice(BLK * q, BLK * (q + 1))
                    dve.transpose(pt[k % 2][rows, :, :, :].rearrange("p h t k -> p (h t) k")[:, :, rows],
                                  e[rows, :, :, :].rearrange("p h t k -> p (h t) k")).then_inc(m.pt_ok, 1)

            def by_distance(i):
                wait(dve, m.pd_ok, 2 * i)
                dve.memset(p15[:, :, :, :], 0.0).then_inc(m.p15_zero, 1)
                dve.wait_ge(m.p15_zero, i + 1)
                dve.wait_ge(m.pc_ok, HP * (i + 1))
                for s in range(NREL):
                    wait(dve, m.p15_sum, NREL * i + s)
                    dst = p15[:, :, :, NREL - 1 - s:2 * NREL - 1 - s]
                    dve.scalar_tensor_tensor(dst, pc[:, :, :, :], own[:, s:s + 1], dst,
                                             op0=ALU.mult, op1=ALU.add).then_inc(m.p15_sum, 1)
                dve.wait_ge(m.p15_sum, NREL * (i + 1))
                wait(dve, m.pd_psum, i)
                dve.tensor_copy(pd[:, :, :, 0:1], p15[:, :, :, NREL - 1:NREL]).then_inc(m.pd_ok, 1)
                dve.tensor_tensor(pd[:, :, :, 1:], p15[:, :, :, NREL:], p15[:, :, :, NREL - 2::-1], ALU.add).then_inc(m.pd_ok, 1)

            def output(i, t):
                dve.wait_ge(m.w_psum, TT * i + t + 1)
                if t < 2:
                    wait(dve, m.stored[t], 16 * 2 * i)
                else:
                    dve.wait_ge(m.stored[t % 2], 16 * (2 * i + 1))
                bank = (fin, pr[:, through_pr.index(("W", 1)) % 2, :], pr[:, through_pr.index(("W", 2)) % 2, :],
                        o_ps[:, 0, :])[t]
                dve.tensor_tensor(so[:, t % 2, :], bank[:, 0:E], bout[:, :], ALU.add).then_inc(m.so_ok, 1)
                dve.wait_ge(m.so_ok, TT * i + t + 1)
                dve.scalar_tensor_tensor(so[:, t % 2, :], so[:, t % 2, :], 0.5, q2[:, t, :], op0=ALU.mult,
                                         op1=ALU.mult).then_inc(m.sg_ok, 1)
                dve.wait_ge(m.sg_ok, TT * i + t + 1)
                if t == 0:
                    dve.wait_ge(m.xr_load, 16 * (i + 1))
                dve.tensor_tensor(so[:, t % 2, :], so[:, t % 2, :], xr[:, t, :], ALU.add).then_inc(m.x2_ok, 1)

            norm_stats(0)
            normalise(0)
            low_parts(0)

            def body(i):
                last = isinstance(i, int) and i >= NT1 - 1
                key_distances(i)
                for k in range(2 * TT):
                    dve.wait_ge(m.v_psum, 2 * TT * i + k + 1)
                    if k == 0:
                        wait(dve, m.o_psum, HP * i)
                    t, half = k // 2, k % 2
                    dve.tensor_tensor(v[:, t, 512 * half:512 * (half + 1)], pr[:, through_pr.index(("V", k)) % 2, :],
                                      bv[:, 512 * half:512 * (half + 1)], ALU.add).then_inc(m.v_ok, 1)
                    own_keys(i, k)
                for k in range(HP):
                    scores(i, k)
                    if k >= 1:
                        probabilities(i, k - 1)
                    if k == 1 and not last:
                        norm_stats(i + 1)
                    if k == 3 and not last:
                        normalise(i + 1)
                probabilities(i, HP - 1)
                by_distance(i)
                dve.wait_ge(m.tanh_ok, i + 1)
                dve.scalar_tensor_tensor(q2[:, :, :], th[:, :, :], 1.0, q2[:, :, :], op0=ALU.add,
                                         op1=ALU.mult).then_inc(m.gate_ok, 1)
                dve.wait_ge(m.gate_ok, i + 1)
                if not last:
                    low_parts(i + 1)
                for t in range(TT):
                    output(i, t)

            over_batches(dve, body)

        @block.gpsimd
        def _(pool):
            pool.wait_ge(m.consts_ok, 2)
            pool.wait_ge(m.x_load, 16)

            def rstd_of(i):
                pool.wait_ge(m.aggr, TT * (i + 1))
                wait(pool, m.xn_ok, i)
                stand_alone(pool, m.pool_passed)
                pool.tensor_scalar(veps[:, :], mv[:, :, 1], LN_EPS, None, ALU.add).then_inc(m.veps_ok, 1)
                pool.wait_ge(m.veps_ok, i + 1)
                pool.tensor_tensor(rstd[:, :], veps[:, :], mhalf[:, :], ALU.pow).then_inc(m.rstd_ok, 1)

            rstd_of(0)
            pool.wait_ge(m.b_load, 16 * BLOADS)

            def body(i):
                last = isinstance(i, int) and i >= NT1 - 1
                pool.wait_ge(m.r_sum, NREL * (i + 1))
                wait(pool, m.sc_ok, HP * i)
                for t in range(TT):
                    pool.tensor_tensor(rm[:, t, :, :].rearrange("p h (n s) -> p h n s", n=4),
                                       rt[:, t, :, :].unsqueeze(2).to_broadcast([P, H1, 4, NREL]),
                                       apart[:, :].rearrange("p (n s) -> p n s", n=4).unsqueeze(1).to_broadcast([P, H1, 4, NREL]),
                                       ALU.add).then_inc(m.rm_ok, 1)
                for t in range(TT):
                    pool.wait_ge(m.sq_ok, TT * i + t + 1)
                    if t == 0:
                        wait(pool, m.x2_ok, TT * i)
                    pool.tensor_tensor(q2[:, t, :], sq[:, t % 2, 0:E], sq[:, t % 2, E:2 * E], ALU.add).then_inc(m.q2_ok, 1)
                if not last:
                    rstd_of(i + 1)

            over_batches(pool, body)


def layout1(a):
    kd, vd = a["L1_attn_k_dist_emb"][:NREL], a["L1_attn_v_dist_emb"][:NREL]
    kdx = np.zeros((2, D1, 2, NREL), np.float32)
    vdx = np.zeros((2, D1, HP, H1, NREL), np.float32)
    for h in range(2):
        kdx[h, :, h, :] = kd.T
        for hp in range(HP):
            vdx[h, :, hp, 2 * hp + h, :] = vd.T
    p = np.arange(P)
    key = np.arange(BLK)
    out = {
        "win": a["L1_attn_W_in"].T,
        "wqn": a["L1_attn_W_in"][:H1 * D1],
        "bqk": a["L1_attn_b_in"][:2 * H1 * D1].reshape(2 * HP, P).T,
        "bv": a["L1_attn_b_in"][2 * H1 * D1:],
        "kdx": kdx.reshape(P, 2, NREL),
        "vdx": vdx.reshape(P, HP, H1 * NREL),
        "wout": a["L1_attn_W_out"].T,
        "bout": a["L1_attn_b_out"],
        "theta": a["L1_ffn_theta"], "phi": a["L1_ffn_phi"],
        "theta_noise": a["L1_ffn_theta_noise"], "phi_noise": a["L1_ffn_phi_noise"],
        "apart": np.where((p[:, None] % BLK) // NREL == key[None, :] // NREL, 0.0, NEG).astype(np.float32),
        "own": (p[:, None] % NREL == np.arange(NREL)[None, :]).astype(np.float32),
        "ones": np.ones((P, P), np.float32),
        "ident": np.eye(P, dtype=np.float32),
    }
    return {k: np.ascontiguousarray(v) for k, v in out.items()}


def layout0(a):
    def halves(w):
        return w.reshape(2, HG, 2, F0, E).transpose(4, 0, 2, 1, 3).reshape(E, HALF, HG * F0)

    pick = np.zeros((P, HALF, BLK), np.float32)
    which = np.zeros((2, HG, HG, S), np.float32)
    for i in range(HALF):
        pick[:, i, i] = 1.0
        which[:, i, i, :] = 1.0
    out = {
        "x": a["L0_attn_x"],
        "wqk": np.concatenate([halves(a["L0_attn_Wq"]), halves(a["L0_attn_Wk"])], axis=2),
        "wcat": np.concatenate([a["L0_attn_Wv"].T, a["L0_ffn_w_route"].T, a["L0_ffn_compress"].T], axis=1),
        "wo": a["L0_attn_Wo"].T,
        "normw": a["L0_attn_norm_w"].reshape(KC, P).T,
        "bo": a["L0_attn_bo"],
        "dw": a["L0_attn_diff_weight"].reshape(1),
        "routed": a["L0_ffn_routed"].transpose(0, 2, 1).reshape(NE * R, E),
        "ident": np.eye(P, dtype=np.float32),
        "rank8": np.arange(NE, 0, -1, dtype=np.float32),
        "pick": pick,
        "which": which.reshape(MROWS, HG, S),
    }
    return {k: np.ascontiguousarray(v) for k, v in out.items()}


def build(nc, io0, io1, out):
    x1 = nc.dram_tensor("x1", [S, B, E], F32).ap()
    layer0(nc, io0, x1)
    layer1(nc, io1, x1, out)


def kernel(**inputs):
    import concourse.bacc as bacc
    from concourse.bass_utils import run_bass_kernel_spmd as run

    nc = bacc.Bacc("TRN2", target_bir_lowering=False, num_devices=1)
    a = {k: np.asarray(v) for k, v in inputs.items()}
    arrays, io = {}, []
    for layer, layout in enumerate((layout0, layout1)):
        io.append({})
        for k, v in layout(a).items():
            arrays[f"in{layer}_{k}"] = v
            io[-1][k] = nc.dram_tensor(f"in{layer}_{k}", v.shape, mybir.dt.from_np(v.dtype), kind="ExternalInput").ap()
    out = nc.dram_tensor("out", [S, B, E], F32, kind="ExternalOutput").ap()
    build(nc, *io, out)
    r = run(nc, [arrays], core_ids=[0])
    return np.ascontiguousarray(r.results[0]["out"].transpose(1, 0, 2))
```

```python
from contextlib import ExitStack

import numpy as np

import concourse.bass as bass
from concourse import mybir

F32 = mybir.dt.float32
F32R = mybir.dt.float32r
I32 = mybir.dt.int32
ALU = mybir.AluOpType
ACT = mybir.ActivationFunctionType
X = mybir.AxisListType.X

P = 128
B, S, E = 8, 512, 256
KC = E // P
QT = S // P
LN_EPS = 1e-5

H0 = 8
DH0 = E // H0
F0 = DH0 // 2
HG = 4
HALF = 4
UNITS = 16
NE, R = 8, 16
WCAT = E + NE + R
STACK = 4 * F0
MROW = 96
MROWS = 2 * HG
LEAD = 24
S_BANK = [w % 3 for w in range(UNITS - 1)] + [1]
S_BACK = [next(d for d in range(1, UNITS) if S_BANK[w - d] == S_BANK[w]) for w in range(UNITS)]
D_PARTS = ((0, 0), (1, 1), (2, 0), (3, 1), (3, 0))
SUMS = 11
LAG = 2
SCALE0 = float(F0) ** -0.5
EPS32 = float(np.finfo(np.float32).eps)

H1 = 16
D1 = 64
HP = H1 // 2
NREL = 8
NS = 64
NT1 = S // NS
TOK = NS * B
TT = TOK // P
BLK = 32
NBLK = TOK // BLK
NEG = -1e30


class Semaphores:
    pass


def wait(eng, sem, value):
    if not (isinstance(value, int) and value <= 0):
        eng.wait_ge(sem, value)


def stand_alone(eng, passed):
    eng.sem_inc(passed, 1)


def over_batches(eng, body, before=1):
    for b in range(before):
        body(b)
    with eng.Fori(before, B - 1) as b:
        body(b)
    body(B - 1)


def layer0_jobs(b):
    nxt = not (isinstance(b, int) and b >= B - 1)
    prv = not (isinstance(b, int) and b < 1)
    jobs = [((0, 1), "PROJ", 4 * b + 3, 0), ((0, 4), "V", b, 2), ((0, 6), "V", b, 3), ((0, 9), "M", 4 * b + 1, 0)]
    if nxt:
        jobs += [((0, 11), "XT", b + 1, 0), ((0, 13), "XT", b + 1, 1)]
    if prv:
        jobs += [((0, 15), "TD", b - 1, 0), ((1, 1), "TA", b - 1, 0), ((1, 3), "TA", b - 1, 1),
                 ((1, 5), "TA", b - 1, 2), ((1, 7), "TA", b - 1, 3)]
    jobs += [((1, 9), "M", 4 * b + 2, 0)]
    if nxt:
        jobs += [((1, 11), "PROJ", 4 * b + 4, 0), ((1, 14), "V", b + 1, 0), ((2, 0), "PROJ", 4 * b + 5, 0)]
    if prv:
        jobs += [((2, 3), "OT", b - 1, 0), ((2, 5), "OT", b - 1, 1), ((2, 7), "ZT", b - 1, 0)]
    jobs += [((2, 9), "M", 4 * b + 3, 0)]
    if prv:
        jobs += [((2, 11), "WF", b - 1, 0), ((2, 14), "WF", b - 1, 1)]
    if nxt:
        jobs += [((3, 1), "PROJ", 4 * b + 6, 0)]
    if prv:
        jobs += [((3, 4), "WF", b - 1, 2), ((3, 7), "WF", b - 1, 3)]
    if nxt:
        jobs += [((3, 10), "M", 4 * b + 4, 0), ((3, 13), "V", b + 1, 1)]
    return jobs


FIRST_JOBS = [("XT", 0, 0), ("XT", 0, 1), ("PROJ", 0, 0), ("PROJ", 1, 0), ("PROJ", 2, 0),
              ("V", 0, 0), ("V", 0, 1), ("M", 0, 0)]
LAST_JOBS = [("TD", B - 1, 0)] + [("TA", B - 1, t) for t in range(QT)] + [("OT", B - 1, 0), ("OT", B - 1, 1),
             ("ZT", B - 1, 0)] + [("WF", B - 1, t) for t in range(QT)]


def layer0(nc, io, x1_dram):
    with ExitStack() as ctx:
        def sb(name, shape, dt=F32):
            return ctx.enter_context(nc.sbuf_tensor(name, shape, dt))

        def bank(name):
            return ctx.enter_context(nc.psum_tensor(name, [P, 512], F32))

        def sem(name):
            return ctx.enter_context(nc.semaphore(name))

        ident = sb("ident0", [P, P])
        wqk_h, wqk_l = sb("wqk_h", [P, KC, HALF, P], F32R), sb("wqk_l", [P, KC, HALF, P], F32R)
        wcat = sb("wcat", [P, KC, WCAT])
        wo = sb("wo", [P, KC, E])
        normw = sb("normw", [P, KC])
        routed = sb("routed", [P, E])
        bo = sb("bo", [P, E])
        dw = sb("dw", [P, 1])
        one_dw, neg_dw = sb("one_dw", [P, 1]), sb("neg_dw", [P, 1])
        rank8 = sb("rank8", [P, NE])
        pick = sb("pick", [P, HALF, BLK])
        mhalf = sb("mhalf", [P, QT])
        xb = sb("xb", [P, QT, E])
        stat, mv = sb("stat", [P, QT, 6]), sb("mv", [P, QT, 2])
        veps, rstd = sb("veps", [P, QT]), sb("rstd", [P, QT])
        xn = sb("xn", [P, QT, E])
        xt = sb("xt", [P, KC, S])
        xt_h, xt_l = sb("xt_h", [P, KC, S], F32R), sb("xt_l", [P, KC, S], F32R)
        qk_h, qk_l = sb("qk_h", [P, S], F32R), sb("qk_l", [P, S], F32R)
        qst = [sb(f"qst{i}", [P, HG, S], F32R) for i in range(HALF)]
        kst = [sb(f"kst{i}", [P, HG, S], F32R) for i in range(HALF)]
        vnew = sb("vnew", [P, QT, WCAT])
        v = sb("v", [P, QT, E])
        lc = sb("lc", [P, QT, NE + R])
        negmax = sb("negmax", [P, 2, QT, HG])
        msplit = sb("msplit", [P, QT, 2, HG], F32R)
        mrow = sb("mrow", [P, S], F32R)
        probs = sb("probs", [P, 4, HG, S])
        sums = sb("sums", [P, 2, HG, S])
        wqk = sums[:, 0, 0:2, :].rearrange("p a (k n) -> p a k n", k=HALF)
        which = probs[:, 0, :, :]
        at = sb("at", [P, HALF, S])
        dt_ = sb("dt", [P, S])
        rec = sb("rec", [P, QT, HALF, HG])
        an = sb("an", [P, HALF, HG, DH0])
        o = sb("o", [P, QT, E])
        ss, ms, rms = sb("ss", [P, QT]), sb("ms", [P, QT]), sb("rms", [P, QT])
        ot = sb("ot", [P, KC, S])
        gt = sb("gt", [P, 8, QT, NE])
        gs = sb("gs", [P, 8, QT])
        z, zt = sb("z", [P, QT, NE, R]), sb("zt", [P, S])
        th, s_, g_ = sb("th", [P, QT, E]), sb("s_", [P, QT, E]), sb("g_", [P, QT, E])
        xr, x1o = sb("xr", [P, QT, E]), sb("x1o", [P, 2, E])

        s_bank = [bank("s_bank0"), bank("s_bank1"), bank("s_bank2")]
        t_bank = [bank("t_bank0"), bank("t_bank1")]
        a_bank = bank("a_bank0")
        d_bank = bank("d_bank")
        misc = bank("misc0")

        park = nc.dram_tensor("park", [2, P, S], F32).ap()

        m = Semaphores()
        m.w_load = sem("w_load0")
        m.wsplit = sem("wsplit0")
        m.x_load = sem("x_load0")
        m.stats = sem("stats0")
        m.aggr = sem("aggr0")
        m.veps_ok = sem("veps_ok0")
        m.rstd_ok = sem("rstd_ok0")
        m.xn_ok = sem("xn_ok0")
        m.xt_psum = sem("xt_psum0")
        m.xt_high = sem("xt_high0")
        m.xt_low = sem("xt_low0")
        m.xt_sum = sem("xt_sum0")
        m.proj_psum = sem("proj_psum0")
        m.qk_high = sem("qk_high0")
        m.qk_low = sem("qk_low0")
        m.parked = sem("parked0")
        m.stacked = sem("stacked0")
        m.v_psum = sem("v_psum0")
        m.vnew_ok = sem("vnew_ok0")
        m.v_ok = sem("v_ok0")
        m.lc_ok = sem("lc_ok0")
        m.s_done = sem("s_done0")
        m.max_done = sem("max_done0")
        m.m_high = sem("m_high0")
        m.m_low = sem("m_low0")
        m.m_psum = sem("m_psum0")
        m.m_evac = sem("m_evac0")
        m.m_placed = sem("m_placed0")
        m.t_done = sem("t_done0")
        m.exp_done = sem("exp_done0")
        m.sum_ok = sem("sum_ok0")
        m.a_done = sem("a_done0")
        m.d_done = sem("d_done0")
        m.a_evac = sem("a_evac0")
        m.d_evac = sem("d_evac0")
        m.td_psum = sem("td_psum0")
        m.recip_ok = sem("recip_ok0")
        m.rec_ok = sem("rec_ok0")
        m.ta_psum = sem("ta_psum0")
        m.an_ok = sem("an_ok0")
        m.o_ok = sem("o_ok0")
        m.ss_ok = sem("ss_ok0")
        m.ms_ok = sem("ms_ok0")
        m.rms_ok = sem("rms_ok0")
        m.ot_psum = sem("ot_psum0")
        m.ot_evac = sem("ot_evac0")
        m.prod_ok = sem("prod_ok0")
        m.zeros = sem("zeros0")
        m.mhalf_ok = sem("mhalf_ok0")
        m.which_ok = sem("which_ok0")
        m.fold = sem("fold0")
        m.gate = sem("gate0")
        m.gate_d = sem("gate_d0")
        m.gate_e = sem("gate_e0")
        m.z_ok = sem("z_ok0")
        m.zt_psum = sem("zt_psum0")
        m.zt_evac = sem("zt_evac0")
        m.wf_psum = sem("wf_psum0")
        m.tanh_ok = sem("tanh_ok0")
        m.s_ok = sem("s_ok0")
        m.wf_gate = sem("wf_gate0")
        m.sg_ok = sem("sg_ok0")
        m.xr_load = sem("xr_load0")
        m.x1_ok = sem("x1_ok0")
        m.x1_stored_even = sem("x1_stored_even0")
        m.x1_stored_odd = sem("x1_stored_odd0")
        m.sp_passed = sem("sp_passed0")
        m.dve_passed = sem("dve_passed0")
        m.pool_passed = sem("pool_passed0")
        m.x1_stored = (m.x1_stored_even, m.x1_stored_odd)

        def drained(kind, i, k):
            return {"XT": (m.xt_low, KC * i + k + 1), "PROJ": (m.qk_low, i + 1), "V": (m.vnew_ok, QT * i + k + 1),
                    "M": (m.m_evac, i + 1), "TD": (m.recip_ok, i + 1), "TA": (m.an_ok, QT * i + k + 1),
                    "OT": (m.ot_evac, KC * i + k + 1), "ZT": (m.zt_evac, i + 1),
                    "WF": (m.wf_gate, QT * i + k + 1)}[kind]

        LOADS = 11
        block = ctx.enter_context(nc.Block())

        @block.sync
        def _(sp):
            sp.dma_start(xb[:, :, :], io["x"][0].rearrange("(t p) c -> p t c", p=P)).then_inc(m.x_load, 16)
            for dst, src in (
                    (ident[:, :], io["ident"]), (wqk, io["wqk"].rearrange("(k p) h n -> p k h n", p=P)),
                    (wcat[:, :, :], io["wcat"].rearrange("(k p) n -> p k n", p=P)),
                    (wo[:, :, :], io["wo"].rearrange("(k p) n -> p k n", p=P)),
                    (normw[:, :], io["normw"]), (routed[:, :], io["routed"]),
                    (bo[:, :], io["bo"].partition_broadcast(P)), (dw[:, :], io["dw"].partition_broadcast(P)),
                    (rank8[:, :], io["rank8"].partition_broadcast(P)), (pick[:, :, :], io["pick"]),
                    (which[MROW:MROW + MROWS], io["which"])):
                sp.dma_start(dst, src).then_inc(m.w_load, 16)

            def park_parts(i):
                sp.wait_ge(m.qk_high, i + 1)
                stand_alone(sp, m.sp_passed)
                wait(sp, m.stacked, 128 * i)
                sp.dma_start(park[0], qk_h[:, :].bitcast(F32)).then_inc(m.parked, 16)
                sp.wait_ge(m.qk_low, i + 1)
                sp.dma_start(park[1], qk_l[:, :].bitcast(F32)).then_inc(m.parked, 16)

            def fill_stacks(i, slot):
                sp.wait_ge(m.parked, 32 * i + 32)
                for r in range(4):
                    for side, stack, part in ((0, qst, r // 2), (1, kst, r % 2)):
                        src = park[part, 64 * side:64 * side + 64, :].rearrange("(h f) q -> f h q", f=F0)
                        sp.dma_start(stack[slot][F0 * r:F0 * r + F0, :, :].bitcast(F32), src).then_inc(m.stacked, 16)

            def place_max(i, slot):
                sp.wait_ge(m.m_evac, i + 1)
                sp.dma_start(qst[slot][MROW:MROW + MROWS, :, :].bitcast(F32),
                             mrow[MROW:MROW + MROWS, :].bitcast(F32).unsqueeze(1).to_broadcast([MROWS, HG, S])
                             ).then_inc(m.m_placed, 16)

            def load_x(b):
                wait(sp, m.xn_ok, QT * b)
                stand_alone(sp, m.sp_passed)
                sp.dma_start(xb[:, :, :], io["x"][b].rearrange("(t p) c -> p t c", p=P)).then_inc(m.x_load, 16)

            def load_residual(b):
                wait(sp, m.x1_ok, QT * b)
                stand_alone(sp, m.sp_passed)
                sp.dma_start(xr[:, :, :], io["x"][b].rearrange("(t p) c -> p t c", p=P)).then_inc(m.xr_load, 16)

            def store_x1(b, t):
                sp.wait_ge(m.x1_ok, QT * b + t + 1)
                stand_alone(sp, m.sp_passed)
                sp.dma_start(x1_dram[t * P:(t + 1) * P, b, :], x1o[:, t % 2, :]).then_inc(m.x1_stored[t % 2], 16)

            for i in range(3):
                park_parts(i)
                fill_stacks(i, i)
            place_max(0, 0)

            def body(b):
                for hf, v_, kind, i, k in slots(b):
                    if kind == "START" and hf == 0:
                        if not (isinstance(b, int) and b >= B - 1):
                            load_x(b + 1)
                        if not (isinstance(b, int) and b < 1):
                            load_residual(b - 1)
                    if kind == "PROJ":
                        park_parts(i)
                        fill_stacks(i, k)
                    if kind == "M":
                        place_max(i, k)
                    if kind == "WF" and k < QT - 1:
                        store_x1(i, k)
                if not (isinstance(b, int) and b < 1):
                    store_x1(b - 1, QT - 1)

            def slots(b):
                out = [(0, -1, "START", 0, 0)]
                for (hf, v_), kind, i, k in layer0_jobs(b):
                    if kind == "PROJ":
                        k = (3, 0, 1, 2)[hf]
                    if kind == "M":
                        k = (1, 2, 3, 0)[hf]
                    out.append((hf, v_, kind, i, k))
                return out

            over_batches(sp, body, 2)
            load_residual(B - 1)
            for t in range(QT):
                store_x1(B - 1, t)
            for stored in m.x1_stored:
                sp.wait_ge(stored, 16 * B * QT // 2)

        @block.tensor
        def _(pe):
            pe.wait_ge(m.wsplit, 2)
            pe.wait_ge(m.zeros, 2 * HALF)
            pe.wait_ge(m.which_ok, HALF)
            pe.wait_ge(m.fold, 5)

            def job(kind, i, k):
                if kind == "XT":
                    pe.wait_ge(m.xn_ok, QT * (i + 1))
                    for t in range(QT):
                        mm = pe.transpose(misc[:, t * P:(t + 1) * P], xn[:, t, k * P:(k + 1) * P], ident[:, :])
                    mm.then_inc(m.xt_psum, 1)
                if kind == "PROJ":
                    hf = k
                    n = 0
                    for kc in range(KC):
                        for w, x in ((wqk_h, xt_h), (wqk_h, xt_l), (wqk_l, xt_h)):
                            mm = pe.matmul(misc[:, :], w[:, kc, hf, :], x[:, kc, :], start=(n == 0), stop=(n == 5))
                            n += 1
                    mm.then_inc(m.proj_psum, 1)
                if kind == "V":
                    if k == 0:
                        pe.wait_ge(m.xt_sum, i + 1)
                    for kc in range(KC):
                        mm = pe.matmul(misc[:, 0:WCAT], xt[:, kc, k * P:(k + 1) * P], wcat[:, kc, :],
                                       start=(kc == 0), stop=(kc == KC - 1))
                    mm.then_inc(m.v_psum, 1)
                if kind == "M":
                    pe.wait_ge(m.m_low, i + 1)
                    for c in range(QT):
                        mm = pe.matmul(misc[MROW:MROW + MROWS, c * P:(c + 1) * P],
                                       msplit[:, c, :, :].bitcast(F32).rearrange("p a h -> p (a h)"),
                                       ident[:, :], start=True, stop=True)
                    mm.then_inc(m.m_psum, 1)
                if kind == "TD":
                    pe.wait_ge(m.d_evac, i + 1)
                    for t in range(QT):
                        mm = pe.transpose(misc[:, t * P:(t + 1) * P], dt_[:, t * P:(t + 1) * P], ident[:, :])
                    mm.then_inc(m.td_psum, 1)
                if kind == "TA":
                    pe.wait_ge(m.a_evac, HALF * (i + 1))
                    for hf in range(HALF):
                        mm = pe.transpose(misc[:, hf * P:(hf + 1) * P], at[:, hf, k * P:(k + 1) * P], ident[:, :])
                    mm.then_inc(m.ta_psum, 1)
                if kind == "OT":
                    pe.wait_ge(m.o_ok, QT * (i + 1))
                    for t in range(QT):
                        mm = pe.transpose(misc[:, t * P:(t + 1) * P], o[:, t, k * P:(k + 1) * P], ident[:, :])
                    mm.then_inc(m.ot_psum, 1)
                if kind == "ZT":
                    pe.wait_ge(m.z_ok, i + 1)
                    for t in range(QT):
                        mm = pe.transpose(misc[:, t * P:(t + 1) * P], z[:, t, :, :].rearrange("p e r -> p (e r)"),
                                          ident[:, :])
                    mm.then_inc(m.zt_psum, 1)
                if kind == "WF":
                    for kc in range(KC):
                        pe.matmul(misc[:, 0:E], ot[:, kc, k * P:(k + 1) * P], wo[:, kc, :],
                                  start=(kc == 0), stop=(kc == KC - 1))
                    pe.matmul(misc[:, E:2 * E], zt[:, k * P:(k + 1) * P], routed[:, :],
                              start=True, stop=True).then_inc(m.wf_psum, 1)

            def score_max(n, w, slot, i):
                if w == 0:
                    pe.wait_ge(m.stacked, 128 * (i + 1))
                wait(pe, m.max_done, n - S_BACK[w] + 1)
                j, c = w // 4, w % 4
                pe.matmul(s_bank[S_BANK[w]][:, :], qst[slot][0:MROW, j, c * P:(c + 1) * P], kst[slot][0:MROW, j, :],
                          start=True, stop=True).then_inc(m.s_done, 1)

            def score_exp(g, w, slot, i):
                if w == 0:
                    pe.wait_ge(m.m_placed, 16 * (i + 1))
                wait(pe, m.exp_done, g - 1)
                c, j = w // 4, w % 4
                pe.matmul(t_bank[w % 2][:, :], kst[slot][0:MROW + MROWS, j, c * P:(c + 1) * P],
                          qst[slot][0:MROW + MROWS, j, :], start=True, stop=True).then_inc(m.t_done, 1)

            def value_step(b, hf, c):
                y = HALF * b + hf
                hg = hf // 2
                if c == 0:
                    wait(pe, m.a_evac, y)
                    if hf == 0:
                        pe.wait_ge(m.v_ok, b + 1)
                pe.wait_ge(m.exp_done, UNITS * y + 4 * c + 4)
                for h in range(HG):
                    mm = pe.matmul(a_bank[BLK * h:BLK * h + BLK, :],
                                   v[:, c, hg * P + h * DH0:hg * P + (h + 1) * DH0], probs[:, c, h, :],
                                   start=(c == 0), stop=(c == 3))
                mm.then_inc(m.a_done, 1)

            def denominators(b, d):
                hf, buf = D_PARTS[d]
                if d == 0:
                    wait(pe, m.d_evac, b)
                pe.wait_ge(m.sum_ok, SUMS * b + (3, 6, 9, 10, 11)[d])
                for h in range(HG):
                    mm = pe.matmul(d_bank[BLK * h:BLK * h + BLK, :], pick[:, hf, :], sums[:, buf, h, :],
                                   start=(d == 0), stop=(d == len(D_PARTS) - 1))
                mm.then_inc(m.d_done, 1)

            prev = None

            def side(kind, i, k):
                nonlocal prev
                if prev is not None:
                    wait(pe, *drained(*prev))
                job(kind, i, k)
                prev = (kind, i, 0 if kind in ("PROJ", "M") else k)

            for kind, i, k in FIRST_JOBS[:-1]:
                side(kind, i, i if kind == "PROJ" else k)
            for n in range(LEAD):
                score_max(n, n % UNITS, n // UNITS, n // UNITS)
            side(*FIRST_JOBS[-1])

            def body(b):
                nonlocal prev
                last = isinstance(b, int) and b >= B - 1
                if not isinstance(b, int):
                    _, kind, i, k = layer0_jobs(b - 1)[-1]
                    prev = (kind, i, k)
                jobs = layer0_jobs(b)
                for hf in range(HALF):
                    for w in range(UNITS):
                        g = HALF * UNITS * b + UNITS * hf + w
                        score_exp(g, w, hf, HALF * b + hf)
                        ahead = hf * UNITS + w + LEAD
                        if not (last and ahead >= HALF * UNITS):
                            score_max(g + LEAD, ahead % UNITS, ahead // UNITS % HALF, HALF * b + ahead // UNITS)
                        if w % 4 == 3:
                            step = 4 * hf + w // 4 - LAG
                            if step >= 0:
                                value_step(b, step // 4, step % 4)
                            elif not (isinstance(b, int) and b < 1):
                                value_step(b - 1, (step + 16) // 4, (step + 16) % 4)
                        if w == 10 and hf:
                            denominators(b, hf - 1)
                        if hf == 0 and w in (2, 6) and not (isinstance(b, int) and b < 1):
                            denominators(b - 1, 3 if w == 2 else 4)
                        for (jh, jw), kind, i, k in jobs:
                            if (jh, jw) == (hf, w):
                                side(kind, i, (3, 0, 1, 2)[hf] if kind == "PROJ" else k)

            over_batches(pe, body, 2)
            for step in range(16 - LAG, 16):
                value_step(B - 1, step // 4, step % 4)
            denominators(B - 1, 3)
            denominators(B - 1, 4)
            for kind, i, k in LAST_JOBS:
                side(kind, i, k)

        @block.scalar
        def _(act):
            act.wait_ge(m.w_load, 16 * LOADS)
            act.activation(wqk_h[:, :, :, :], wqk, ACT.Copy).then_inc(m.wsplit, 1)

            def exp_tile(b, hf, w):
                g = HALF * UNITS * b + UNITS * hf + w
                act.wait_ge(m.t_done, g + 1)
                c, j = w // 4, w % 4
                if j == 0:
                    wait(act, m.a_done, 4 * (HALF * b + hf - 1) + c + 1)
                    if hf:
                        wait(act, m.sum_ok, SUMS * b + 3 * (hf - 1) + max(c, 1))
                    else:
                        wait(act, m.sum_ok, SUMS * (b - 1) + 10 + c // 2)
                act.activation(probs[:, c, j, :], t_bank[w % 2][:, :], ACT.Exp, scale=SCALE0).then_inc(m.exp_done, 1)

            def side(kind, i, k):
                if kind == "XT":
                    act.wait_ge(m.xt_psum, KC * i + k + 1)
                    if k == 0:
                        wait(act, m.proj_psum, 4 * i)
                        wait(act, m.xt_sum, i)
                    act.activation(xt_h[:, k, :], misc[:, :], ACT.Copy).then_inc(m.xt_high, 1)
                if kind == "PROJ":
                    act.wait_ge(m.proj_psum, i + 1)
                    wait(act, m.parked, 32 * i)
                    act.activation(qk_h[:, :], misc[:, :], ACT.Copy).then_inc(m.qk_high, 1)
                if kind == "V":
                    act.wait_ge(m.v_psum, QT * i + k + 1)
                    wait(act, m.lc_ok, i)
                    act.activation(vnew[:, k, :], misc[:, 0:WCAT], ACT.Copy).then_inc(m.vnew_ok, 1)
                if kind == "M":
                    act.wait_ge(m.m_psum, i + 1)
                    wait(act, m.m_placed, 16 * i)
                    act.activation(mrow[MROW:MROW + MROWS, :], misc[MROW:MROW + MROWS, :], ACT.Copy).then_inc(m.m_evac, 1)
                if kind == "DEV":
                    act.wait_ge(m.d_done, len(D_PARTS) * (i + 1))
                    wait(act, m.td_psum, i)
                    act.activation(dt_[:, :], d_bank[:, :], ACT.Copy).then_inc(m.d_evac, 1)
                if kind == "SQ":
                    act.wait_ge(m.o_ok, QT * i + k + 1)
                    if k == 0:
                        wait(act, m.ms_ok, i)
                        wait(act, m.wf_gate, QT * i)
                    act.activation(th[:, k, :], o[:, k, :], ACT.Square, accum_out=ss[:, k:k + 1]).then_inc(m.ss_ok, 1)
                if kind == "OT":
                    act.wait_ge(m.ot_psum, KC * i + k + 1)
                    wait(act, m.wf_psum, QT * i)
                    act.activation(ot[:, k, :], misc[:, :], ACT.Copy).then_inc(m.ot_evac, 1)
                if kind == "ZT":
                    act.wait_ge(m.zt_psum, i + 1)
                    act.activation(zt[:, :], misc[:, :], ACT.Copy).then_inc(m.zt_evac, 1)
                if kind == "WF":
                    act.wait_ge(m.wf_psum, QT * i + k + 1)
                    if k == 0:
                        act.wait_ge(m.ss_ok, QT * (i + 1))
                    act.activation(th[:, k, :], misc[:, E:2 * E], ACT.Tanh).then_inc(m.tanh_ok, 1)
                if kind == "GEXP":
                    act.wait_ge(m.gate_d, i + 1)
                    act.activation(gs[:, 5, :], gs[:, 4, :], ACT.Exp).then_inc(m.gate_e, 1)

            for kind, i, k in FIRST_JOBS:
                side(kind, i, k)

            def body(b):
                first = isinstance(b, int) and b < 1
                jobs = layer0_jobs(b)
                for hf in range(HALF):
                    for w in range(UNITS):
                        exp_tile(b, hf, w)
                        if w == 8:
                            if hf:
                                act.wait_ge(m.a_done, 4 * (HALF * b + hf))
                                if hf == 1:
                                    wait(act, m.ta_psum, QT * b)
                                act.activation(at[:, hf - 1, :], a_bank[:, :], ACT.Copy).then_inc(m.a_evac, 1)
                            elif not first:
                                act.wait_ge(m.a_done, 16 * b)
                                act.activation(at[:, 3, :], a_bank[:, :], ACT.Copy).then_inc(m.a_evac, 1)
                        if (hf, w) == (0, 9) and not first:
                            side("DEV", b - 1, 0)
                        if hf == 2 and w == 2:
                            side("GEXP", b, 0)
                        for (jh, jw), kind, i, k in jobs:
                            if (jh, jw) == (hf, w):
                                side(kind, i, k)
                        if not first and hf == 1 and w in (3, 5, 7, 9):
                            side("SQ", b - 1, (w - 3) // 2)

            over_batches(act, body, 2)
            act.wait_ge(m.a_done, 16 * B)
            act.activation(at[:, 3, :], a_bank[:, :], ACT.Copy).then_inc(m.a_evac, 1)
            side("DEV", B - 1, 0)
            for kind, i, k in LAST_JOBS:
                side(kind, i, k)
                if kind == "TA":
                    side("SQ", i, k)

        @block.vector
        def _(dve):
            for i in range(HALF):
                dve.memset(qst[i][STACK:MROW, :, :].bitcast(F32), 0.0).then_inc(m.zeros, 1)
                dve.memset(kst[i][STACK:MROW, :, :].bitcast(F32), 0.0).then_inc(m.zeros, 1)
            dve.memset(mhalf[:, :], -0.5).then_inc(m.mhalf_ok, 1)

            def norm_stats(b, tiles):
                dve.wait_ge(m.x_load, 16 * (b + 1))
                for t in tiles:
                    dve.bn_stats(stat[:, t, :], xb[:, t, :]).then_inc(m.stats, 1)

            def norm_ends(b):
                dve.wait_ge(m.stats, QT * (b + 1))
                wait(dve, m.veps_ok, b)
                stand_alone(dve, m.dve_passed)
                for t in range(QT):
                    dve.bn_aggr(mv[:, t, :], stat[:, t, :]).then_inc(m.aggr, 1)

            def normalise(b, tiles):
                dve.wait_ge(m.rstd_ok, b + 1)
                wait(dve, m.xt_psum, KC * b)
                for t in tiles:
                    ins = dve.tensor_scalar(xn[:, t, :], xb[:, t, :], mv[:, t, 0:1], rstd[:, t:t + 1],
                                            ALU.subtract, ALU.mult)
                    ins.then_inc(m.xn_ok, 1)

            norm_stats(0, range(QT))
            norm_ends(0)
            dve.wait_ge(m.w_load, 16 * LOADS)
            dve.wait_ge(m.wsplit, 1)
            dve.tensor_tensor(wqk_l[:, :, :, :], wqk, wqk_h[:, :, :, :].bitcast(F32),
                              ALU.subtract).then_inc(m.wsplit, 1)
            for i in range(HALF):
                dve.tensor_copy(kst[i][MROW:MROW + MROWS, :, :], which[MROW:MROW + MROWS]).then_inc(m.which_ok, 1)
            normalise(0, range(QT))
            dve.tensor_scalar(one_dw[:, :], dw[:, :], -1.0, 1.0, ALU.mult, ALU.add).then_inc(m.fold, 1)
            dve.tensor_scalar(neg_dw[:, :], dw[:, :], -1.0, None, ALU.mult).then_inc(m.fold, 1)
            dve.wait_ge(m.fold, 2)
            for kc in range(KC):
                dve.tensor_scalar(wo[:, kc, :], wo[:, kc, :], normw[:, kc:kc + 1], one_dw[:, 0:1], ALU.mult,
                                  ALU.mult).then_inc(m.fold, 1)
            dve.tensor_scalar(bo[:, :], bo[:, :], one_dw[:, 0:1], None, ALU.mult).then_inc(m.fold, 1)

            def max_tile(n, w, i_par):
                dve.wait_ge(m.s_done, n + 1)
                j, c = w // 4, w % 4
                dve.tensor_reduce(negmax[:, i_par, c, j:j + 1], s_bank[S_BANK[w]][:, :], X, ALU.max,
                                  negate=True).then_inc(m.max_done, 1)

            def side(kind, i, k):
                if kind == "XT":
                    dve.wait_ge(m.xt_high, KC * i + k + 1)
                    dve.tensor_tensor(xt_l[:, k, :], misc[:, :], xt_h[:, k, :].bitcast(F32),
                                      ALU.subtract).then_inc(m.xt_low, 1)
                if kind == "PROJ":
                    dve.wait_ge(m.qk_high, i + 1)
                    wait(dve, m.parked, 32 * i)
                    dve.tensor_tensor(qk_l[:, :], misc[:, :], qk_h[:, :].bitcast(F32), ALU.subtract).then_inc(m.qk_low, 1)
                if kind == "MS":
                    dve.wait_ge(m.max_done, UNITS * (i + 1))
                    wait(dve, m.m_psum, i)
                    dve.tensor_copy(msplit[:, :, 0, :], negmax[:, k, :, :]).then_inc(m.m_high, 1)
                    dve.wait_ge(m.m_high, i + 1)
                    dve.tensor_tensor(msplit[:, :, 1, :], negmax[:, k, :, :], msplit[:, :, 0, :].bitcast(F32),
                                      ALU.subtract).then_inc(m.m_low, 1)
                if kind == "VCOPY":
                    dve.wait_ge(m.vnew_ok, QT * (i + 1))
                    wait(dve, m.a_done, 16 * i)
                    dve.tensor_copy(v[:, :, :], vnew[:, :, 0:E]).then_inc(m.v_ok, 1)
                    dve.tensor_copy(lc[:, :, :], vnew[:, :, E:WCAT]).then_inc(m.lc_ok, 1)
                if kind == "TD":
                    dve.wait_ge(m.td_psum, i + 1)
                    dve.reciprocal(rec[:, :, :, :].rearrange("p t s h -> p t h s"),
                                   misc[:, :].rearrange("p (t h s) -> p t h s", t=QT, h=HG)[:, :, :, 0:HALF]
                                   ).then_inc(m.recip_ok, 1)
                    dve.wait_ge(m.recip_ok, i + 1)
                    for hg in range(2):
                        one = rec[:, :, 2 * hg + 1, :]
                        ins = dve.tensor_scalar(one, one, neg_dw[:, 0:1], None, ALU.mult)
                    ins.then_inc(m.rec_ok, 1)
                if kind == "TA":
                    dve.wait_ge(m.rec_ok, i + 1)
                    dve.wait_ge(m.ta_psum, QT * i + k + 1)
                    wait(dve, m.o_ok, QT * i + k)
                    if k == 0:
                        wait(dve, m.ot_psum, KC * i)
                        wait(dve, m.ss_ok, QT * i)
                    dve.tensor_tensor(an[:, :, :, :], misc[:, :].rearrange("p (s h e) -> p s h e", s=HALF, h=HG),
                                      rec[:, k, :, :].unsqueeze(3).to_broadcast([P, HALF, HG, DH0]),
                                      ALU.mult).then_inc(m.an_ok, 1)
                    dve.wait_ge(m.an_ok, QT * i + k + 1)
                    maps = an[:, :, :, :].rearrange("p (g i) h e -> p g i (h e)", g=2)
                    dve.tensor_tensor(o[:, k, :].rearrange("p (g n) -> p g n", g=2), maps[:, :, 0, :],
                                      maps[:, :, 1, :], ALU.add).then_inc(m.o_ok, 1)
                if kind == "WF":
                    dve.wait_ge(m.tanh_ok, QT * i + k + 1)
                    dve.wait_ge(m.rms_ok, i + 1)
                    wait(dve, m.x1_ok, QT * (i - 1) + k + 1)
                    dve.scalar_tensor_tensor(s_[:, k, :], misc[:, 0:E], rms[:, k:k + 1], bo[:, :],
                                             op0=ALU.mult, op1=ALU.add).then_inc(m.s_ok, 1)
                    dve.scalar_tensor_tensor(g_[:, k, :], th[:, k, :], 1.0, misc[:, E:2 * E],
                                             op0=ALU.add, op1=ALU.mult).then_inc(m.wf_gate, 1)

            GATES = 17

            def wide(k):
                return gs[:, k, :].unsqueeze(2).to_broadcast([P, QT, NE])

            def gate(b):
                lg = lc[:, :, 0:NE]
                w8 = rank8[:, :].unsqueeze(1).to_broadcast([P, QT, NE])
                n = GATES * b
                dve.wait_ge(m.lc_ok, b + 1)
                wait(dve, m.z_ok, b)
                for src, top, num, hot in ((lg, 0, 1, 1), (gt[:, 2, :, :], 2, 3, 3)):
                    dve.tensor_reduce(gs[:, top, :], src, X, ALU.max).then_inc(m.gate, 1)
                    dve.wait_ge(m.gate, n + 1)
                    dve.tensor_tensor(gt[:, 0, :, :], src, wide(top), ALU.is_equal).then_inc(m.gate, 1)
                    dve.wait_ge(m.gate, n + 2)
                    dve.tensor_tensor(gt[:, 0, :, :], gt[:, 0, :, :], w8, ALU.mult).then_inc(m.gate, 1)
                    dve.wait_ge(m.gate, n + 3)
                    dve.tensor_reduce(gs[:, num, :], gt[:, 0, :, :], X, ALU.max).then_inc(m.gate, 1)
                    dve.wait_ge(m.gate, n + 4)
                    dve.tensor_tensor(gt[:, hot, :, :], gt[:, 0, :, :], wide(num), ALU.is_equal).then_inc(m.gate, 1)
                    dve.wait_ge(m.gate, n + 5)
                    n = n + 5
                    if top == 0:
                        dve.scalar_tensor_tensor(gt[:, 2, :, :], gt[:, 1, :, :], -3e38, lg,
                                                 op0=ALU.mult, op1=ALU.add).then_inc(m.gate, 1)
                        dve.wait_ge(m.gate, n + 1)
                        n = n + 1
                dve.tensor_tensor(gs[:, 4, :], gs[:, 2, :], gs[:, 0, :], ALU.subtract).then_inc(m.gate_d, 1)

            def gate_end(b):
                n = GATES * b + 11
                dve.wait_ge(m.gate_e, b + 1)
                dve.tensor_scalar(gs[:, 6, :], gs[:, 5, :], 1.0, None, ALU.add).then_inc(m.gate, 1)
                dve.wait_ge(m.gate, n + 1)
                dve.reciprocal(gs[:, 7, :], gs[:, 6, :]).then_inc(m.gate, 1)
                dve.wait_ge(m.gate, n + 2)
                dve.tensor_tensor(gs[:, 6, :], gs[:, 5, :], gs[:, 7, :], ALU.mult).then_inc(m.gate, 1)
                dve.tensor_tensor(gt[:, 4, :, :], gt[:, 1, :, :], wide(7), ALU.mult).then_inc(m.gate, 1)
                dve.wait_ge(m.gate, n + 4)
                dve.tensor_tensor(gt[:, 5, :, :], gt[:, 3, :, :], wide(6), ALU.mult).then_inc(m.gate, 1)
                dve.wait_ge(m.gate, n + 5)
                dve.tensor_tensor(gt[:, 6, :, :], gt[:, 4, :, :], gt[:, 5, :, :], ALU.add).then_inc(m.gate, 1)

            def gated(b):
                dve.wait_ge(m.gate, GATES * (b + 1))
                wait(dve, m.zt_psum, b)
                for t in range(QT):
                    ins = dve.tensor_tensor(z[:, t, :, :], gt[:, 6, t, :].unsqueeze(2).to_broadcast([P, NE, R]),
                                            lc[:, t, NE:NE + R].unsqueeze(1).to_broadcast([P, NE, R]), ALU.mult)
                ins.then_inc(m.z_ok, 1)

            for kind, i, k in FIRST_JOBS[:-1]:
                side(kind, i, k)
            for n in range(LEAD):
                max_tile(n, n % UNITS, n // UNITS % 2)
                if n == UNITS - 1:
                    side("MS", 0, 0)

            def body(b):
                first = isinstance(b, int) and b < 1
                last = isinstance(b, int) and b >= B - 1
                jobs = layer0_jobs(b)
                for hf in range(HALF):
                    for w in range(UNITS):
                        ahead = hf * UNITS + w + LEAD
                        if not (last and ahead >= HALF * UNITS):
                            max_tile(HALF * UNITS * b + ahead, ahead % UNITS, ahead // UNITS % 2)
                        if w == 7 and not (last and hf == 3):
                            side("MS", HALF * b + hf + 1, (hf + 1) % 2)
                        if hf == 0 and w in (0, 2) and not last:
                            norm_stats(b + 1, (w, w + 1))
                        if (hf, w) == (0, 3) and not last:
                            norm_ends(b + 1)
                        if hf == 0 and w in (6, 9) and not last:
                            normalise(b + 1, (0, 1) if w == 6 else (2, 3))
                        if (hf, w) == (0, 8):
                            side("VCOPY", b, 0)
                        if (hf, w) == (1, 14):
                            gate(b)
                        if (hf, w) == (3, 8):
                            gate_end(b)
                        if (hf, w) == (3, 13):
                            gated(b)
                        for (jh, jw), kind, i, k in jobs:
                            if (jh, jw) == (hf, w):
                                side(kind, i, k)

            over_batches(dve, body, 2)
            for kind, i, k in LAST_JOBS:
                side(kind, i, k)

        @block.gpsimd
        def _(pool):
            def rstd_of(b):
                pool.wait_ge(m.aggr, QT * (b + 1))
                wait(pool, m.xn_ok, QT * b)
                stand_alone(pool, m.pool_passed)
                pool.tensor_scalar(veps[:, :], mv[:, :, 1], LN_EPS, None, ALU.add).then_inc(m.veps_ok, 1)
                pool.wait_ge(m.veps_ok, b + 1)
                pool.tensor_tensor(rstd[:, :], veps[:, :], mhalf[:, :], ALU.pow).then_inc(m.rstd_ok, 1)

            def add_chunk(b, hf, c):
                pool.wait_ge(m.exp_done, UNITS * (HALF * b + hf) + HG * (c + 1))
                if c == 1:
                    wait(pool, m.d_done, len(D_PARTS) * b + max(hf - 1, 0))
                else:
                    pool.wait_ge(m.sum_ok, SUMS * b + 3 * hf + c - 1)
                before = probs[:, 0, :, :] if c == 1 else sums[:, hf % 2, :, :]
                pool.tensor_tensor(sums[:, hf % 2, :, :], before, probs[:, c, :, :], ALU.add).then_inc(m.sum_ok, 1)

            def add_pair(b, c2):
                pool.wait_ge(m.exp_done, UNITS * (HALF * b + 3) + 8 * (c2 + 1))
                pool.wait_ge(m.d_done, len(D_PARTS) * b + 2 + c2)
                pool.tensor_tensor(sums[:, 1 - c2, :, :], probs[:, 2 * c2, :, :], probs[:, 2 * c2 + 1, :, :],
                                   ALU.add).then_inc(m.sum_ok, 1)

            def add_parts(b):
                pool.wait_ge(m.xt_low, KC * (b + 1))
                wait(pool, m.v_psum, QT * b)
                pool.tensor_tensor(xt[:, :, :], xt_h[:, :, :].bitcast(F32), xt_l[:, :, :].bitcast(F32),
                                   ALU.add).then_inc(m.xt_sum, 1)

            def rms_of(b):
                pool.wait_ge(m.ss_ok, QT * (b + 1))
                wait(pool, m.wf_gate, QT * b)
                stand_alone(pool, m.pool_passed)
                pool.tensor_scalar(ms[:, :], ss[:, :], 1.0 / E, EPS32, ALU.mult, ALU.add).then_inc(m.ms_ok, 1)
                pool.wait_ge(m.ms_ok, b + 1)
                pool.tensor_tensor(rms[:, :], ms[:, :], mhalf[:, :], ALU.pow).then_inc(m.rms_ok, 1)

            def residual(b, k):
                pool.wait_ge(m.wf_gate, QT * b + k + 1)
                pool.tensor_tensor(g_[:, k, :], s_[:, k, :], g_[:, k, :], ALU.mult).then_inc(m.prod_ok, 1)
                pool.wait_ge(m.prod_ok, QT * b + k + 1)
                if k == 0:
                    pool.wait_ge(m.xr_load, 16 * (b + 1))
                wait(pool, m.x1_stored[k % 2], 16 * (QT // 2 * b + k // 2))
                pool.tensor_tensor(x1o[:, k % 2, :], xr[:, k, :], g_[:, k, :], ALU.add).then_inc(m.x1_ok, 1)

            pool.wait_ge(m.mhalf_ok, 1)
            pool.wait_ge(m.x_load, 16)
            rstd_of(0)
            add_parts(0)

            def body(b):
                first = isinstance(b, int) and b < 1
                last = isinstance(b, int) and b >= B - 1
                if not first:
                    add_pair(b - 1, 1)
                if not last:
                    rstd_of(b + 1)
                for hf in range(HALF - 1):
                    for c in range(1, 4):
                        add_chunk(b, hf, c)
                        if (hf, c) == (1, 1) and not last:
                            add_parts(b + 1)
                        if (hf, c) == (1, 2) and not first:
                            rms_of(b - 1)
                        if (hf, c) == (2, 2) and not first:
                            residual(b - 1, 0)
                        if (hf, c) == (2, 3) and not first:
                            for k in range(1, QT):
                                residual(b - 1, k)
                add_pair(b, 0)

            over_batches(pool, body, 2)
            add_pair(B - 1, 1)
            rms_of(B - 1)
            for k in range(QT):
                residual(B - 1, k)


def layer1_steps():
    steps = [("V", k) for k in range(2 * TT)] + [("Q", 0), ("K", 0)]
    for hp in range(HP):
        if hp + 1 < HP:
            steps += [("Q", hp + 1), ("K", hp + 1)]
        steps += [("S", hp)]
        if hp >= 2:
            steps += [("AV", hp - 2)]
    return steps + [("F", 0), ("F", 1), ("AV", HP - 2), ("F", 2), ("F", 3), ("AV", HP - 1)]


W_ORDER = (1, 2, 0, 3)
W_DONE = {t: n + 1 for n, t in enumerate(W_ORDER)}


TWO_PI = (6.28125, 0.0019350051879882812, 3.019916050561733e-07)
ROUND = 1.5 * 2.0 ** 23
PI_BELOW = 3.1415925


def layer1(nc, io, x1_dram, out):
    with ExitStack() as ctx:
        def sb(name, shape, dt=F32):
            return ctx.enter_context(nc.sbuf_tensor(name, shape, dt))

        def banks(name, n=1):
            return ctx.enter_context(nc.psum_tensor(name, [P, n, 512], F32))

        def sem(name):
            return ctx.enter_context(nc.semaphore(name))

        W3 = 3 * H1 * D1
        win_h, win_l = sb("win_h", [P, KC, W3], F32R), sb("win_l", [P, KC, W3], F32R)
        cs_h, cs_l = sb("cs_h", [P, KC, 2 * E], F32R), sb("cs_l", [P, KC, 2 * E], F32R)
        wout = sb("wout", [P, HP, E])
        gk = sb("gk", [P, KC, H1, NREL])
        ud = sb("ud", [P, E])
        beta = sb("beta", [P, H1, NREL])
        bqkv, bout = sb("bqkv", [P, 3 * HP]), sb("bout", [P, E])
        ident = sb("ident1", [P, P])
        apart = sb("apart", [P, BLK])
        own = sb("own", [P, NREL])
        kdx = sb("kdx", [P, 2, NREL])
        mhalf, halfpi = sb("mhalf1", [P, TT]), sb("halfpi", [P, 1])
        work = sb("work", [P, KC * W3])
        v = work[:, 0:TT * H1 * D1].rearrange("p (t n) -> p t n", t=TT)
        rm = work[:, TT * H1 * D1:].rearrange("p (h t k) -> p h t k", t=TT, h=H1)
        xb, xn, xr = sb("xb1", [P, TT, E]), sb("xn1", [P, TT, E]), sb("xr1", [P, TT, E])
        stat, mv = sb("stat1", [P, TT, 6]), sb("mv1", [P, TT, 2])
        veps, rstd = sb("veps1", [P, TT]), sb("rstd1", [P, TT])
        xt = sb("xt1", [P, KC, TOK])
        xt_h, xt_l = sb("xt_h1", [P, KC, TOK], F32R), sb("xt_l1", [P, KC, TOK], F32R)
        qt, kt = sb("qt", [P, 2, TOK]), sb("kt", [P, 2, TOK])
        sc, ex = sb("sc", [P, 2, 2, TT, BLK]), sb("ex", [P, 2, 2, TT, BLK])
        mx, sm, rc = sb("mx", [P, 2, 2, TT]), sb("sm", [P, 2, 2, TT]), sb("rc", [P, 2, 2, TT])
        ec = sb("ec", [P, 2, 2, TT, NREL])
        pt = [sb(f"pt{i}", [P, 2, TT, P]) for i in range(2)]
        ot = sb("ot1", [P, HP, TOK])
        r15, rt = sb("r15", [P, H1, TT, 2 * NREL - 1]), sb("rt", [P, H1, TT, NREL])
        p15, pc = sb("p15", [P, H1, TT, 2 * NREL - 1]), sb("pc", [P, H1, TT, NREL])
        pd = sb("pd", [P, TT, H1, NREL])
        pdt = sb("pdt", [P, TOK])
        sq = sb("sq", [P, 2, 2 * E])
        q2, th = sb("q2", [P, TT, E]), sb("th1", [P, TT, E])
        so = sb("so", [P, 2, E])
        wqn = ot[:, 0:4, :].rearrange("p a b -> p (a b)").rearrange("p (h c) -> p h c", h=HP)
        vdx = ot[:, 4:6, :].rearrange("p a b -> p (a b)").rearrange("p (h c) -> p h c", h=HP)
        kdb = ot[:, 6, 0:HP * 2 * NREL].rearrange("p (h c) -> p h c", h=HP)
        ones = ot[:, 7, 0:P]
        ang = [t[:, 0:KC, :] for t in (xb, xn)]
        noise = [t[:, 0:KC, :] for t in (q2, th)]
        turns = [xb[:, KC:2 * KC, :], xn[:, KC:2 * KC, :]]
        cs = xr[:, :, :].rearrange("p (k a) n -> p k (a n)", k=KC)

        pr = banks("pr", 2)
        s_ps = banks("s_ps", 2)
        o_ps = banks("o_ps", 2)
        misc = banks("misc1")[:, 0, :]
        fin = banks("fin")[:, 0, :]

        m = Semaphores()
        m.w_load = sem("w_load1")
        m.w_high = sem("w_high1")
        m.w_low = sem("w_low1")
        m.b_load = sem("b_load1")
        m.theta_load = sem("theta_load1")
        m.trig = sem("trig1")
        m.sin_ok = sem("sin_ok1")
        m.cs_high = sem("cs_high1")
        m.cs_low = sem("cs_low1")
        m.zero_pt = sem("zero_pt1")
        m.consts_ok = sem("consts_ok1")
        m.kdb_ok = sem("kdb_ok1")
        m.g_psum = sem("g_psum1")
        m.g_ok = sem("g_ok1")
        m.x_load = sem("x_load1")
        m.stats = sem("stats1")
        m.aggr = sem("aggr1")
        m.veps_ok = sem("veps_ok1")
        m.rstd_ok = sem("rstd_ok1")
        m.xn_ok = sem("xn_ok1")
        m.xt_psum = sem("xt_psum1")
        m.xt_high = sem("xt_high1")
        m.xt_low = sem("xt_low1")
        m.r_psum = sem("r_psum1")
        m.r_evac = sem("r_evac1")
        m.r_flip = sem("r_flip1")
        m.r_sum = sem("r_sum1")
        m.rm_ok = sem("rm_ok1")
        m.v_psum = sem("v_psum1")
        m.v_ok = sem("v_ok1")
        m.qk_psum = sem("qk_psum1")
        m.qk_ok = sem("qk_ok1")
        m.s_psum = sem("s_psum1")
        m.sc_ok = sem("sc_ok1")
        m.mx_ok = sem("mx_ok1")
        m.sub_ok = sem("sub_ok1")
        m.ex_ok = sem("ex_ok1")
        m.ec_ok = sem("ec_ok1")
        m.sm_ok = sem("sm_ok1")
        m.rc_ok = sem("rc_ok1")
        m.pc_ok = sem("pc_ok1")
        m.p_ok = sem("p_ok1")
        m.pt_ok = sem("pt_ok1")
        m.o_psum = sem("o_psum1")
        m.ot_ok = sem("ot_ok1")
        m.f_psum = sem("f_psum1")
        m.sq_ok = sem("sq_ok1")
        m.q2_ok = sem("q2_ok1")
        m.sqrt_ok = sem("sqrt_ok1")
        m.tanh_ok = sem("tanh_ok1")
        m.gate_ok = sem("gate_ok1")
        m.p15_zero = sem("p15_zero1")
        m.p15_sum = sem("p15_sum1")
        m.pd_ok = sem("pd_ok1")
        m.pd_psum = sem("pd_psum1")
        m.pdt_ok = sem("pdt_ok1")
        m.w_psum = sem("w_psum1")
        m.so_ok = sem("so_ok1")
        m.sg_ok = sem("sg_ok1")
        m.xr_load = sem("xr_load1")
        m.x2_ok = sem("x2_ok1")
        m.stored_even = sem("stored_even1")
        m.stored_odd = sem("stored_odd1")
        m.sp_passed = sem("sp_passed1")
        m.dve_passed = sem("dve_passed1")
        m.pool_passed = sem("pool_passed1")
        m.pe_passed = sem("pe_passed1")
        m.stored = (m.stored_even, m.stored_odd)

        def drained(kind, i, k):
            return {"V": (m.v_ok, 2 * TT * i + k + 1), "Q": (m.qk_ok, 2 * HP * i + 2 * k + 1),
                    "K": (m.qk_ok, 2 * HP * i + 2 * k + 2), "F": (m.sq_ok, TT * i + k + 1),
                    "W": (m.so_ok, TT * i + W_DONE.get(k, 0)), "R": (m.r_evac, i + 1), "XT": (m.xt_low, KC * i + k + 1),
                    "PD": (m.pdt_ok, i + 1)}[kind]

        steps = layer1_steps()
        through_pr = [x for x in steps if x[0] in "VQKF"] + [("W", 1), ("W", 2)]
        assert len(through_pr) % 2 == 0
        BLOADS, TLOADS = 10, 4

        block = ctx.enter_context(nc.Block())

        @block.sync
        def _(sp):
            sp.dma_start(work[:, :].rearrange("p (k n) -> p k n", k=KC),
                         io["win"].rearrange("(k p) n -> p k n", p=P)).then_inc(m.w_load, 16)
            for dst, name in ((ang[0], "theta"), (ang[1], "phi"), (noise[0], "theta_noise"), (noise[1], "phi_noise")):
                sp.dma_start(dst, io[name].rearrange("(k p) n -> p k n", p=P)).then_inc(m.theta_load, 16)
            for dst, src in (
                    (wqn, io["wqn"].rearrange("(h p) c -> p h c", p=P)), (vdx, io["vdx"]), (kdx[:, :, :], io["kdx"]),
                    (wout[:, :, :], io["wout"].rearrange("(h p) c -> p h c", p=P)), (bqkv[:, :], io["bqkv"]),
                    (bout[:, :], io["bout"].partition_broadcast(P)),
                    (ident[:, :], io["ident"]), (apart[:, :], io["apart"]), (own[:, :], io["own"]),
                    (ones, io["ones"])):
                sp.dma_start(dst, src).then_inc(m.b_load, 16)

            def rows(i):
                return x1_dram.rearrange("n s c -> (n s) c").rearrange("(i t p) c -> i p t c", t=TT, p=P)[i]

            def load_x(i):
                wait(sp, m.xn_ok, i)
                stand_alone(sp, m.sp_passed)
                sp.dma_start(xb[:, :, :], rows(i)).then_inc(m.x_load, 16)

            sp.wait_ge(m.sin_ok, 2)
            load_x(0)
            sp.wait_ge(m.cs_low, 1)

            def body(i):
                wait(sp, m.x2_ok, TT * i)
                stand_alone(sp, m.sp_passed)
                sp.dma_start(xr[:, :, :], rows(i)).then_inc(m.xr_load, 16)
                if not (isinstance(i, int) and i >= NT1 - 1):
                    load_x(i + 1)
                o_rows = out.rearrange("n s c -> (n s) c").rearrange("(i t p) c -> i t p c", t=TT, p=P)
                for t in range(TT):
                    sp.wait_ge(m.x2_ok, TT * i + t + 1)
                    stand_alone(sp, m.sp_passed)
                    sp.dma_start(o_rows[i, W_ORDER[t]], so[:, t % 2, :]).then_inc(m.stored[t % 2], 16)

            over_batches(sp, body)
            for stored in m.stored:
                sp.wait_ge(stored, 16 * NT1 * TT // 2)

        @block.tensor
        def _(pe):
            pe.wait_ge(m.b_load, 16 * BLOADS)
            for hp in range(HP):
                for kc in range(KC):
                    pe.matmul(misc[:, kc * P + 2 * NREL * hp:kc * P + 2 * NREL * (hp + 1)],
                              wqn[:, hp, kc * P:(kc + 1) * P], kdx[:, :, :].rearrange("p a b -> p (a b)"),
                              start=True, stop=True)
            for hp in range(HP):
                mm = pe.matmul(fin[:, 0:E], vdx[:, hp, :], wout[:, hp, :], start=(hp == 0), stop=(hp == HP - 1))
            pe.wait_ge(m.kdb_ok, HP)
            for hp in range(HP):
                mm = pe.matmul(o_ps[:, 0, 2 * NREL * hp:2 * NREL * (hp + 1)], ones, kdb[:, hp, :],
                               start=True, stop=True)
            mm.then_inc(m.g_psum, 1)
            pe.wait_ge(m.g_ok, 3)
            pe.wait_ge(m.w_low, 1)
            pe.wait_ge(m.cs_low, 1)
            pe.wait_ge(m.zero_pt, 2)

            prev_misc = [None]

            def misc_free():
                if prev_misc[0] is not None:
                    wait(pe, *drained(*prev_misc[0]))

            def three(dst, w_h, w_l, x_h, x_l, inc):
                n = 0
                for kc in range(KC):
                    for a, b in ((w_h, x_h), (w_h, x_l), (w_l, x_h)):
                        mm = pe.matmul(dst, a(kc), b(kc), start=(n == 0), stop=(n == 3 * KC - 1))
                        n += 1
                mm.then_inc(inc, 1)

            def transposes(i, kc):
                pe.wait_ge(m.xn_ok, i + 1)
                misc_free()
                for t in range(TT):
                    mm = pe.transpose(misc[:, t * P:(t + 1) * P], xn[:, t, kc * P:(kc + 1) * P], ident[:, :])
                mm.then_inc(m.xt_psum, 1)
                prev_misc[0] = ("XT", i, kc)

            def free_pr(i, kind, k):
                n = through_pr.index((kind, k))
                if n >= 2:
                    wait(pe, *drained(through_pr[n - 2][0], i, through_pr[n - 2][1]))
                elif not (isinstance(i, int) and i < 1):
                    wait(pe, *drained(through_pr[n - 2][0], i - 1, through_pr[n - 2][1]))
                return pr[:, n % 2, :]

            for kc in range(KC):
                transposes(0, kc)

            def body(i):
                last = isinstance(i, int) and i >= NT1 - 1
                if not isinstance(i, int):
                    prev_misc[0] = ("PD", i - 1, 0)
                misc_free()
                pe.wait_ge(m.xt_low, KC * (i + 1))
                for t in range(TT):
                    for kc in range(KC):
                        mm = pe.matmul(misc[:, t * P:(t + 1) * P], xt[:, kc, t * P:(t + 1) * P],
                                       gk[:, kc, :, :].rearrange("p h r -> p (h r)"), start=(kc == 0), stop=(kc == KC - 1))
                mm.then_inc(m.r_psum, 1)
                prev_misc[0] = ("R", i, 0)

                for kind, k in steps:
                    if kind == "V":
                        t, half = k // 2, k % 2
                        c = 2 * H1 * D1 + 512 * half
                        three(free_pr(i, kind, k),
                              lambda kc: xt_h[:, kc, t * P:(t + 1) * P], lambda kc: xt_l[:, kc, t * P:(t + 1) * P],
                              lambda kc: win_h[:, kc, c:c + 512], lambda kc: win_l[:, kc, c:c + 512], m.v_psum)
                    if kind in ("Q", "K"):
                        c = H1 * D1 * (kind == "K") + P * k
                        three(free_pr(i, kind, k),
                              lambda kc: win_h[:, kc, c:c + P], lambda kc: win_l[:, kc, c:c + P],
                              lambda kc: xt_h[:, kc, :], lambda kc: xt_l[:, kc, :], m.qk_psum)
                    if kind == "F":
                        three(free_pr(i, kind, k),
                              lambda kc: xt_h[:, kc, k * P:(k + 1) * P], lambda kc: xt_l[:, kc, k * P:(k + 1) * P],
                              lambda kc: cs_h[:, kc, :], lambda kc: cs_l[:, kc, :], m.f_psum)
                    if kind == "S":
                        pe.wait_ge(m.qk_ok, 2 * HP * i + 2 * k + 2)
                        wait(pe, m.sc_ok, HP * i + k)
                        stand_alone(pe, m.pe_passed)
                        for blk in range(NBLK):
                            q, t = blk % 4, blk // 4
                            for h in range(2):
                                mm = pe.matmul(s_ps[BLK * q:BLK * (q + 1), h, BLK * t:BLK * (t + 1)],
                                               qt[D1 * h:D1 * (h + 1), k % 2, BLK * blk:BLK * (blk + 1)],
                                               kt[D1 * h:D1 * (h + 1), k % 2, BLK * blk:BLK * (blk + 1)],
                                               start=True, stop=True)
                        mm.then_inc(m.s_psum, 1)
                    if kind == "AV":
                        pe.wait_ge(m.pt_ok, 4 * (HP * i + k + 1))
                        if k == 0:
                            pe.wait_ge(m.v_ok, 2 * TT * (i + 1))
                            wait(pe, m.so_ok, TT * i)
                        wait(pe, m.ot_ok, HP * i + k - 1)
                        for t in range(TT):
                            for h in range(2):
                                c = D1 * (2 * k + h)
                                mm = pe.matmul(o_ps[D1 * h:D1 * (h + 1), k % 2, P * t:P * (t + 1)],
                                               v[:, t, c:c + D1], pt[k % 2][:, h, t, :], start=True, stop=True)
                        mm.then_inc(m.o_psum, 1)

                def w_bank(t):
                    return (fin, pr[:, through_pr.index(("W", 1)) % 2, :], pr[:, through_pr.index(("W", 2)) % 2, :],
                            o_ps[:, 0, :])[t]

                for t in range(TT):
                    if t < KC and not last:
                        transposes(i + 1, t)
                    if t == 3:
                        pe.wait_ge(m.pd_ok, 2 * (i + 1))
                        misc_free()
                        for u in range(TT):
                            mm = pe.transpose(misc[:, u * P:(u + 1) * P], pd[:, u, :, :].rearrange("p h r -> p (h r)"),
                                              ident[:, :])
                        mm.then_inc(m.pd_psum, 1)
                        prev_misc[0] = ("PD", i, 0)
                    if t == 0:
                        wait(pe, m.so_ok, TT * i)
                        pe.wait_ge(m.ot_ok, HP * i + HP - 1)
                    if t in (1, 2):
                        free_pr(i, "W", t)
                    for hp in range(HP):
                        if t == 0 and hp == HP - 1:
                            pe.wait_ge(m.ot_ok, HP * (i + 1))
                        pe.matmul(w_bank(t)[:, 0:E], ot[:, hp, t * P:(t + 1) * P], wout[:, hp, :],
                                  start=(hp == 0), stop=False)
                pe.wait_ge(m.pdt_ok, i + 1)
                for t in W_ORDER:
                    pe.matmul(w_bank(t)[:, 0:E], pdt[:, t * P:(t + 1) * P], ud[:, :],
                              start=False, stop=True).then_inc(m.w_psum, 1)

            over_batches(pe, body)

        @block.scalar
        def _(act):
            act.wait_ge(m.w_load, 16)
            act.activation(win_h[:, :, :].rearrange("p k n -> p (k n)"), work[:, :], ACT.Copy).then_inc(m.w_high, 1)
            act.wait_ge(m.trig, 8)
            act.activation(cs[:, :, 0:E], turns[0], ACT.Sin, scale=-1.0, bias=halfpi[:, 0:1]).then_inc(m.sin_ok, 1)
            act.wait_ge(m.trig, 15)
            act.activation(cs[:, :, E:2 * E], ang[1], ACT.Sin).then_inc(m.sin_ok, 1)
            act.wait_ge(m.sin_ok, 2)
            act.activation(cs_h[:, :, :], cs, ACT.Copy).then_inc(m.cs_high, 1)
            act.wait_ge(m.g_psum, 1)
            act.activation(gk[:, :, :, :].rearrange("p k h r -> p (k h r)"), misc[:, 0:KC * P], ACT.Copy).then_inc(m.g_ok, 1)
            act.activation(ud[:, :], fin[:, 0:E], ACT.Copy).then_inc(m.g_ok, 1)
            act.activation(beta[:, :, :].rearrange("p h r -> p (h r)"), o_ps[:, 0, 0:P], ACT.Copy).then_inc(m.g_ok, 1)

            def transposed(i, kc):
                act.wait_ge(m.xt_psum, KC * i + kc + 1)
                if kc == 0:
                    wait(act, m.qk_psum, 2 * HP * i)
                    wait(act, m.f_psum, TT * i)
                    wait(act, m.v_psum, 2 * TT * i)
                    wait(act, m.r_psum, i)
                act.activation(xt[:, kc, :], misc[:, :], ACT.Copy)
                act.activation(xt_h[:, kc, :], misc[:, :], ACT.Copy).then_inc(m.xt_high, 1)

            for kc in range(KC):
                transposed(0, kc)

            def exp_pair(i, k):
                act.wait_ge(m.sub_ok, HP * i + k + 1)
                wait(act, m.pt_ok, 4 * (HP * i + k - 1))
                act.activation(ex[:, k % 2, :, :, :], sc[:, k % 2, :, :, :], ACT.Exp, scale=D1 ** -0.5).then_inc(m.ex_ok, 1)

            def body(i):
                last = isinstance(i, int) and i >= NT1 - 1
                for kind, k in steps:
                    if kind == "V":
                        act.wait_ge(m.v_psum, 2 * TT * i + k + 1)
                        if k == 0:
                            wait(act, m.o_psum, HP * i)
                        c = 512 * (k % 2)
                        act.activation(v[:, k // 2, c:c + 512], pr[:, through_pr.index(("V", k)) % 2, :],
                                       ACT.Copy).then_inc(m.v_ok, 1)
                    if kind in ("Q", "K"):
                        side = int(kind == "K")
                        n = 2 * HP * i + 2 * k + side
                        act.wait_ge(m.qk_psum, n + 1)
                        wait(act, m.s_psum, HP * i + k - 1)
                        bank = pr[:, through_pr.index((kind, k)) % 2, :]
                        act.activation((qt, kt)[side][:, k % 2, :], bank, ACT.Identity,
                                       bias=bqkv[:, HP * side + k:HP * side + k + 1]).then_inc(m.qk_ok, 1)
                    if kind == "F":
                        if k == 0:
                            exp_pair(i, HP - 1)
                        act.wait_ge(m.f_psum, TT * i + k + 1)
                        wait(act, m.q2_ok, TT * i + k - 1)
                        act.activation(sq[:, k % 2, :], pr[:, through_pr.index((kind, k)) % 2, :],
                                       ACT.Square).then_inc(m.sq_ok, 1)
                    if kind == "S" and k >= 1:
                        exp_pair(i, k - 1)
                    if kind == "AV":
                        act.wait_ge(m.o_psum, HP * i + k + 1)
                        if k == 0:
                            wait(act, m.w_psum, TT * i)
                        act.activation(ot[:, k, :], o_ps[:, k % 2, :], ACT.Identity,
                                       bias=bqkv[:, 2 * HP + k:2 * HP + k + 1]).then_inc(m.ot_ok, 1)
                if not last:
                    for kc in range(KC):
                        transposed(i + 1, kc)
                act.wait_ge(m.q2_ok, TT * (i + 1))
                wait(act, m.gate_ok, i)
                act.activation(q2[:, :, :], q2[:, :, :], ACT.Sqrt).then_inc(m.sqrt_ok, 1)
                act.wait_ge(m.sqrt_ok, i + 1)
                act.activation(th[:, :, :], q2[:, :, :], ACT.Tanh, scale=0.5).then_inc(m.tanh_ok, 1)
                act.wait_ge(m.pd_psum, i + 1)
                act.activation(pdt[:, :], misc[:, :], ACT.Copy).then_inc(m.pdt_ok, 1)

            over_batches(act, body)

        @block.vector
        def _(dve):
            for i in range(2):
                dve.memset(pt[i][:, :, :, :], 0.0).then_inc(m.zero_pt, 1)
            dve.memset(mhalf[:, :], -0.5).then_inc(m.consts_ok, 1)
            dve.memset(halfpi[:, :], float(np.pi / 2)).then_inc(m.consts_ok, 1)
            dve.wait_ge(m.theta_load, 16 * TLOADS)
            dve.wait_ge(m.consts_ok, 2)
            n = 0
            for a in range(2):
                ops = [lambda: dve.tensor_tensor(ang[a], ang[a], noise[a], ALU.add),
                       lambda: dve.tensor_scalar(turns[a], ang[a], float(1 / (2 * np.pi)), ROUND, ALU.mult, ALU.add),
                       lambda: dve.tensor_scalar(turns[a], turns[a], ROUND, None, ALU.subtract)]
                ops += [(lambda c: lambda: dve.scalar_tensor_tensor(ang[a], turns[a], -c, ang[a], op0=ALU.mult, op1=ALU.add))(c)
                        for c in TWO_PI]
                ops += [lambda: dve.tensor_scalar(ang[a], ang[a], PI_BELOW, -PI_BELOW, ALU.min, ALU.max)]
                if a == 0:
                    ops += [lambda: dve.scalar_tensor_tensor(turns[0], ang[0], -1.0, ang[0], op0=ALU.mult, op1=ALU.max)]
                for op in ops:
                    op().then_inc(m.trig, 1)
                    n += 1
                    dve.wait_ge(m.trig, n)
            dve.wait_ge(m.w_high, 1)
            dve.tensor_tensor(win_l[:, :, :].rearrange("p k n -> p (k n)"), work[:, :],
                              win_h[:, :, :].rearrange("p k n -> p (k n)").bitcast(F32), ALU.subtract).then_inc(m.w_low, 1)
            dve.wait_ge(m.b_load, 16 * BLOADS)
            for hp in range(HP):
                dve.tensor_scalar(kdb[:, hp, :], kdx[:, :, :].rearrange("p a b -> p (a b)"), bqkv[:, hp:hp + 1], None,
                                  ALU.mult).then_inc(m.kdb_ok, 1)
            dve.wait_ge(m.cs_high, 1)
            dve.tensor_tensor(cs_l[:, :, :], cs, cs_h[:, :, :].bitcast(F32), ALU.subtract).then_inc(m.cs_low, 1)
            dve.wait_ge(m.w_low, 1)
            dve.wait_ge(m.g_ok, 3)

            def norm_stats(i):
                dve.wait_ge(m.x_load, 16 * (i + 1))
                for t in range(TT):
                    dve.bn_stats(stat[:, t, :], xb[:, t, :]).then_inc(m.stats, 1)
                dve.wait_ge(m.stats, TT * (i + 1))
                wait(dve, m.veps_ok, i)
                stand_alone(dve, m.dve_passed)
                for t in range(TT):
                    dve.bn_aggr(mv[:, t, :], stat[:, t, :]).then_inc(m.aggr, 1)

            def normalise(i):
                dve.wait_ge(m.rstd_ok, i + 1)
                wait(dve, m.xt_psum, KC * i)
                for t in range(TT):
                    ins = dve.tensor_scalar(xn[:, t, :], xb[:, t, :], mv[:, t, 0:1], rstd[:, t:t + 1],
                                            ALU.subtract, ALU.mult)
                ins.then_inc(m.xn_ok, 1)

            def low_parts(i, kc):
                dve.wait_ge(m.xt_high, KC * i + kc + 1)
                dve.tensor_tensor(xt_l[:, kc, :], misc[:, :], xt_h[:, kc, :].bitcast(F32),
                                  ALU.subtract).then_inc(m.xt_low, 1)

            def key_distances(i):
                dve.wait_ge(m.r_psum, i + 1)
                wait(dve, m.r_sum, 2 * NREL * i)
                dve.tensor_tensor(r15[:, :, :, NREL - 1:].rearrange("p h t r -> p t h r"), misc[:, :].rearrange("p (t h r) -> p t h r", t=TT, h=H1),
                                  beta[:, :, :].unsqueeze(1).to_broadcast([P, TT, H1, NREL]), ALU.add).then_inc(m.r_evac, 1)
                dve.wait_ge(m.r_evac, i + 1)
                dve.tensor_copy(r15[:, :, :, 0:NREL - 1], r15[:, :, :, 2 * NREL - 2:NREL - 1:-1]).then_inc(m.r_flip, 1)

            def own_keys(i, half, s):
                heads = slice(half * HP, (half + 1) * HP)
                src, dst = r15[:, heads, :, NREL - 1 - s:2 * NREL - 1 - s], rt[:, heads, :, :]
                if s == 0:
                    dve.wait_ge(m.r_flip, i + 1)
                    wait(dve, m.rm_ok, TT * i)
                    dve.tensor_scalar(dst, src, own[:, 0:1], None, ALU.mult).then_inc(m.r_sum, 1)
                else:
                    dve.wait_ge(m.r_sum, NREL * (2 * i + half) + s)
                    dve.scalar_tensor_tensor(dst, src, own[:, s:s + 1], dst,
                                             op0=ALU.mult, op1=ALU.add).then_inc(m.r_sum, 1)

            def scores(i, k):
                n = HP * i + k
                dve.wait_ge(m.s_psum, n + 1)
                wait(dve, m.ex_ok, n - 1)
                if k % 2 == 0:
                    dve.wait_ge(m.rm_ok, 4 * i + k // 2 + 1)
                a = sc[:, k % 2, :, :, :]
                dve.tensor_tensor(a, s_ps[:, :, 0:TT * BLK].rearrange("p h (t k) -> p h t k", t=TT),
                                  rm[:, 2 * k:2 * k + 2, :, :], ALU.add).then_inc(m.sc_ok, 1)
                dve.wait_ge(m.sc_ok, n + 1)
                dve.tensor_reduce(mx[:, k % 2, :, :], a, X, ALU.max).then_inc(m.mx_ok, 1)

            def key_sums(i, k):
                n = HP * i + k
                e = ex[:, k % 2, :, :, :]
                dve.wait_ge(m.ex_ok, n + 1)
                wait(dve, m.pc_ok, n - 1)
                dve.tensor_reduce(ec[:, k % 2, :, :, :].rearrange("p h t s -> p (h t) s"),
                                  e.rearrange("p h t (n s) -> p (h t) s n", n=4), X, ALU.add).then_inc(m.ec_ok, 1)
                dve.wait_ge(m.ec_ok, n + 1)
                dve.tensor_reduce(sm[:, k % 2, :, :], ec[:, k % 2, :, :, :], X, ALU.add).then_inc(m.sm_ok, 1)
                dve.wait_ge(m.sm_ok, n + 1)
                wait(dve, m.p_ok, n - 1)
                dve.reciprocal(rc[:, k % 2, :, :], sm[:, k % 2, :, :]).then_inc(m.rc_ok, 1)
                dve.wait_ge(m.rc_ok, n + 1)
                if k == 0:
                    wait(dve, m.p15_sum, 2 * NREL * i)
                dve.tensor_tensor(pc[:, 2 * k:2 * k + 2, :, :], ec[:, k % 2, :, :, :],
                                  rc[:, k % 2, :, :].unsqueeze(3).to_broadcast([P, 2, TT, NREL]), ALU.mult).then_inc(m.pc_ok, 1)

            def transposed_blocks(i, k):
                n = HP * i + k
                e = ex[:, k % 2, :, :, :]
                dve.wait_ge(m.p_ok, n + 1)
                wait(dve, m.o_psum, n - 1)
                for q in range(4):
                    rows = slice(BLK * q, BLK * (q + 1))
                    dve.transpose(pt[k % 2][rows, :, :, :].rearrange("p h t k -> p (h t) k")[:, :, rows],
                                  e[rows, :, :, :].rearrange("p h t k -> p (h t) k")).then_inc(m.pt_ok, 1)

            def by_distance(i, half, batches):
                heads = slice(half * HP, (half + 1) * HP)
                n = NREL * (2 * i + half)
                if half == 0 and 0 in batches:
                    dve.wait_ge(m.p15_zero, i + 1)
                dve.wait_ge(m.pc_ok, HP * i + HP // 2 * (half + 1))
                for s in batches:
                    wait(dve, m.p15_sum, n + s)
                    dst = p15[:, heads, :, NREL - 1 - s:2 * NREL - 1 - s]
                    dve.scalar_tensor_tensor(dst, pc[:, heads, :, :], own[:, s:s + 1], dst,
                                             op0=ALU.mult, op1=ALU.add).then_inc(m.p15_sum, 1)

            def distances(i):
                dve.wait_ge(m.p15_sum, 2 * NREL * (i + 1))
                wait(dve, m.pd_psum, i)
                by_head = pd[:, :, :, :].rearrange("p t h r -> p h t r")
                dve.tensor_copy(by_head[:, :, :, 0:1], p15[:, :, :, NREL - 1:NREL]).then_inc(m.pd_ok, 1)
                dve.tensor_tensor(by_head[:, :, :, 1:], p15[:, :, :, NREL:], p15[:, :, :, NREL - 2::-1], ALU.add).then_inc(m.pd_ok, 1)

            def read_output(i, n):
                t = W_ORDER[n]
                dve.wait_ge(m.w_psum, TT * i + n + 1)
                if n < 2:
                    wait(dve, m.stored[n], 16 * 2 * i)
                else:
                    dve.wait_ge(m.stored[n % 2], 16 * (2 * i + 1))
                bank = (fin, pr[:, through_pr.index(("W", 1)) % 2, :], pr[:, through_pr.index(("W", 2)) % 2, :],
                        o_ps[:, 0, :])[t]
                dve.tensor_tensor(so[:, n % 2, :], bank[:, 0:E], bout[:, :], ALU.add).then_inc(m.so_ok, 1)

            def gate_output(i, n):
                t = W_ORDER[n]
                dve.wait_ge(m.so_ok, TT * i + n + 1)
                dve.scalar_tensor_tensor(so[:, n % 2, :], so[:, n % 2, :], 0.5, q2[:, t, :], op0=ALU.mult,
                                         op1=ALU.mult).then_inc(m.sg_ok, 1)
                dve.wait_ge(m.sg_ok, TT * i + n + 1)
                if n == 0:
                    dve.wait_ge(m.xr_load, 16 * (i + 1))
                dve.tensor_tensor(so[:, n % 2, :], so[:, n % 2, :], xr[:, t, :], ALU.add).then_inc(m.x2_ok, 1)

            norm_stats(0)
            normalise(0)
            for kc in range(KC):
                low_parts(0, kc)

            def body(i):
                last = isinstance(i, int) and i >= NT1 - 1
                key_distances(i)
                for half in range(2):
                    for s in range(NREL):
                        own_keys(i, half, s)
                for k in range(HP):
                    if k >= 1:
                        key_sums(i, k - 1)
                    scores(i, k)
                    if k >= 1:
                        transposed_blocks(i, k - 1)
                    if k == 1 and not last:
                        norm_stats(i + 1)
                    if k == 3 and not last:
                        normalise(i + 1)
                    if k >= 4:
                        by_distance(i, 0, ((0, 1, 2), (3, 4, 5), (6, 7), ())[k - 4])
                key_sums(i, HP - 1)
                transposed_blocks(i, HP - 1)
                if not last:
                    low_parts(i + 1, 0)
                by_distance(i, 1, range(NREL))
                distances(i)
                if not last:
                    low_parts(i + 1, 1)
                dve.wait_ge(m.tanh_ok, i + 1)
                dve.scalar_tensor_tensor(q2[:, :, :], th[:, :, :], 1.0, q2[:, :, :], op0=ALU.add,
                                         op1=ALU.mult).then_inc(m.gate_ok, 1)
                dve.wait_ge(m.gate_ok, i + 1)
                for n in (0, 2):
                    read_output(i, n)
                    read_output(i, n + 1)
                    gate_output(i, n)
                    gate_output(i, n + 1)

            over_batches(dve, body)

        @block.gpsimd
        def _(pool):
            pool.wait_ge(m.consts_ok, 2)
            pool.wait_ge(m.x_load, 16)

            def rstd_of(i):
                pool.wait_ge(m.aggr, TT * (i + 1))
                wait(pool, m.xn_ok, i)
                stand_alone(pool, m.pool_passed)
                pool.tensor_scalar(veps[:, :], mv[:, :, 1], LN_EPS, None, ALU.add).then_inc(m.veps_ok, 1)
                pool.wait_ge(m.veps_ok, i + 1)
                pool.tensor_tensor(rstd[:, :], veps[:, :], mhalf[:, :], ALU.pow).then_inc(m.rstd_ok, 1)

            def less_maximum(i, k):
                pool.wait_ge(m.mx_ok, HP * i + k + 1)
                pool.tensor_tensor(sc[:, k % 2, :, :, :], sc[:, k % 2, :, :, :],
                                   mx[:, k % 2, :, :].unsqueeze(3).to_broadcast([P, 2, TT, BLK]),
                                   ALU.subtract).then_inc(m.sub_ok, 1)

            def weigh(i, k):
                pool.wait_ge(m.rc_ok, HP * i + k + 1)
                pool.tensor_tensor(ex[:, k % 2, :, :, :], ex[:, k % 2, :, :, :],
                                   rc[:, k % 2, :, :].unsqueeze(3).to_broadcast([P, 2, TT, BLK]),
                                   ALU.mult).then_inc(m.p_ok, 1)

            rstd_of(0)
            pool.wait_ge(m.b_load, 16 * BLOADS)

            def body(i):
                last = isinstance(i, int) and i >= NT1 - 1
                wait(pool, m.sc_ok, HP * i)
                for g in range(4):
                    if g % 2 == 0:
                        pool.wait_ge(m.r_sum, NREL * (2 * i + g // 2 + 1))
                    heads = slice(4 * g, 4 * (g + 1))
                    pool.tensor_tensor(
                        rm[:, heads, :, :].rearrange("p h t (n s) -> p (h t) n s", n=4),
                        rt[:, heads, :, :].rearrange("p h t s -> p (h t) s").unsqueeze(2).to_broadcast([P, 4 * TT, 4, NREL]),
                        apart[:, :].rearrange("p (n s) -> p n s", n=4).unsqueeze(1).to_broadcast([P, 4 * TT, 4, NREL]),
                        ALU.add).then_inc(m.rm_ok, 1)
                wait(pool, m.pd_ok, 2 * i)
                stand_alone(pool, m.pool_passed)
                pool.memset(p15[:, :, :, :], 0.0).then_inc(m.p15_zero, 1)
                for k in range(HP):
                    if k >= 1:
                        weigh(i, k - 1)
                    less_maximum(i, k)
                    if k == 2 and not last:
                        rstd_of(i + 1)
                weigh(i, HP - 1)
                for t in range(TT):
                    pool.wait_ge(m.sq_ok, TT * i + t + 1)
                    if t == 0:
                        wait(pool, m.x2_ok, TT * i)
                    pool.tensor_tensor(q2[:, t, :], sq[:, t % 2, 0:E], sq[:, t % 2, E:2 * E], ALU.add).then_inc(m.q2_ok, 1)

            over_batches(pool, body)


def layout1(a):
    kd, vd = a["L1_attn_k_dist_emb"][:NREL], a["L1_attn_v_dist_emb"][:NREL]
    kdx = np.zeros((2, D1, 2, NREL), np.float32)
    vdx = np.zeros((2, D1, HP, H1, NREL), np.float32)
    for h in range(2):
        kdx[h, :, h, :] = kd.T
        for hp in range(HP):
            vdx[h, :, hp, 2 * hp + h, :] = vd.T
    p = np.arange(P)
    key = np.arange(BLK)
    out = {
        "win": a["L1_attn_W_in"].T,
        "wqn": a["L1_attn_W_in"][:H1 * D1],
        "bqkv": a["L1_attn_b_in"].reshape(3 * HP, P).T,
        "kdx": kdx.reshape(P, 2, NREL),
        "vdx": vdx.reshape(P, HP, H1 * NREL),
        "wout": a["L1_attn_W_out"].T,
        "bout": a["L1_attn_b_out"],
        "theta": a["L1_ffn_theta"], "phi": a["L1_ffn_phi"],
        "theta_noise": a["L1_ffn_theta_noise"], "phi_noise": a["L1_ffn_phi_noise"],
        "apart": np.where((p[:, None] % BLK) // NREL == key[None, :] // NREL, 0.0, NEG).astype(np.float32),
        "own": (p[:, None] % NREL == np.arange(NREL)[None, :]).astype(np.float32),
        "ones": np.ones((P, P), np.float32),
        "ident": np.eye(P, dtype=np.float32),
    }
    return {k: np.ascontiguousarray(v) for k, v in out.items()}


def layout0(a):
    def halves(w):
        return w.reshape(2, HG, 2, F0, E).transpose(4, 0, 2, 1, 3).reshape(E, HALF, HG * F0)

    pick = np.zeros((P, HALF, BLK), np.float32)
    which = np.zeros((2, HG, HG, S), np.float32)
    for i in range(HALF):
        pick[:, i, i] = 1.0
        which[:, i, i, :] = 1.0
    out = {
        "x": a["L0_attn_x"],
        "wqk": np.concatenate([halves(a["L0_attn_Wq"]), halves(a["L0_attn_Wk"])], axis=2),
        "wcat": np.concatenate([a["L0_attn_Wv"].T, a["L0_ffn_w_route"].T, a["L0_ffn_compress"].T], axis=1),
        "wo": a["L0_attn_Wo"].T,
        "normw": a["L0_attn_norm_w"].reshape(KC, P).T,
        "bo": a["L0_attn_bo"],
        "dw": a["L0_attn_diff_weight"].reshape(1),
        "routed": a["L0_ffn_routed"].transpose(0, 2, 1).reshape(NE * R, E),
        "ident": np.eye(P, dtype=np.float32),
        "rank8": np.arange(NE, 0, -1, dtype=np.float32),
        "pick": pick,
        "which": which.reshape(MROWS, HG, S),
    }
    return {k: np.ascontiguousarray(v) for k, v in out.items()}


def build(nc, io0, io1, out):
    x1 = nc.dram_tensor("x1", [S, B, E], F32).ap()
    layer0(nc, io0, x1)
    layer1(nc, io1, x1, out)


def kernel(**inputs):
    import concourse.bacc as bacc
    from concourse.bass_utils import run_bass_kernel_spmd as run

    nc = bacc.Bacc("TRN2", target_bir_lowering=False, num_devices=1)
    a = {k: np.asarray(v) for k, v in inputs.items()}
    arrays, io = {}, []
    for layer, layout in enumerate((layout0, layout1)):
        io.append({})
        for k, v in layout(a).items():
            arrays[f"in{layer}_{k}"] = v
            io[-1][k] = nc.dram_tensor(f"in{layer}_{k}", v.shape, mybir.dt.from_np(v.dtype), kind="ExternalInput").ap()
    out = nc.dram_tensor("out", [S, B, E], F32, kind="ExternalOutput").ap()
    build(nc, *io, out)
    r = run(nc, [arrays], core_ids=[0])
    return np.ascontiguousarray(r.results[0]["out"].transpose(1, 0, 2))
```

```python
from contextlib import ExitStack

import numpy as np

import concourse.bass as bass
from concourse import mybir

F32 = mybir.dt.float32
F32R = mybir.dt.float32r
I32 = mybir.dt.int32
ALU = mybir.AluOpType
ACT = mybir.ActivationFunctionType
X = mybir.AxisListType.X

P = 128
B, S, E = 8, 512, 256
KC = E // P
QT = S // P
LN_EPS = 1e-5

H0 = 8
DH0 = E // H0
F0 = DH0 // 2
HG = 4
HALF = 4
UNITS = 16
NE, R = 8, 16
WCAT = E + NE + R
STACK = 4 * F0
MROW = 96
MROWS = 2 * HG
LEAD = 24
S_BANK = [w % 3 for w in range(UNITS - 1)] + [1]
S_BACK = [next(d for d in range(1, UNITS) if S_BANK[w - d] == S_BANK[w]) for w in range(UNITS)]
D_PARTS = ((0, 0), (1, 1), (2, 0), (3, 1), (3, 0))
SUMS = 11
LAG = 2
SCALE0 = float(F0) ** -0.5
EPS32 = float(np.finfo(np.float32).eps)

H1 = 16
D1 = 64
HP = H1 // 2
NREL = 8
NS = 64
NT1 = S // NS
TOK = NS * B
TT = TOK // P
BLK = 32
NBLK = TOK // BLK
NEG = -1e30


class Semaphores:
    pass


def wait(eng, sem, value):
    if not (isinstance(value, int) and value <= 0):
        eng.wait_ge(sem, value)


def stand_alone(eng, passed):
    eng.sem_inc(passed, 1)


def over_batches(eng, body, before=1):
    for b in range(before):
        body(b)
    with eng.Fori(before, B - 1) as b:
        body(b)
    body(B - 1)


SLOTS = ((0, 1), (0, 4), (0, 6), (0, 9), (0, 11), (0, 14),
         (1, 0), (1, 1), (1, 4), (1, 5), (1, 7), (1, 9), (1, 10), (1, 13),
         (2, 0), (2, 3), (2, 5), (2, 8), (2, 10), (2, 11), (2, 14),
         (3, 1), (3, 5), (3, 7), (3, 9), (3, 13))
JOBS = (("PROJ", 3, 0), ("V", 0, 2), ("V", 0, 3), ("M", 1, 0), ("XT", 1, 0), ("XT", 1, 1), ("TD", -1, 0),
        ("TA", -1, 0), ("TA", -1, 1), ("TA", -1, 2), ("TA", -1, 3), ("M", 2, 0), ("PROJ", 4, 0), ("V", 1, 0),
        ("PROJ", 5, 0), ("OT", -1, 0), ("OT", -1, 1), ("ZT", -1, 0), ("M", 3, 0), ("WF", -1, 0), ("WF", -1, 1),
        ("PROJ", 6, 0), ("WF", -1, 2), ("WF", -1, 3), ("M", 4, 0), ("V", 1, 1))
STATS, NORMS = ((0, 2), (0, 3)), ((0, 6), (0, 9))
NORM_ENDS, VALUES_COPY = (0, 3), (0, 7)
GATE, GATE_END, GATED = (1, 15), (3, 6), (3, 15)
SUM_STEP, LATE_SUMS, EVAC_STEP = 9, (2, 8), 7


def layer0_jobs(b):
    nxt = not (isinstance(b, int) and b >= B - 1)
    prv = not (isinstance(b, int) and b < 1)
    jobs = []
    for slot, (kind, shift, k) in zip(SLOTS, JOBS):
        by_half = kind in ("PROJ", "M")
        if (shift < 0 and not prv) or (shift >= (4 if by_half else 1) and not nxt):
            continue
        jobs.append((slot, kind, HALF * b + shift if by_half else b + shift, k))
    return jobs


FIRST_JOBS = [("XT", 0, 0), ("XT", 0, 1), ("PROJ", 0, 0), ("PROJ", 1, 0), ("V", 0, 0), ("V", 0, 1),
              ("PROJ", 2, 0), ("M", 0, 0)]
LAST_JOBS = [("TD", B - 1, 0)] + [("TA", B - 1, t) for t in range(QT)] + [("OT", B - 1, 0), ("OT", B - 1, 1),
             ("ZT", B - 1, 0)] + [("WF", B - 1, t) for t in range(QT)]


TWO_PI = (6.28125, 0.0019350051879882812, 3.019916050561733e-07)
ROUND = 1.5 * 2.0 ** 23
PI_BELOW = 3.1415925

ROOM = 16384


class Shared:

    def __init__(self, nc, ctx):
        def sb(name, shape, dt=F32):
            return ctx.enter_context(nc.sbuf_tensor(name, shape, dt))

        def rooms(*shapes):
            parts, at = [], 0
            for shape in shapes:
                size = int(np.prod(shape))
                part = room[:, at:at + size]
                names = "abc"[:len(shape)]
                if len(shape) > 1:
                    part = part.rearrange(f"p ({' '.join(names)}) -> p {' '.join(names)}",
                                          **{n: d for n, d in zip(names[:-1], shape[:-1])})
                parts.append(part)
                at += size
            assert at == ROOM
            return parts

        room = sb("room", [P, ROOM])
        self.probs, self.sums, self.at, self.xb, self.xn = rooms(
            (4, HG, S), (2, HG, S), (HALF, S), (QT, E), (QT, E))
        self.work, self.ot, self.q2, self.th, self.wout, self.sq, self.kt = rooms(
            (KC * 3 * H1 * D1,), (HP, TOK), (TT, E), (TT, E), (HP, E), (2, 2 * E), (2, TOK))

        self.wqn = self.ot[:, 0:4, :].rearrange("p a b -> p (a b)").rearrange("p (h c) -> p h c", h=HP)
        self.vdx = self.ot[:, 4:6, :].rearrange("p a b -> p (a b)").rearrange("p (h c) -> p h c", h=HP)
        self.kdb = self.ot[:, 6, 0:HP * 2 * NREL].rearrange("p (h c) -> p h c", h=HP)
        self.ones = self.ot[:, 7, 0:P]
        halves = [part[:, i, :].rearrange("p (k n) -> p k n", k=KC) for part in (self.sq, self.kt) for i in range(2)]
        self.ang, self.turns = halves[0::2], halves[1::2]
        self.noise = (self.q2[:, 0:KC, :], self.th[:, 0:KC, :])
        self.ident = sb("ident", [P, P])
        self.bqkv = sb("bqkv", [P, 3 * HP])
        self.apart = sb("apart", [P, BLK])
        self.own = sb("own", [P, NREL])
        self.kdx = sb("kdx", [P, 2, NREL])
        self.w_load = ctx.enter_context(nc.semaphore("w_load1"))
        self.b_load = ctx.enter_context(nc.semaphore("b_load1"))
        self.theta_load = ctx.enter_context(nc.semaphore("theta_load1"))
        self.trig = ctx.enter_context(nc.semaphore("trig1"))

    B_LOADS, THETA_LOADS = 8, 4

    def load_first(self, sp, io):
        for dst, name in ((self.ang[0], "theta"), (self.noise[0], "theta_noise"), (self.ang[1], "phi"),
                          (self.noise[1], "phi_noise")):
            sp.dma_start(dst, io[name].rearrange("(k p) n -> p k n", p=P)).then_inc(self.theta_load, 16)
        sp.dma_start(self.work.rearrange("p (k n) -> p k n", k=KC),
                     io["win"].rearrange("(k p) n -> p k n", p=P)).then_inc(self.w_load, 16)
        for dst, src in (
                (self.wqn, io["wqn"].rearrange("(h p) c -> p h c", p=P)), (self.vdx, io["vdx"]),
                (self.kdx[:, :, :], io["kdx"]), (self.bqkv[:, :], io["bqkv"]), (self.apart[:, :], io["apart"]),
                (self.own[:, :], io["own"]), (self.ones, io["ones"])):
            sp.dma_start(dst, src).then_inc(self.b_load, 16)

    def load_last(self, sp, io):
        sp.dma_start(self.wout, io["wout"].rearrange("(h p) c -> p h c", p=P)).then_inc(self.b_load, 16)

    def less_turns(self, dve, a):
        ang, turns = self.ang[a], self.turns[a]
        if a == 0:
            dve.wait_ge(self.theta_load, 16 * self.THETA_LOADS)
        n = 8 * a
        dve.tensor_tensor(ang, ang, self.noise[a], ALU.add).then_inc(self.trig, 1)
        dve.wait_ge(self.trig, n + 1)
        dve.tensor_scalar(turns, ang, float(1 / (2 * np.pi)), ROUND, ALU.mult, ALU.add).then_inc(self.trig, 1)
        dve.wait_ge(self.trig, n + 2)
        dve.tensor_scalar(turns, turns, ROUND, None, ALU.subtract).then_inc(self.trig, 1)
        dve.wait_ge(self.trig, n + 3)
        for i, c in enumerate(TWO_PI):
            dve.scalar_tensor_tensor(ang, turns, -c, ang, op0=ALU.mult, op1=ALU.add).then_inc(self.trig, 1)
            dve.wait_ge(self.trig, n + 4 + i)
        dve.tensor_scalar(ang, ang, PI_BELOW, -PI_BELOW, ALU.min, ALU.max).then_inc(self.trig, 1)
        if a == 0:
            dve.wait_ge(self.trig, n + 7)
            dve.scalar_tensor_tensor(turns, ang, -1.0, ang, op0=ALU.mult, op1=ALU.max).then_inc(self.trig, 1)


def layer0(nc, io, io1, shared, x1_dram):
    with ExitStack() as ctx:
        def sb(name, shape, dt=F32):
            return ctx.enter_context(nc.sbuf_tensor(name, shape, dt))

        def bank(name):
            return ctx.enter_context(nc.psum_tensor(name, [P, 512], F32))

        def sem(name):
            return ctx.enter_context(nc.semaphore(name))

        ident = shared.ident
        wqk_h, wqk_l = sb("wqk_h", [P, KC, HALF, P], F32R), sb("wqk_l", [P, KC, HALF, P], F32R)
        wcat = sb("wcat", [P, KC, WCAT])
        wo = sb("wo", [P, KC, E])
        normw = sb("normw", [P, KC])
        routed = sb("routed", [P, E])
        bo = sb("bo", [P, E])
        dw = sb("dw", [P, 1])
        one_dw, neg_dw = sb("one_dw", [P, 1]), sb("neg_dw", [P, 1])
        rank8 = sb("rank8", [P, NE])
        pick = sb("pick", [P, HALF, BLK])
        mhalf = sb("mhalf", [P, QT])
        xb, xn = shared.xb, shared.xn
        stat, mv = sb("stat", [P, QT, 6]), sb("mv", [P, QT, 2])
        veps, rstd = sb("veps", [P, QT]), sb("rstd", [P, QT])
        xt = sb("xt", [P, KC, S])
        xt_h, xt_l = sb("xt_h", [P, KC, S], F32R), sb("xt_l", [P, KC, S], F32R)
        qk_h, qk_l = sb("qk_h", [P, S], F32R), sb("qk_l", [P, S], F32R)
        qst = [sb(f"qst{i}", [P, HG, S], F32R) for i in range(HALF)]
        kst = [sb(f"kst{i}", [P, HG, S], F32R) for i in range(HALF)]
        vnew = sb("vnew", [P, QT, WCAT])
        v = sb("v", [P, QT, E])
        lc = sb("lc", [P, QT, NE + R])
        negmax = sb("negmax", [P, 2, QT, HG])
        msplit = sb("msplit", [P, QT, 2, HG], F32R)
        mrow = sb("mrow", [P, S], F32R)
        probs = shared.probs
        which = probs[:, 0, :, :]
        sums = shared.sums
        wqk = sums[:, 0, 0:2, :].rearrange("p a (k n) -> p a k n", k=HALF)
        at = shared.at
        dt_ = sb("dt", [P, S])
        rec = sb("rec", [P, QT, HALF, HG])
        an = sb("an", [P, HALF, HG, DH0])
        o = sb("o", [P, QT, E])
        ss, ms, rms = sb("ss", [P, QT]), sb("ms", [P, QT]), sb("rms", [P, QT])
        ot = sb("ot", [P, KC, S])
        gt = sb("gt", [P, 8, QT, NE])
        gs = sb("gs", [P, 8, QT])
        z, zt = sb("z", [P, QT, NE, R]), sb("zt", [P, S])
        th, s_, g_ = sb("th", [P, QT, E]), sb("s_", [P, QT, E]), sb("g_", [P, QT, E])
        xr, x1o = sb("xr", [P, QT, E]), sb("x1o", [P, 2, E])

        s_bank = [bank("s_bank0"), bank("s_bank1"), bank("s_bank2")]
        t_bank = [bank("t_bank0"), bank("t_bank1")]
        a_bank = bank("a_bank0")
        d_bank = bank("d_bank")
        misc = bank("misc0")
        first_banks = (a_bank, d_bank, misc, t_bank[0], t_bank[1])
        last_banks = (misc, s_bank[0], s_bank[1], s_bank[2], t_bank[0], t_bank[1])
        assert first_banks[(len(FIRST_JOBS) - 1) % len(first_banks)] is misc

        park = nc.dram_tensor("park", [2, P, S], F32).ap()

        m = Semaphores()
        m.w_load = sem("w_load0")
        m.wsplit = sem("wsplit0")
        m.x_load = sem("x_load0")
        m.stats = sem("stats0")
        m.aggr = sem("aggr0")
        m.veps_ok = sem("veps_ok0")
        m.rstd_ok = sem("rstd_ok0")
        m.xn_ok = sem("xn_ok0")
        m.xt_psum = sem("xt_psum0")
        m.xt_high = sem("xt_high0")
        m.xt_low = sem("xt_low0")
        m.xt_sum = sem("xt_sum0")
        m.proj_psum = sem("proj_psum0")
        m.qk_high = sem("qk_high0")
        m.qk_low = sem("qk_low0")
        m.parked = sem("parked0")
        m.stacked = sem("stacked0")
        m.v_psum = sem("v_psum0")
        m.vnew_ok = sem("vnew_ok0")
        m.v_ok = sem("v_ok0")
        m.lc_ok = sem("lc_ok0")
        m.s_done = sem("s_done0")
        m.max_done = sem("max_done0")
        m.m_high = sem("m_high0")
        m.m_low = sem("m_low0")
        m.m_psum = sem("m_psum0")
        m.m_evac = sem("m_evac0")
        m.m_placed = sem("m_placed0")
        m.t_done = sem("t_done0")
        m.exp_done = sem("exp_done0")
        m.sum_ok = sem("sum_ok0")
        m.a_done = sem("a_done0")
        m.d_done = sem("d_done0")
        m.a_evac = sem("a_evac0")
        m.d_evac = sem("d_evac0")
        m.td_psum = sem("td_psum0")
        m.recip_ok = sem("recip_ok0")
        m.rec_ok = sem("rec_ok0")
        m.ta_psum = sem("ta_psum0")
        m.an_ok = sem("an_ok0")
        m.o_ok = sem("o_ok0")
        m.ss_ok = sem("ss_ok0")
        m.ms_ok = sem("ms_ok0")
        m.rms_ok = sem("rms_ok0")
        m.ot_psum = sem("ot_psum0")
        m.ot_evac = sem("ot_evac0")
        m.prod_ok = sem("prod_ok0")
        m.zeros = sem("zeros0")
        m.zeros_late = sem("zeros_late0")
        m.mhalf_ok = sem("mhalf_ok0")
        m.which_ok = sem("which_ok0")
        m.fold = sem("fold0")
        m.gate = sem("gate0")
        m.gate_d = sem("gate_d0")
        m.gate_e = sem("gate_e0")
        m.z_ok = sem("z_ok0")
        m.zt_psum = sem("zt_psum0")
        m.zt_evac = sem("zt_evac0")
        m.wf_psum = sem("wf_psum0")
        m.tanh_ok = sem("tanh_ok0")
        m.s_ok = sem("s_ok0")
        m.wf_gate = sem("wf_gate0")
        m.sg_ok = sem("sg_ok0")
        m.xr_load = sem("xr_load0")
        m.x1_ok = sem("x1_ok0")
        m.x1_stored_even = sem("x1_stored_even0")
        m.x1_stored_odd = sem("x1_stored_odd0")
        m.sp_passed = sem("sp_passed0")
        m.dve_passed = sem("dve_passed0")
        m.pool_passed = sem("pool_passed0")
        m.x1_stored = (m.x1_stored_even, m.x1_stored_odd)

        def x1_tile(b, t):
            return o[:, t, :] if isinstance(b, int) and b >= B - 1 else x1o[:, t % 2, :]

        def drained(kind, i, k):
            return {"XT": (m.xt_low, KC * i + k + 1), "PROJ": (m.qk_low, i + 1), "V": (m.vnew_ok, QT * i + k + 1),
                    "M": (m.m_evac, i + 1), "TD": (m.recip_ok, i + 1), "TA": (m.an_ok, QT * i + k + 1),
                    "OT": (m.ot_evac, KC * i + k + 1), "ZT": (m.zt_evac, i + 1),
                    "WF": (m.wf_gate, QT * i + k + 1)}[kind]

        LOADS = 11
        block = ctx.enter_context(nc.Block())

        @block.sync
        def _(sp):
            sp.dma_start(xb[:, :, :], io["x"][0].rearrange("(t p) c -> p t c", p=P)).then_inc(m.x_load, 16)
            for dst, src in (
                    (ident[:, :], io["ident"]), (wqk, io["wqk"].rearrange("(k p) h n -> p k h n", p=P)),
                    (wcat[:, :, :], io["wcat"].rearrange("(k p) n -> p k n", p=P)),
                    (wo[:, :, :], io["wo"].rearrange("(k p) n -> p k n", p=P)),
                    (normw[:, :], io["normw"]), (routed[:, :], io["routed"]),
                    (bo[:, :], io["bo"].partition_broadcast(P)), (dw[:, :], io["dw"].partition_broadcast(P)),
                    (rank8[:, :], io["rank8"].partition_broadcast(P)), (pick[:, :, :], io["pick"]),
                    (which[MROW:MROW + MROWS], io["which"])):
                sp.dma_start(dst, src).then_inc(m.w_load, 16)

            def park_parts(i):
                sp.wait_ge(m.qk_high, i + 1)
                stand_alone(sp, m.sp_passed)
                wait(sp, m.stacked, 128 * i)
                sp.dma_start(park[0], qk_h[:, :].bitcast(F32)).then_inc(m.parked, 16)
                sp.wait_ge(m.qk_low, i + 1)
                sp.dma_start(park[1], qk_l[:, :].bitcast(F32)).then_inc(m.parked, 16)

            def fill_stacks(i, slot):
                sp.wait_ge(m.parked, 32 * i + 32)
                for r in range(4):
                    for side, stack, part in ((0, qst, r // 2), (1, kst, r % 2)):
                        src = park[part, 64 * side:64 * side + 64, :].rearrange("(h f) q -> f h q", f=F0)
                        sp.dma_start(stack[slot][F0 * r:F0 * r + F0, :, :].bitcast(F32), src).then_inc(m.stacked, 16)

            def place_max(i, slot):
                sp.wait_ge(m.m_evac, i + 1)
                sp.dma_start(qst[slot][MROW:MROW + MROWS, :, :].bitcast(F32),
                             mrow[MROW:MROW + MROWS, :].bitcast(F32).unsqueeze(1).to_broadcast([MROWS, HG, S])
                             ).then_inc(m.m_placed, 16)

            def load_x(b):
                wait(sp, m.xn_ok, QT * b)
                stand_alone(sp, m.sp_passed)
                sp.dma_start(xb[:, :, :], io["x"][b].rearrange("(t p) c -> p t c", p=P)).then_inc(m.x_load, 16)

            def load_residual(b):
                wait(sp, m.x1_ok, QT * b)
                stand_alone(sp, m.sp_passed)
                sp.dma_start(xr[:, :, :], io["x"][b].rearrange("(t p) c -> p t c", p=P)).then_inc(m.xr_load, 16)

            def store_x1(b, t):
                sp.wait_ge(m.x1_ok, QT * b + t + 1)
                stand_alone(sp, m.sp_passed)
                sp.dma_start(x1_dram[t * P:(t + 1) * P, b, :], x1_tile(b, t)).then_inc(m.x1_stored[t % 2], 16)

            for i in range(3):
                park_parts(i)
                if i == 2:
                    place_max(0, 0)
                fill_stacks(i, i)

            def body(b):
                for hf, v_, kind, i, k in slots(b):
                    if kind == "START" and hf == 0:
                        if not (isinstance(b, int) and b >= B - 1):
                            load_x(b + 1)
                        if not (isinstance(b, int) and b < 1):
                            load_residual(b - 1)
                    if kind == "PROJ":
                        park_parts(i)
                        fill_stacks(i, k)
                    if kind == "M":
                        place_max(i, k)
                    if kind == "WF" and k < QT - 1:
                        store_x1(i, k)
                if not (isinstance(b, int) and b < 1):
                    store_x1(b - 1, QT - 1)

            def slots(b):
                out = [(0, -1, "START", 0, 0)]
                for (hf, v_), kind, i, k in layer0_jobs(b):
                    if kind == "PROJ":
                        k = (3, 0, 1, 2)[hf]
                    if kind == "M":
                        k = (1, 2, 3, 0)[hf]
                    out.append((hf, v_, kind, i, k))
                return out

            over_batches(sp, body, 2)
            load_residual(B - 1)
            sp.wait_ge(m.a_done, 16 * B)
            sp.wait_ge(m.d_done, len(D_PARTS) * B)
            sp.wait_ge(m.xt_psum, KC * B)
            shared.load_first(sp, io1)
            sp.wait_ge(m.ta_psum, QT * B)
            shared.load_last(sp, io1)
            for t in range(QT):
                store_x1(B - 1, t)
            for stored in m.x1_stored:
                sp.wait_ge(stored, 16 * B * QT // 2)

        @block.tensor
        def _(pe):
            pe.wait_ge(m.w_load, 16 * LOADS)

            def job(kind, i, k, bank):
                if kind == "XT":
                    pe.wait_ge(m.xn_ok, QT * (i + 1))
                    for t in range(QT):
                        mm = pe.transpose(bank[:, t * P:(t + 1) * P], xn[:, t, k * P:(k + 1) * P], ident[:, :])
                    mm.then_inc(m.xt_psum, 1)
                if kind == "PROJ":
                    hf = k
                    n = 0
                    for kc in range(KC):
                        for w, x in ((wqk_h, xt_h), (wqk_h, xt_l), (wqk_l, xt_h)):
                            mm = pe.matmul(bank[:, :], w[:, kc, hf, :], x[:, kc, :], start=(n == 0), stop=(n == 5))
                            n += 1
                    mm.then_inc(m.proj_psum, 1)
                if kind == "V":
                    if k == 0:
                        pe.wait_ge(m.xt_sum, i + 1)
                    for kc in range(KC):
                        mm = pe.matmul(bank[:, 0:WCAT], xt[:, kc, k * P:(k + 1) * P], wcat[:, kc, :],
                                       start=(kc == 0), stop=(kc == KC - 1))
                    mm.then_inc(m.v_psum, 1)
                if kind == "M":
                    pe.wait_ge(m.m_low, i + 1)
                    for c in range(QT):
                        mm = pe.matmul(bank[MROW:MROW + MROWS, c * P:(c + 1) * P],
                                       msplit[:, c, :, :].bitcast(F32).rearrange("p a h -> p (a h)"),
                                       ident[:, :], start=True, stop=True)
                    mm.then_inc(m.m_psum, 1)
                if kind == "TD":
                    pe.wait_ge(m.d_evac, i + 1)
                    for t in range(QT):
                        mm = pe.transpose(bank[:, t * P:(t + 1) * P], dt_[:, t * P:(t + 1) * P], ident[:, :])
                    mm.then_inc(m.td_psum, 1)
                if kind == "TA":
                    pe.wait_ge(m.a_evac, HALF * (i + 1))
                    for hf in range(HALF):
                        mm = pe.transpose(bank[:, hf * P:(hf + 1) * P], at[:, hf, k * P:(k + 1) * P], ident[:, :])
                    mm.then_inc(m.ta_psum, 1)
                if kind == "OT":
                    pe.wait_ge(m.o_ok, QT * (i + 1))
                    for t in range(QT):
                        mm = pe.transpose(bank[:, t * P:(t + 1) * P], o[:, t, k * P:(k + 1) * P], ident[:, :])
                    mm.then_inc(m.ot_psum, 1)
                if kind == "ZT":
                    pe.wait_ge(m.z_ok, i + 1)
                    for t in range(QT):
                        mm = pe.transpose(bank[:, t * P:(t + 1) * P], z[:, t, :, :].rearrange("p e r -> p (e r)"),
                                          ident[:, :])
                    mm.then_inc(m.zt_psum, 1)
                if kind == "WF":
                    for kc in range(KC):
                        pe.matmul(bank[:, 0:E], ot[:, kc, k * P:(k + 1) * P], wo[:, kc, :],
                                  start=(kc == 0), stop=(kc == KC - 1))
                    pe.matmul(bank[:, E:2 * E], zt[:, k * P:(k + 1) * P], routed[:, :],
                              start=True, stop=True).then_inc(m.wf_psum, 1)

            def score_max(n, w, slot, i):
                if w == 0:
                    pe.wait_ge(m.stacked, 128 * (i + 1))
                wait(pe, m.max_done, n - S_BACK[w] + 1)
                j, c = w // 4, w % 4
                pe.matmul(s_bank[S_BANK[w]][:, :], qst[slot][0:MROW, j, c * P:(c + 1) * P], kst[slot][0:MROW, j, :],
                          start=True, stop=True).then_inc(m.s_done, 1)

            def score_exp(g, w, slot, i):
                if w == 0:
                    pe.wait_ge(m.m_placed, 16 * (i + 1))
                wait(pe, m.exp_done, g - 1)
                c, j = w // 4, w % 4
                pe.matmul(t_bank[w % 2][:, :], kst[slot][0:MROW + MROWS, j, c * P:(c + 1) * P],
                          qst[slot][0:MROW + MROWS, j, :], start=True, stop=True).then_inc(m.t_done, 1)

            def value_step(b, hf, c):
                y = HALF * b + hf
                hg = hf // 2
                if c == 0:
                    wait(pe, m.a_evac, y)
                    if hf == 0:
                        pe.wait_ge(m.v_ok, b + 1)
                pe.wait_ge(m.exp_done, UNITS * y + 4 * c + 4)
                for h in range(HG):
                    mm = pe.matmul(a_bank[BLK * h:BLK * h + BLK, :],
                                   v[:, c, hg * P + h * DH0:hg * P + (h + 1) * DH0], probs[:, c, h, :],
                                   start=(c == 0), stop=(c == 3))
                mm.then_inc(m.a_done, 1)

            def denominators(b, d):
                hf, buf = D_PARTS[d]
                if d == 0:
                    wait(pe, m.d_evac, b)
                pe.wait_ge(m.sum_ok, SUMS * b + (3, 6, 9, 10, 11)[d])
                for h in range(HG):
                    mm = pe.matmul(d_bank[BLK * h:BLK * h + BLK, :], pick[:, hf, :], sums[:, buf, h, :],
                                   start=(d == 0), stop=(d == len(D_PARTS) - 1))
                mm.then_inc(m.d_done, 1)

            prev = None

            def side(kind, i, k):
                nonlocal prev
                wait(pe, *drained(*prev))
                job(kind, i, k, misc)
                prev = (kind, i, 0 if kind in ("PROJ", "M") else k)

            def done(n):
                kind, i, k = FIRST_JOBS[n]
                return drained(kind, i, k)

            def first_job(n):
                kind, i, k = FIRST_JOBS[n]
                if n >= len(first_banks):
                    pe.wait_ge(*done(n - len(first_banks)))
                if kind == "PROJ":
                    pe.wait_ge(m.wsplit, 2)
                    pe.wait_ge(m.xt_low, KC)
                job(kind, i, i if kind == "PROJ" else k, first_banks[n % len(first_banks)])

            for n in range(len(FIRST_JOBS) - 2):
                first_job(n)
            for n in range(LEAD):
                if n % UNITS == 0:
                    pe.wait_ge(m.zeros, 2 * (n // UNITS) + 2)
                score_max(n, n % UNITS, n // UNITS, n // UNITS)
                if n == UNITS - 1:
                    first_job(len(FIRST_JOBS) - 2)
                if n == UNITS + 2:
                    first_job(len(FIRST_JOBS) - 1)
            for n in range(len(FIRST_JOBS) - len(first_banks), len(FIRST_JOBS) - 1):
                pe.wait_ge(*done(n))
            pe.wait_ge(m.zeros_late, HALF)
            pe.wait_ge(m.which_ok, HALF)
            pe.wait_ge(m.fold, 5)
            prev = FIRST_JOBS[-1]

            def body(b):
                nonlocal prev
                last = isinstance(b, int) and b >= B - 1
                if not isinstance(b, int):
                    _, kind, i, k = layer0_jobs(b - 1)[-1]
                    prev = (kind, i, k)
                jobs = layer0_jobs(b)
                for hf in range(HALF):
                    for w in range(UNITS):
                        g = HALF * UNITS * b + UNITS * hf + w
                        score_exp(g, w, hf, HALF * b + hf)
                        ahead = hf * UNITS + w + LEAD
                        if not (last and ahead >= HALF * UNITS):
                            score_max(g + LEAD, ahead % UNITS, ahead // UNITS % HALF, HALF * b + ahead // UNITS)
                        if w % 4 == 3:
                            step = 4 * hf + w // 4 - LAG
                            if step >= 0:
                                value_step(b, step // 4, step % 4)
                            elif not (isinstance(b, int) and b < 1):
                                value_step(b - 1, (step + 16) // 4, (step + 16) % 4)
                        if w == SUM_STEP and hf:
                            denominators(b, hf - 1)
                        if hf == 0 and w in LATE_SUMS and not (isinstance(b, int) and b < 1):
                            denominators(b - 1, 3 + LATE_SUMS.index(w))
                        for (jh, jw), kind, i, k in jobs:
                            if (jh, jw) == (hf, w):
                                side(kind, i, (3, 0, 1, 2)[hf] if kind == "PROJ" else k)

            over_batches(pe, body, 2)
            for step in range(16 - LAG, 16):
                value_step(B - 1, step // 4, step % 4)
            denominators(B - 1, 3)
            denominators(B - 1, 4)
            wait(pe, *drained(*prev))
            pe.wait_ge(m.max_done, B * HALF * UNITS)
            pe.wait_ge(m.exp_done, B * HALF * UNITS)
            for n, (kind, i, k) in enumerate(LAST_JOBS):
                if n >= len(last_banks):
                    pe.wait_ge(*drained(*LAST_JOBS[n - len(last_banks)]))
                if kind == "WF" and k == 0:
                    pe.wait_ge(m.ot_evac, KC * B)
                    pe.wait_ge(m.zt_evac, B)
                job(kind, i, k, last_banks[n % len(last_banks)])

        @block.scalar
        def _(act):
            act.wait_ge(m.w_load, 16 * LOADS)
            act.activation(wqk_h[:, :, :, :], wqk, ACT.Copy).then_inc(m.wsplit, 1)

            def exp_tile(b, hf, w):
                g = HALF * UNITS * b + UNITS * hf + w
                act.wait_ge(m.t_done, g + 1)
                c, j = w // 4, w % 4
                if j == 0:
                    wait(act, m.a_done, 4 * (HALF * b + hf - 1) + c + 1)
                    if hf:
                        wait(act, m.sum_ok, SUMS * b + 3 * (hf - 1) + max(c, 1))
                    else:
                        wait(act, m.sum_ok, SUMS * (b - 1) + 10 + c // 2)
                act.activation(probs[:, c, j, :], t_bank[w % 2][:, :], ACT.Exp, scale=SCALE0).then_inc(m.exp_done, 1)

            def side(kind, i, k, bank=misc):
                if kind == "XT":
                    act.wait_ge(m.xt_psum, KC * i + k + 1)
                    if k == 0:
                        wait(act, m.proj_psum, 4 * i)
                        wait(act, m.xt_sum, i)
                    act.activation(xt_h[:, k, :], bank[:, :], ACT.Copy).then_inc(m.xt_high, 1)
                if kind == "PROJ":
                    act.wait_ge(m.proj_psum, i + 1)
                    wait(act, m.parked, 32 * i)
                    act.activation(qk_h[:, :], bank[:, :], ACT.Copy).then_inc(m.qk_high, 1)
                if kind == "V":
                    act.wait_ge(m.v_psum, QT * i + k + 1)
                    wait(act, m.lc_ok, i)
                    act.activation(vnew[:, k, :], bank[:, 0:WCAT], ACT.Copy).then_inc(m.vnew_ok, 1)
                if kind == "M":
                    act.wait_ge(m.m_psum, i + 1)
                    wait(act, m.m_placed, 16 * i)
                    act.activation(mrow[MROW:MROW + MROWS, :], bank[MROW:MROW + MROWS, :], ACT.Copy).then_inc(m.m_evac, 1)
                if kind == "DEV":
                    act.wait_ge(m.d_done, len(D_PARTS) * (i + 1))
                    wait(act, m.td_psum, i)
                    act.activation(dt_[:, :], d_bank[:, :], ACT.Copy).then_inc(m.d_evac, 1)
                if kind == "SQ":
                    act.wait_ge(m.o_ok, QT * i + k + 1)
                    if k == 0:
                        wait(act, m.ms_ok, i)
                        wait(act, m.wf_gate, QT * i)
                    act.activation(th[:, k, :], o[:, k, :], ACT.Square, accum_out=ss[:, k:k + 1]).then_inc(m.ss_ok, 1)
                if kind == "OT":
                    act.wait_ge(m.ot_psum, KC * i + k + 1)
                    wait(act, m.wf_psum, QT * i)
                    act.activation(ot[:, k, :], bank[:, :], ACT.Copy).then_inc(m.ot_evac, 1)
                if kind == "ZT":
                    act.wait_ge(m.zt_psum, i + 1)
                    act.activation(zt[:, :], bank[:, :], ACT.Copy).then_inc(m.zt_evac, 1)
                if kind == "WF":
                    act.wait_ge(m.wf_psum, QT * i + k + 1)
                    if k == 0:
                        act.wait_ge(m.ss_ok, QT * (i + 1))
                    act.activation(th[:, k, :], bank[:, E:2 * E], ACT.Tanh).then_inc(m.tanh_ok, 1)
                if kind == "GEXP":
                    act.wait_ge(m.gate_d, i + 1)
                    act.activation(gs[:, 5, :], gs[:, 4, :], ACT.Exp).then_inc(m.gate_e, 1)

            for n, (kind, i, k) in enumerate(FIRST_JOBS):
                side(kind, i, k, first_banks[n % len(first_banks)])
                if (kind, k) == ("V", 1):
                    for slot in range(HALF):
                        act.activation(kst[slot][MROW:MROW + MROWS, :, :], which[MROW:MROW + MROWS],
                                       ACT.Copy).then_inc(m.which_ok, 1)
                    act.wait_ge(m.which_ok, HALF)

            def body(b):
                first = isinstance(b, int) and b < 1
                jobs = layer0_jobs(b)
                for hf in range(HALF):
                    for w in range(UNITS):
                        exp_tile(b, hf, w)
                        if w == EVAC_STEP:
                            if hf:
                                act.wait_ge(m.a_done, 4 * (HALF * b + hf))
                                if hf == 1:
                                    wait(act, m.ta_psum, QT * b)
                                act.activation(at[:, hf - 1, :], a_bank[:, :], ACT.Copy).then_inc(m.a_evac, 1)
                            elif not first:
                                act.wait_ge(m.a_done, 16 * b)
                                act.activation(at[:, 3, :], a_bank[:, :], ACT.Copy).then_inc(m.a_evac, 1)
                        if (hf, w) == (0, 9) and not first:
                            side("DEV", b - 1, 0)
                        if hf == 2 and w == 2:
                            side("GEXP", b, 0)
                        for (jh, jw), kind, i, k in jobs:
                            if (jh, jw) == (hf, w):
                                side(kind, i, k)
                        if not first and hf == 1 and w in (3, 5, 7, 9):
                            side("SQ", b - 1, (w - 3) // 2)

            over_batches(act, body, 2)
            act.wait_ge(m.a_done, 16 * B)
            act.activation(at[:, 3, :], a_bank[:, :], ACT.Copy).then_inc(m.a_evac, 1)
            side("DEV", B - 1, 0)
            for n, (kind, i, k) in enumerate(LAST_JOBS):
                side(kind, i, k, last_banks[n % len(last_banks)])
                if kind == "TA":
                    side("SQ", i, k)

        @block.vector
        def _(dve):
            dve.memset(mhalf[:, :], -0.5).then_inc(m.mhalf_ok, 1)

            def norm_stats(b, tiles):
                dve.wait_ge(m.x_load, 16 * (b + 1))
                for t in tiles:
                    dve.bn_stats(stat[:, t, :], xb[:, t, :]).then_inc(m.stats, 1)

            def norm_ends(b):
                dve.wait_ge(m.stats, QT * (b + 1))
                wait(dve, m.veps_ok, b)
                stand_alone(dve, m.dve_passed)
                for t in range(QT):
                    dve.bn_aggr(mv[:, t, :], stat[:, t, :]).then_inc(m.aggr, 1)

            def normalise(b, tiles):
                dve.wait_ge(m.rstd_ok, b + 1)
                wait(dve, m.xt_psum, KC * b)
                for t in tiles:
                    ins = dve.tensor_scalar(xn[:, t, :], xb[:, t, :], mv[:, t, 0:1], rstd[:, t:t + 1],
                                            ALU.subtract, ALU.mult)
                    ins.then_inc(m.xn_ok, 1)

            def zero_rows(i):
                dve.memset(qst[i][STACK:MROW, :, :].bitcast(F32), 0.0).then_inc(m.zeros, 1)
                dve.memset(kst[i][STACK:MROW, :, :].bitcast(F32), 0.0).then_inc(m.zeros, 1)

            norm_stats(0, range(QT))
            norm_ends(0)
            dve.wait_ge(m.w_load, 16 * LOADS)
            dve.wait_ge(m.wsplit, 1)
            dve.tensor_tensor(wqk_l[:, :, :, :], wqk, wqk_h[:, :, :, :].bitcast(F32),
                              ALU.subtract).then_inc(m.wsplit, 1)
            normalise(0, range(QT))
            dve.tensor_scalar(one_dw[:, :], dw[:, :], -1.0, 1.0, ALU.mult, ALU.add).then_inc(m.fold, 1)
            dve.tensor_scalar(neg_dw[:, :], dw[:, :], -1.0, None, ALU.mult).then_inc(m.fold, 1)
            dve.wait_ge(m.fold, 2)
            for kc in range(KC):
                dve.tensor_scalar(wo[:, kc, :], wo[:, kc, :], normw[:, kc:kc + 1], one_dw[:, 0:1], ALU.mult,
                                  ALU.mult).then_inc(m.fold, 1)
            dve.tensor_scalar(bo[:, :], bo[:, :], one_dw[:, 0:1], None, ALU.mult).then_inc(m.fold, 1)

            def max_tile(n, w, i_par):
                dve.wait_ge(m.s_done, n + 1)
                j, c = w // 4, w % 4
                dve.tensor_reduce(negmax[:, i_par, c, j:j + 1], s_bank[S_BANK[w]][:, :], X, ALU.max,
                                  negate=True).then_inc(m.max_done, 1)

            def side(kind, i, k, bank=misc):
                if kind == "XT":
                    dve.wait_ge(m.xt_high, KC * i + k + 1)
                    dve.tensor_tensor(xt_l[:, k, :], bank[:, :], xt_h[:, k, :].bitcast(F32),
                                      ALU.subtract).then_inc(m.xt_low, 1)
                if kind == "PROJ":
                    dve.wait_ge(m.qk_high, i + 1)
                    wait(dve, m.parked, 32 * i)
                    dve.tensor_tensor(qk_l[:, :], bank[:, :], qk_h[:, :].bitcast(F32), ALU.subtract).then_inc(m.qk_low, 1)
                if kind == "MS":
                    dve.wait_ge(m.max_done, UNITS * (i + 1))
                    wait(dve, m.m_psum, i)
                    dve.tensor_copy(msplit[:, :, 0, :], negmax[:, k, :, :]).then_inc(m.m_high, 1)
                    dve.wait_ge(m.m_high, i + 1)
                    dve.tensor_tensor(msplit[:, :, 1, :], negmax[:, k, :, :], msplit[:, :, 0, :].bitcast(F32),
                                      ALU.subtract).then_inc(m.m_low, 1)
                if kind == "VCOPY":
                    dve.wait_ge(m.vnew_ok, QT * (i + 1))
                    wait(dve, m.a_done, 16 * i)
                    dve.tensor_copy(v[:, :, :], vnew[:, :, 0:E]).then_inc(m.v_ok, 1)
                    dve.tensor_copy(lc[:, :, :], vnew[:, :, E:WCAT]).then_inc(m.lc_ok, 1)
                if kind == "TD":
                    dve.wait_ge(m.td_psum, i + 1)
                    dve.reciprocal(rec[:, :, :, :].rearrange("p t s h -> p t h s"),
                                   bank[:, :].rearrange("p (t h s) -> p t h s", t=QT, h=HG)[:, :, :, 0:HALF]
                                   ).then_inc(m.recip_ok, 1)
                    dve.wait_ge(m.recip_ok, i + 1)
                    for hg in range(2):
                        one = rec[:, :, 2 * hg + 1, :]
                        ins = dve.tensor_scalar(one, one, neg_dw[:, 0:1], None, ALU.mult)
                    ins.then_inc(m.rec_ok, 1)
                if kind == "TA":
                    dve.wait_ge(m.rec_ok, i + 1)
                    dve.wait_ge(m.ta_psum, QT * i + k + 1)
                    wait(dve, m.o_ok, QT * i + k)
                    if k == 0:
                        wait(dve, m.ot_psum, KC * i)
                        wait(dve, m.ss_ok, QT * i)
                    dve.tensor_tensor(an[:, :, :, :], bank[:, :].rearrange("p (s h e) -> p s h e", s=HALF, h=HG),
                                      rec[:, k, :, :].unsqueeze(3).to_broadcast([P, HALF, HG, DH0]),
                                      ALU.mult).then_inc(m.an_ok, 1)
                    dve.wait_ge(m.an_ok, QT * i + k + 1)
                    maps = an[:, :, :, :].rearrange("p (g i) h e -> p g i (h e)", g=2)
                    dve.tensor_tensor(o[:, k, :].rearrange("p (g n) -> p g n", g=2), maps[:, :, 0, :],
                                      maps[:, :, 1, :], ALU.add).then_inc(m.o_ok, 1)
                if kind == "WF":
                    dve.wait_ge(m.tanh_ok, QT * i + k + 1)
                    dve.wait_ge(m.rms_ok, i + 1)
                    wait(dve, m.x1_ok, QT * (i - 1) + k + 1)
                    dve.scalar_tensor_tensor(s_[:, k, :], bank[:, 0:E], rms[:, k:k + 1], bo[:, :],
                                             op0=ALU.mult, op1=ALU.add).then_inc(m.s_ok, 1)
                    dve.scalar_tensor_tensor(g_[:, k, :], th[:, k, :], 1.0, bank[:, E:2 * E],
                                             op0=ALU.add, op1=ALU.mult).then_inc(m.wf_gate, 1)

            GATES = 17

            def wide(k):
                return gs[:, k, :].unsqueeze(2).to_broadcast([P, QT, NE])

            def gate(b):
                lg = lc[:, :, 0:NE]
                w8 = rank8[:, :].unsqueeze(1).to_broadcast([P, QT, NE])
                n = GATES * b
                dve.wait_ge(m.lc_ok, b + 1)
                wait(dve, m.z_ok, b)
                for src, top, num, hot in ((lg, 0, 1, 1), (gt[:, 2, :, :], 2, 3, 3)):
                    dve.tensor_reduce(gs[:, top, :], src, X, ALU.max).then_inc(m.gate, 1)
                    dve.wait_ge(m.gate, n + 1)
                    dve.tensor_tensor(gt[:, 0, :, :], src, wide(top), ALU.is_equal).then_inc(m.gate, 1)
                    dve.wait_ge(m.gate, n + 2)
                    dve.tensor_tensor(gt[:, 0, :, :], gt[:, 0, :, :], w8, ALU.mult).then_inc(m.gate, 1)
                    dve.wait_ge(m.gate, n + 3)
                    dve.tensor_reduce(gs[:, num, :], gt[:, 0, :, :], X, ALU.max).then_inc(m.gate, 1)
                    dve.wait_ge(m.gate, n + 4)
                    dve.tensor_tensor(gt[:, hot, :, :], gt[:, 0, :, :], wide(num), ALU.is_equal).then_inc(m.gate, 1)
                    dve.wait_ge(m.gate, n + 5)
                    n = n + 5
                    if top == 0:
                        dve.scalar_tensor_tensor(gt[:, 2, :, :], gt[:, 1, :, :], -3e38, lg,
                                                 op0=ALU.mult, op1=ALU.add).then_inc(m.gate, 1)
                        dve.wait_ge(m.gate, n + 1)
                        n = n + 1
                dve.tensor_tensor(gs[:, 4, :], gs[:, 2, :], gs[:, 0, :], ALU.subtract).then_inc(m.gate_d, 1)

            def gate_end(b):
                n = GATES * b + 11
                dve.wait_ge(m.gate_e, b + 1)
                dve.tensor_scalar(gs[:, 6, :], gs[:, 5, :], 1.0, None, ALU.add).then_inc(m.gate, 1)
                dve.wait_ge(m.gate, n + 1)
                dve.reciprocal(gs[:, 7, :], gs[:, 6, :]).then_inc(m.gate, 1)
                dve.wait_ge(m.gate, n + 2)
                dve.tensor_tensor(gs[:, 6, :], gs[:, 5, :], gs[:, 7, :], ALU.mult).then_inc(m.gate, 1)
                dve.tensor_tensor(gt[:, 4, :, :], gt[:, 1, :, :], wide(7), ALU.mult).then_inc(m.gate, 1)
                dve.wait_ge(m.gate, n + 4)
                dve.tensor_tensor(gt[:, 5, :, :], gt[:, 3, :, :], wide(6), ALU.mult).then_inc(m.gate, 1)
                dve.wait_ge(m.gate, n + 5)
                dve.tensor_tensor(gt[:, 6, :, :], gt[:, 4, :, :], gt[:, 5, :, :], ALU.add).then_inc(m.gate, 1)

            def gated(b):
                dve.wait_ge(m.gate, GATES * (b + 1))
                wait(dve, m.zt_psum, b)
                for t in range(QT):
                    ins = dve.tensor_tensor(z[:, t, :, :], gt[:, 6, t, :].unsqueeze(2).to_broadcast([P, NE, R]),
                                            lc[:, t, NE:NE + R].unsqueeze(1).to_broadcast([P, NE, R]), ALU.mult)
                ins.then_inc(m.z_ok, 1)

            for n, (kind, i, k) in enumerate(FIRST_JOBS):
                if kind in ("XT", "PROJ") and i < 2:
                    side(kind, i, k, first_banks[n % len(first_banks)])
                if kind == "PROJ" and i < 2:
                    zero_rows(i)
            for n in range(LEAD):
                max_tile(n, n % UNITS, n // UNITS % 2)
                if n == UNITS - 1:
                    side("MS", 0, 0)
                    side("PROJ", 2, 0, first_banks[(len(FIRST_JOBS) - 2) % len(first_banks)])

            def body(b):
                first = isinstance(b, int) and b < 1
                last = isinstance(b, int) and b >= B - 1
                jobs = layer0_jobs(b)
                for hf in range(HALF):
                    for w in range(UNITS):
                        ahead = hf * UNITS + w + LEAD
                        if not (last and ahead >= HALF * UNITS):
                            max_tile(HALF * UNITS * b + ahead, ahead % UNITS, ahead // UNITS % 2)
                        if w == 7 and not (last and hf == 3):
                            side("MS", HALF * b + hf + 1, (hf + 1) % 2)
                        if not last:
                            for n in range(2):
                                if (hf, w) == STATS[n]:
                                    norm_stats(b + 1, (2 * n, 2 * n + 1))
                                if (hf, w) == NORMS[n]:
                                    normalise(b + 1, (2 * n, 2 * n + 1))
                            if (hf, w) == NORM_ENDS:
                                norm_ends(b + 1)
                        if (hf, w) == VALUES_COPY:
                            side("VCOPY", b, 0)
                        if (hf, w) == GATE:
                            gate(b)
                        if (hf, w) == GATE_END:
                            gate_end(b)
                        if (hf, w) == GATED:
                            gated(b)
                        for (jh, jw), kind, i, k in jobs:
                            if (jh, jw) == (hf, w):
                                side(kind, i, k)

            over_batches(dve, body, 2)
            for n, (kind, i, k) in enumerate(LAST_JOBS):
                if (kind, k) == ("WF", 0):
                    shared.less_turns(dve, 0)
                side(kind, i, k, last_banks[n % len(last_banks)])
            shared.less_turns(dve, 1)

        @block.gpsimd
        def _(pool):
            def rstd_of(b):
                pool.wait_ge(m.aggr, QT * (b + 1))
                wait(pool, m.xn_ok, QT * b)
                stand_alone(pool, m.pool_passed)
                pool.tensor_scalar(veps[:, :], mv[:, :, 1], LN_EPS, None, ALU.add).then_inc(m.veps_ok, 1)
                pool.wait_ge(m.veps_ok, b + 1)
                pool.tensor_tensor(rstd[:, :], veps[:, :], mhalf[:, :], ALU.pow).then_inc(m.rstd_ok, 1)

            def add_chunk(b, hf, c):
                pool.wait_ge(m.exp_done, UNITS * (HALF * b + hf) + HG * (c + 1))
                if c == 1:
                    wait(pool, m.d_done, len(D_PARTS) * b + max(hf - 1, 0))
                else:
                    pool.wait_ge(m.sum_ok, SUMS * b + 3 * hf + c - 1)
                before = probs[:, 0, :, :] if c == 1 else sums[:, hf % 2, :, :]
                pool.tensor_tensor(sums[:, hf % 2, :, :], before, probs[:, c, :, :], ALU.add).then_inc(m.sum_ok, 1)

            def add_pair(b, c2):
                pool.wait_ge(m.exp_done, UNITS * (HALF * b + 3) + 8 * (c2 + 1))
                pool.wait_ge(m.d_done, len(D_PARTS) * b + 2 + c2)
                pool.tensor_tensor(sums[:, 1 - c2, :, :], probs[:, 2 * c2, :, :], probs[:, 2 * c2 + 1, :, :],
                                   ALU.add).then_inc(m.sum_ok, 1)

            def add_parts(b):
                pool.wait_ge(m.xt_low, KC * (b + 1))
                wait(pool, m.v_psum, QT * b)
                pool.tensor_tensor(xt[:, :, :], xt_h[:, :, :].bitcast(F32), xt_l[:, :, :].bitcast(F32),
                                   ALU.add).then_inc(m.xt_sum, 1)

            def rms_of(b):
                pool.wait_ge(m.ss_ok, QT * (b + 1))
                wait(pool, m.wf_gate, QT * b)
                stand_alone(pool, m.pool_passed)
                pool.tensor_scalar(ms[:, :], ss[:, :], 1.0 / E, EPS32, ALU.mult, ALU.add).then_inc(m.ms_ok, 1)
                pool.wait_ge(m.ms_ok, b + 1)
                pool.tensor_tensor(rms[:, :], ms[:, :], mhalf[:, :], ALU.pow).then_inc(m.rms_ok, 1)

            def residual(b, k):
                pool.wait_ge(m.wf_gate, QT * b + k + 1)
                pool.tensor_tensor(g_[:, k, :], s_[:, k, :], g_[:, k, :], ALU.mult).then_inc(m.prod_ok, 1)
                pool.wait_ge(m.prod_ok, QT * b + k + 1)
                if k == 0:
                    pool.wait_ge(m.xr_load, 16 * (b + 1))
                if not (isinstance(b, int) and b >= B - 1):
                    wait(pool, m.x1_stored[k % 2], 16 * (QT // 2 * b + k // 2))
                pool.tensor_tensor(x1_tile(b, k), xr[:, k, :], g_[:, k, :], ALU.add).then_inc(m.x1_ok, 1)

            pool.wait_ge(m.mhalf_ok, 1)
            pool.wait_ge(m.x_load, 16)
            rstd_of(0)
            pool.wait_ge(m.rstd_ok, 1)
            for n in range(HALF):
                stack = (qst, kst)[n % 2][2 + n // 2]
                pool.memset(stack[STACK:MROW, :, :].bitcast(F32), 0.0).then_inc(m.zeros_late, 1)
                pool.wait_ge(m.zeros_late, n + 1)
                if n == 1:
                    add_parts(0)
                    pool.wait_ge(m.xt_sum, 1)

            def body(b):
                first = isinstance(b, int) and b < 1
                last = isinstance(b, int) and b >= B - 1
                if not first:
                    add_pair(b - 1, 1)
                if not last:
                    rstd_of(b + 1)
                for hf in range(HALF - 1):
                    for c in range(1, 4):
                        add_chunk(b, hf, c)
                        if (hf, c) == (1, 1) and not last:
                            add_parts(b + 1)
                        if (hf, c) == (1, 2) and not first:
                            rms_of(b - 1)
                        if (hf, c) == (2, 2) and not first:
                            residual(b - 1, 0)
                        if (hf, c) == (2, 3) and not first:
                            for k in range(1, QT):
                                residual(b - 1, k)
                add_pair(b, 0)

            over_batches(pool, body, 2)
            add_pair(B - 1, 1)
            rms_of(B - 1)
            for k in range(QT):
                residual(B - 1, k)


def layer1_steps():
    steps = [("V", k) for k in range(2 * TT)] + [("Q", 0), ("K", 0)]
    for hp in range(HP):
        if hp + 1 < HP:
            steps += [("Q", hp + 1), ("K", hp + 1)]
        else:
            steps += [("F", 0)]
        steps += [("S", hp)]
        if hp >= 2:
            steps += [("AV", hp - 2)]
    return steps + [("F", 1), ("F", 2), ("AV", HP - 2), ("F", 3), ("AV", HP - 1)]


W_ORDER = (1, 2, 0, 3)
W_DONE = {t: n + 1 for n, t in enumerate(W_ORDER)}


def layer1(nc, io, shared, x1_dram, out):
    with ExitStack() as ctx:
        def sb(name, shape, dt=F32):
            return ctx.enter_context(nc.sbuf_tensor(name, shape, dt))

        def banks(name, n=1):
            return ctx.enter_context(nc.psum_tensor(name, [P, n, 512], F32))

        def sem(name):
            return ctx.enter_context(nc.semaphore(name))

        W3 = 3 * H1 * D1
        win_h, win_l = sb("win_h", [P, KC, W3], F32R), sb("win_l", [P, KC, W3], F32R)
        cs_h, cs_l = sb("cs_h", [P, KC, 2 * E], F32R), sb("cs_l", [P, KC, 2 * E], F32R)
        wout = shared.wout
        gk = sb("gk", [P, KC, H1, NREL])
        ud = sb("ud", [P, E])
        beta = sb("beta", [P, H1, NREL])
        bqkv, bout = shared.bqkv, sb("bout", [P, E])
        ident, apart, own, kdx = shared.ident, shared.apart, shared.own, shared.kdx
        mhalf, halfpi = sb("mhalf1", [P, TT]), sb("halfpi", [P, 1])
        work = shared.work
        v = work[:, 0:TT * H1 * D1].rearrange("p (t n) -> p t n", t=TT)
        rm = work[:, TT * H1 * D1:].rearrange("p (h t k) -> p h t k", t=TT, h=H1)
        xb, xn, xr = sb("xb1", [P, TT, E]), sb("xn1", [P, TT, E]), sb("xr1", [P, TT, E])
        stat, mv = sb("stat1", [P, TT, 6]), sb("mv1", [P, TT, 2])
        veps, rstd = sb("veps1", [P, TT]), sb("rstd1", [P, TT])
        xt = sb("xt1", [P, KC, TOK])
        xt_h, xt_l = sb("xt_h1", [P, KC, TOK], F32R), sb("xt_l1", [P, KC, TOK], F32R)
        qt, kt = sb("qt", [P, 2, TOK]), shared.kt
        sc, ex = sb("sc", [P, 2, 2, TT, BLK]), sb("ex", [P, 2, 2, TT, BLK])
        mx, sm, rc = sb("mx", [P, 2, 2, TT]), sb("sm", [P, 2, 2, TT]), sb("rc", [P, 2, 2, TT])
        ec = sb("ec", [P, 2, 2, TT, NREL])
        pt = [sb(f"pt{i}", [P, 2, TT, P]) for i in range(2)]
        ot = shared.ot
        r15, rt = sb("r15", [P, H1, TT, 2 * NREL - 1]), sb("rt", [P, H1, TT, NREL])
        p15, pc = sb("p15", [P, H1, TT, 2 * NREL - 1]), sb("pc", [P, H1, TT, NREL])
        pd = sb("pd", [P, TT, H1, NREL])
        pdt = sb("pdt", [P, TOK])
        sq, q2, th = shared.sq, shared.q2, shared.th
        so = sb("so", [P, 2, E])
        wqn, vdx, kdb, ones = shared.wqn, shared.vdx, shared.kdb, shared.ones
        ang, turns, noise = shared.ang, shared.turns, shared.noise
        w_in = work.rearrange("p (k n) -> p k n", k=KC)
        cs = xr[:, :, :].rearrange("p (k a) n -> p k (a n)", k=KC)

        pr = banks("pr", 2)
        s_ps = banks("s_ps", 2)
        o_ps = banks("o_ps", 2)
        misc = banks("misc1")[:, 0, :]
        fin = banks("fin")[:, 0, :]

        m = Semaphores()
        m.w_high = sem("w_high1")
        m.w_low = sem("w_low1")
        m.w_load, m.b_load, m.theta_load = shared.w_load, shared.b_load, shared.theta_load
        m.bout_load = sem("bout_load1")
        m.trig = shared.trig
        m.sin_ok = sem("sin_ok1")
        m.cs_high = sem("cs_high1")
        m.cs_low = sem("cs_low1")
        m.zero_pt = sem("zero_pt1")
        m.consts_ok = sem("consts_ok1")
        m.kdb_ok = sem("kdb_ok1")
        m.g_psum = sem("g_psum1")
        m.g_ok = sem("g_ok1")
        m.x_load = sem("x_load1")
        m.stats = sem("stats1")
        m.aggr = sem("aggr1")
        m.veps_ok = sem("veps_ok1")
        m.rstd_ok = sem("rstd_ok1")
        m.xn_ok = sem("xn_ok1")
        m.xt_psum = sem("xt_psum1")
        m.xt_high = sem("xt_high1")
        m.xt_low = sem("xt_low1")
        m.r_psum = sem("r_psum1")
        m.r_evac = sem("r_evac1")
        m.r_flip = sem("r_flip1")
        m.r_sum = sem("r_sum1")
        m.rm_ok = sem("rm_ok1")
        m.v_psum = sem("v_psum1")
        m.v_ok = sem("v_ok1")
        m.qk_psum = sem("qk_psum1")
        m.qk_ok = sem("qk_ok1")
        m.s_psum = sem("s_psum1")
        m.sc_ok = sem("sc_ok1")
        m.mx_ok = sem("mx_ok1")
        m.sub_ok = sem("sub_ok1")
        m.ex_ok = sem("ex_ok1")
        m.ec_ok = sem("ec_ok1")
        m.sm_ok = sem("sm_ok1")
        m.rc_ok = sem("rc_ok1")
        m.pc_ok = sem("pc_ok1")
        m.p_ok = sem("p_ok1")
        m.pt_ok = sem("pt_ok1")
        m.o_psum = sem("o_psum1")
        m.ot_ok = sem("ot_ok1")
        m.f_psum = sem("f_psum1")
        m.sq_ok = sem("sq_ok1")
        m.q2_ok = sem("q2_ok1")
        m.sqrt_ok = sem("sqrt_ok1")
        m.tanh_ok = sem("tanh_ok1")
        m.gate_ok = sem("gate_ok1")
        m.p15_zero = sem("p15_zero1")
        m.p15_sum = sem("p15_sum1")
        m.pd_ok = sem("pd_ok1")
        m.pd_psum = sem("pd_psum1")
        m.pdt_ok = sem("pdt_ok1")
        m.w_psum = sem("w_psum1")
        m.so_ok = sem("so_ok1")
        m.sg_ok = sem("sg_ok1")
        m.xr_load = sem("xr_load1")
        m.x2_ok = sem("x2_ok1")
        m.stored_even = sem("stored_even1")
        m.stored_odd = sem("stored_odd1")
        m.sp_passed = sem("sp_passed1")
        m.dve_passed = sem("dve_passed1")
        m.pool_passed = sem("pool_passed1")
        m.pe_passed = sem("pe_passed1")
        m.stored = (m.stored_even, m.stored_odd)

        def drained(kind, i, k):
            return {"V": (m.v_ok, 2 * TT * i + k + 1), "Q": (m.qk_ok, 2 * HP * i + 2 * k + 1),
                    "K": (m.qk_ok, 2 * HP * i + 2 * k + 2), "F": (m.sq_ok, TT * i + k + 1),
                    "W": (m.so_ok, TT * i + W_DONE.get(k, 0)), "R": (m.r_evac, i + 1), "XT": (m.xt_low, KC * i + k + 1),
                    "PD": (m.pdt_ok, i + 1)}[kind]

        steps = layer1_steps()
        through_pr = [x for x in steps if x[0] in "VQKF"] + [("W", 1), ("W", 2)]
        assert len(through_pr) % 2 == 0
        BLOADS, TLOADS = shared.B_LOADS, shared.THETA_LOADS

        block = ctx.enter_context(nc.Block())

        @block.sync
        def _(sp):
            def rows(i):
                return x1_dram.rearrange("n s c -> (n s) c").rearrange("(i t p) c -> i p t c", t=TT, p=P)[i]

            def load_x(i):
                wait(sp, m.xn_ok, i)
                stand_alone(sp, m.sp_passed)
                sp.dma_start(xb[:, :, :], rows(i)).then_inc(m.x_load, 16)

            load_x(0)
            sp.dma_start(bout[:, :], io["bout"].partition_broadcast(P)).then_inc(m.bout_load, 16)

            def body(i):
                if isinstance(i, int) and i == 0:
                    sp.wait_ge(m.cs_low, 1)
                wait(sp, m.x2_ok, TT * i)
                stand_alone(sp, m.sp_passed)
                sp.dma_start(xr[:, :, :], rows(i)).then_inc(m.xr_load, 16)
                if not (isinstance(i, int) and i >= NT1 - 1):
                    load_x(i + 1)
                o_rows = out.rearrange("n s c -> (n s) c").rearrange("(i t p) c -> i t p c", t=TT, p=P)
                for t in range(TT):
                    sp.wait_ge(m.x2_ok, TT * i + t + 1)
                    stand_alone(sp, m.sp_passed)
                    sp.dma_start(o_rows[i, W_ORDER[t]], so[:, t % 2, :]).then_inc(m.stored[t % 2], 16)

            over_batches(sp, body)
            for stored in m.stored:
                sp.wait_ge(stored, 16 * NT1 * TT // 2)

        @block.tensor
        def _(pe):
            prev_misc = [None]

            def misc_free():
                if prev_misc[0] is not None:
                    wait(pe, *drained(*prev_misc[0]))

            def three(dst, w_h, w_l, x_h, x_l, inc):
                n = 0
                for kc in range(KC):
                    for a, b in ((w_h, x_h), (w_h, x_l), (w_l, x_h)):
                        mm = pe.matmul(dst, a(kc), b(kc), start=(n == 0), stop=(n == 3 * KC - 1))
                        n += 1
                mm.then_inc(inc, 1)

            def transposes(i, kc, bank=misc):
                pe.wait_ge(m.xn_ok, i + 1)
                if bank is misc:
                    misc_free()
                for t in range(TT):
                    mm = pe.transpose(bank[:, t * P:(t + 1) * P], xn[:, t, kc * P:(kc + 1) * P], ident[:, :])
                mm.then_inc(m.xt_psum, 1)
                if bank is misc:
                    prev_misc[0] = ("XT", i, kc)

            def free_pr(i, kind, k):
                n = through_pr.index((kind, k))
                if n >= 2:
                    wait(pe, *drained(through_pr[n - 2][0], i, through_pr[n - 2][1]))
                elif not (isinstance(i, int) and i < 1):
                    wait(pe, *drained(through_pr[n - 2][0], i - 1, through_pr[n - 2][1]))
                return pr[:, n % 2, :]

            pe.wait_ge(m.b_load, 16 * BLOADS)
            for hp in range(HP):
                for kc in range(KC):
                    pe.matmul(o_ps[:, 0, kc * P + 2 * NREL * hp:kc * P + 2 * NREL * (hp + 1)],
                              wqn[:, hp, kc * P:(kc + 1) * P], kdx[:, :, :].rearrange("p a b -> p (a b)"),
                              start=True, stop=True)
            for kc in range(KC):
                transposes(0, kc, (misc, fin)[kc])
            pe.wait_ge(m.kdb_ok, HP)
            for hp in range(HP):
                mm = pe.matmul(o_ps[:, 1, 2 * NREL * hp:2 * NREL * (hp + 1)], ones, kdb[:, hp, :],
                               start=True, stop=True)
            mm.then_inc(m.g_psum, 1)
            pe.wait_ge(m.g_ok, 2)
            pe.wait_ge(m.w_low, 1)
            pe.wait_ge(m.zero_pt, 2)

            def body(i):
                last = isinstance(i, int) and i >= NT1 - 1
                if not isinstance(i, int):
                    prev_misc[0] = ("PD", i - 1, 0)
                misc_free()
                pe.wait_ge(m.xt_low, KC * (i + 1))
                for t in range(TT):
                    for kc in range(KC):
                        mm = pe.matmul(misc[:, t * P:(t + 1) * P], xt[:, kc, t * P:(t + 1) * P],
                                       gk[:, kc, :, :].rearrange("p h r -> p (h r)"), start=(kc == 0), stop=(kc == KC - 1))
                mm.then_inc(m.r_psum, 1)
                prev_misc[0] = ("R", i, 0)

                for kind, k in steps:
                    if isinstance(i, int) and i == 0 and (kind, k) == ("Q", 0):
                        pe.wait_ge(m.w_low, 3)
                        for hp in range(HP):
                            mm = pe.matmul(fin[:, 0:E], vdx[:, hp, :], wout[:, hp, :], start=(hp == 0), stop=(hp == HP - 1))
                        mm.then_inc(m.g_psum, 1)
                    if isinstance(i, int) and i == 0 and (kind, k) == ("F", 0):
                        pe.wait_ge(m.cs_low, 1)
                    if kind == "V":
                        t, half = k // 2, k % 2
                        c = 2 * H1 * D1 + 512 * half
                        three(free_pr(i, kind, k),
                              lambda kc: xt_h[:, kc, t * P:(t + 1) * P], lambda kc: xt_l[:, kc, t * P:(t + 1) * P],
                              lambda kc: win_h[:, kc, c:c + 512], lambda kc: win_l[:, kc, c:c + 512], m.v_psum)
                    if kind in ("Q", "K"):
                        c = H1 * D1 * (kind == "K") + P * k
                        three(free_pr(i, kind, k),
                              lambda kc: win_h[:, kc, c:c + P], lambda kc: win_l[:, kc, c:c + P],
                              lambda kc: xt_h[:, kc, :], lambda kc: xt_l[:, kc, :], m.qk_psum)
                    if kind == "F":
                        three(free_pr(i, kind, k),
                              lambda kc: xt_h[:, kc, k * P:(k + 1) * P], lambda kc: xt_l[:, kc, k * P:(k + 1) * P],
                              lambda kc: cs_h[:, kc, :], lambda kc: cs_l[:, kc, :], m.f_psum)
                    if kind == "S":
                        pe.wait_ge(m.qk_ok, 2 * HP * i + 2 * k + 2)
                        wait(pe, m.sc_ok, HP * i + k)
                        stand_alone(pe, m.pe_passed)
                        for blk in range(NBLK):
                            q, t = blk % 4, blk // 4
                            for h in range(2):
                                mm = pe.matmul(s_ps[BLK * q:BLK * (q + 1), h, BLK * t:BLK * (t + 1)],
                                               qt[D1 * h:D1 * (h + 1), k % 2, BLK * blk:BLK * (blk + 1)],
                                               kt[D1 * h:D1 * (h + 1), k % 2, BLK * blk:BLK * (blk + 1)],
                                               start=True, stop=True)
                        mm.then_inc(m.s_psum, 1)
                    if kind == "AV":
                        pe.wait_ge(m.pt_ok, 4 * (HP * i + k + 1))
                        if k == 0:
                            pe.wait_ge(m.v_ok, 2 * TT * (i + 1))
                            wait(pe, m.so_ok, TT * i)
                        wait(pe, m.ot_ok, HP * i + k - 1)
                        for t in range(TT):
                            for h in range(2):
                                c = D1 * (2 * k + h)
                                mm = pe.matmul(o_ps[D1 * h:D1 * (h + 1), k % 2, P * t:P * (t + 1)],
                                               v[:, t, c:c + D1], pt[k % 2][:, h, t, :], start=True, stop=True)
                        mm.then_inc(m.o_psum, 1)

                def w_bank(t):
                    return (fin, pr[:, through_pr.index(("W", 1)) % 2, :], pr[:, through_pr.index(("W", 2)) % 2, :],
                            o_ps[:, 0, :])[t]

                for t in range(TT):
                    if t < KC and not last:
                        transposes(i + 1, t)
                    if t == 3:
                        pe.wait_ge(m.pd_ok, 2 * (i + 1))
                        misc_free()
                        for u in range(TT):
                            mm = pe.transpose(misc[:, u * P:(u + 1) * P], pd[:, u, :, :].rearrange("p h r -> p (h r)"),
                                              ident[:, :])
                        mm.then_inc(m.pd_psum, 1)
                        prev_misc[0] = ("PD", i, 0)
                    if t == 0:
                        if isinstance(i, int) and i == 0:
                            pe.wait_ge(m.g_ok, 3)
                        wait(pe, m.so_ok, TT * i)
                        pe.wait_ge(m.ot_ok, HP * i + HP - 1)
                    if t in (1, 2):
                        free_pr(i, "W", t)
                    for hp in range(HP):
                        if t == 0 and hp == HP - 1:
                            pe.wait_ge(m.ot_ok, HP * (i + 1))
                        pe.matmul(w_bank(t)[:, 0:E], ot[:, hp, t * P:(t + 1) * P], wout[:, hp, :],
                                  start=(hp == 0), stop=False)
                pe.wait_ge(m.pdt_ok, i + 1)
                for t in W_ORDER:
                    pe.matmul(w_bank(t)[:, 0:E], pdt[:, t * P:(t + 1) * P], ud[:, :],
                              start=False, stop=True).then_inc(m.w_psum, 1)

            over_batches(pe, body)

        @block.scalar
        def _(act):
            act.wait_ge(m.w_load, 16)
            for part in (2, 0, 1):
                cols = slice(part * H1 * D1, (part + 1) * H1 * D1)
                act.activation(win_h[:, :, cols], w_in[:, :, cols], ACT.Copy).then_inc(m.w_high, 1)

            act.wait_ge(m.trig, 15)
            act.wait_ge(m.consts_ok, 2)
            act.activation(cs[:, :, 0:E], turns[0], ACT.Sin, scale=-1.0, bias=halfpi[:, 0:1]).then_inc(m.sin_ok, 1)
            act.activation(cs[:, :, E:2 * E], ang[1], ACT.Sin).then_inc(m.sin_ok, 1)
            act.wait_ge(m.sin_ok, 2)
            act.activation(cs_h[:, :, :], cs, ACT.Copy).then_inc(m.cs_high, 1)

            def transposed(i, kc, bank=misc):
                act.wait_ge(m.xt_psum, KC * i + kc + 1)
                if kc == 0:
                    wait(act, m.qk_psum, 2 * HP * i)
                    wait(act, m.f_psum, TT * i)
                    wait(act, m.v_psum, 2 * TT * i)
                    wait(act, m.r_psum, i)
                act.activation(xt[:, kc, :], bank[:, :], ACT.Copy)
                act.activation(xt_h[:, kc, :], bank[:, :], ACT.Copy).then_inc(m.xt_high, 1)

            for kc in range(KC):
                transposed(0, kc, (misc, fin)[kc])
            act.wait_ge(m.g_psum, 1)
            act.activation(gk[:, :, :, :].rearrange("p k h r -> p (k h r)"), o_ps[:, 0, 0:KC * P], ACT.Copy).then_inc(m.g_ok, 1)
            act.activation(beta[:, :, :].rearrange("p h r -> p (h r)"), o_ps[:, 1, 0:P], ACT.Copy).then_inc(m.g_ok, 1)
            act.wait_ge(m.w_low, 3)

            def exp_pair(i, k):
                act.wait_ge(m.sub_ok, HP * i + k + 1)
                wait(act, m.pt_ok, 4 * (HP * i + k - 1))
                act.activation(ex[:, k % 2, :, :, :], sc[:, k % 2, :, :, :], ACT.Exp, scale=D1 ** -0.5).then_inc(m.ex_ok, 1)

            def body(i):
                last = isinstance(i, int) and i >= NT1 - 1
                for kind, k in steps:
                    if isinstance(i, int) and i == 0 and (kind, k) == ("Q", 0):
                        act.wait_ge(m.g_psum, 2)
                        act.activation(ud[:, :], fin[:, 0:E], ACT.Copy).then_inc(m.g_ok, 1)
                    if kind == "V":
                        act.wait_ge(m.v_psum, 2 * TT * i + k + 1)
                        if k == 0:
                            wait(act, m.o_psum, HP * i)
                        c = 512 * (k % 2)
                        act.activation(v[:, k // 2, c:c + 512], pr[:, through_pr.index(("V", k)) % 2, :],
                                       ACT.Copy).then_inc(m.v_ok, 1)
                    if kind in ("Q", "K"):
                        side = int(kind == "K")
                        n = 2 * HP * i + 2 * k + side
                        act.wait_ge(m.qk_psum, n + 1)
                        wait(act, m.s_psum, HP * i + k - 1)
                        bank = pr[:, through_pr.index((kind, k)) % 2, :]
                        act.activation((qt, kt)[side][:, k % 2, :], bank, ACT.Identity,
                                       bias=bqkv[:, HP * side + k:HP * side + k + 1]).then_inc(m.qk_ok, 1)
                    if kind == "F":
                        if k < 2:
                            exp_pair(i, HP - 2 + k)
                        act.wait_ge(m.f_psum, TT * i + k + 1)
                        wait(act, m.q2_ok, TT * i + k - 1)
                        act.activation(sq[:, k % 2, :], pr[:, through_pr.index((kind, k)) % 2, :],
                                       ACT.Square).then_inc(m.sq_ok, 1)
                    if kind == "Q" and k >= 2:
                        exp_pair(i, k - 2)
                    if kind == "AV":
                        act.wait_ge(m.o_psum, HP * i + k + 1)
                        if k == 0:
                            wait(act, m.w_psum, TT * i)
                        act.activation(ot[:, k, :], o_ps[:, k % 2, :], ACT.Identity,
                                       bias=bqkv[:, 2 * HP + k:2 * HP + k + 1]).then_inc(m.ot_ok, 1)
                if not last:
                    for kc in range(KC):
                        transposed(i + 1, kc)
                act.wait_ge(m.q2_ok, TT * (i + 1))
                wait(act, m.gate_ok, i)
                act.activation(q2[:, :, :], q2[:, :, :], ACT.Sqrt).then_inc(m.sqrt_ok, 1)
                act.wait_ge(m.sqrt_ok, i + 1)
                act.activation(th[:, :, :], q2[:, :, :], ACT.Tanh, scale=0.5).then_inc(m.tanh_ok, 1)
                act.wait_ge(m.pd_psum, i + 1)
                act.activation(pdt[:, :], misc[:, :], ACT.Copy).then_inc(m.pdt_ok, 1)

            over_batches(act, body)

        @block.vector
        def _(dve):
            dve.memset(mhalf[:, :], -0.5).then_inc(m.consts_ok, 1)
            dve.memset(halfpi[:, :], float(np.pi / 2)).then_inc(m.consts_ok, 1)
            def norm_stats(i):
                dve.wait_ge(m.x_load, 16 * (i + 1))
                for t in range(TT):
                    dve.bn_stats(stat[:, t, :], xb[:, t, :]).then_inc(m.stats, 1)
                dve.wait_ge(m.stats, TT * (i + 1))
                wait(dve, m.veps_ok, i)
                stand_alone(dve, m.dve_passed)
                for t in range(TT):
                    dve.bn_aggr(mv[:, t, :], stat[:, t, :]).then_inc(m.aggr, 1)

            def normalise(i):
                dve.wait_ge(m.rstd_ok, i + 1)
                wait(dve, m.xt_psum, KC * i)
                for t in range(TT):
                    ins = dve.tensor_scalar(xn[:, t, :], xb[:, t, :], mv[:, t, 0:1], rstd[:, t:t + 1],
                                            ALU.subtract, ALU.mult)
                ins.then_inc(m.xn_ok, 1)

            def low_parts(i, kc, bank=misc):
                dve.wait_ge(m.xt_high, KC * i + kc + 1)
                dve.tensor_tensor(xt_l[:, kc, :], bank[:, :], xt_h[:, kc, :].bitcast(F32),
                                  ALU.subtract).then_inc(m.xt_low, 1)

            def key_distances(i):
                dve.wait_ge(m.r_psum, i + 1)
                wait(dve, m.r_sum, 2 * NREL * i)
                dve.tensor_tensor(r15[:, :, :, NREL - 1:].rearrange("p h t r -> p t h r"),
                                  misc[:, :].rearrange("p (t h r) -> p t h r", t=TT, h=H1),
                                  beta[:, :, :].unsqueeze(1).to_broadcast([P, TT, H1, NREL]), ALU.add).then_inc(m.r_evac, 1)
                dve.wait_ge(m.r_evac, i + 1)
                dve.tensor_copy(r15[:, :, :, 0:NREL - 1], r15[:, :, :, 2 * NREL - 2:NREL - 1:-1]).then_inc(m.r_flip, 1)

            def own_keys(i, half, s):
                heads = slice(half * HP, (half + 1) * HP)
                src, dst = r15[:, heads, :, NREL - 1 - s:2 * NREL - 1 - s], rt[:, heads, :, :]
                if s == 0:
                    dve.wait_ge(m.r_flip, i + 1)
                    wait(dve, m.rm_ok, TT * i)
                    dve.tensor_scalar(dst, src, own[:, 0:1], None, ALU.mult).then_inc(m.r_sum, 1)
                else:
                    dve.wait_ge(m.r_sum, NREL * (2 * i + half) + s)
                    dve.scalar_tensor_tensor(dst, src, own[:, s:s + 1], dst,
                                             op0=ALU.mult, op1=ALU.add).then_inc(m.r_sum, 1)

            def scores(i, k):
                n = HP * i + k
                dve.wait_ge(m.s_psum, n + 1)
                wait(dve, m.ex_ok, n - 1)
                if k % 2 == 0:
                    dve.wait_ge(m.rm_ok, 4 * i + k // 2 + 1)
                a = sc[:, k % 2, :, :, :]
                dve.tensor_tensor(a, s_ps[:, :, 0:TT * BLK].rearrange("p h (t k) -> p h t k", t=TT),
                                  rm[:, 2 * k:2 * k + 2, :, :], ALU.add).then_inc(m.sc_ok, 1)
                dve.wait_ge(m.sc_ok, n + 1)
                dve.tensor_reduce(mx[:, k % 2, :, :], a, X, ALU.max).then_inc(m.mx_ok, 1)

            def key_sums(i, k):
                n = HP * i + k
                e = ex[:, k % 2, :, :, :]
                dve.wait_ge(m.ex_ok, n + 1)
                wait(dve, m.pc_ok, n - 1)
                dve.tensor_reduce(ec[:, k % 2, :, :, :].rearrange("p h t s -> p (h t) s"),
                                  e.rearrange("p h t (n s) -> p (h t) s n", n=4), X, ALU.add).then_inc(m.ec_ok, 1)
                dve.wait_ge(m.ec_ok, n + 1)
                dve.tensor_reduce(sm[:, k % 2, :, :], ec[:, k % 2, :, :, :], X, ALU.add).then_inc(m.sm_ok, 1)
                dve.wait_ge(m.sm_ok, n + 1)
                wait(dve, m.p_ok, n - 1)
                dve.reciprocal(rc[:, k % 2, :, :], sm[:, k % 2, :, :]).then_inc(m.rc_ok, 1)
                dve.wait_ge(m.rc_ok, n + 1)
                if k == 0:
                    wait(dve, m.p15_sum, 2 * NREL * i)
                dve.tensor_tensor(pc[:, 2 * k:2 * k + 2, :, :], ec[:, k % 2, :, :, :],
                                  rc[:, k % 2, :, :].unsqueeze(3).to_broadcast([P, 2, TT, NREL]), ALU.mult).then_inc(m.pc_ok, 1)

            def transposed_blocks(i, k):
                n = HP * i + k
                e = ex[:, k % 2, :, :, :]
                dve.wait_ge(m.p_ok, n + 1)
                wait(dve, m.o_psum, n - 1)
                for q in range(4):
                    rows = slice(BLK * q, BLK * (q + 1))
                    dve.transpose(pt[k % 2][rows, :, :, :].rearrange("p h t k -> p (h t) k")[:, :, rows],
                                  e[rows, :, :, :].rearrange("p h t k -> p (h t) k")).then_inc(m.pt_ok, 1)

            def by_distance(i, half, batches):
                heads = slice(half * HP, (half + 1) * HP)
                n = NREL * (2 * i + half)
                if half == 0 and 0 in batches:
                    dve.wait_ge(m.p15_zero, i + 1)
                dve.wait_ge(m.pc_ok, HP * i + HP // 2 * (half + 1))
                for s in batches:
                    wait(dve, m.p15_sum, n + s)
                    dst = p15[:, heads, :, NREL - 1 - s:2 * NREL - 1 - s]
                    dve.scalar_tensor_tensor(dst, pc[:, heads, :, :], own[:, s:s + 1], dst,
                                             op0=ALU.mult, op1=ALU.add).then_inc(m.p15_sum, 1)

            def distances(i):
                dve.wait_ge(m.p15_sum, 2 * NREL * (i + 1))
                wait(dve, m.pd_psum, i)
                by_head = pd[:, :, :, :].rearrange("p t h r -> p h t r")
                dve.tensor_copy(by_head[:, :, :, 0:1], p15[:, :, :, NREL - 1:NREL]).then_inc(m.pd_ok, 1)
                dve.tensor_tensor(by_head[:, :, :, 1:], p15[:, :, :, NREL:], p15[:, :, :, NREL - 2::-1], ALU.add).then_inc(m.pd_ok, 1)

            def read_output(i, n):
                t = W_ORDER[n]
                dve.wait_ge(m.w_psum, TT * i + n + 1)
                if n < 2:
                    wait(dve, m.stored[n], 16 * 2 * i)
                else:
                    dve.wait_ge(m.stored[n % 2], 16 * (2 * i + 1))
                bank = (fin, pr[:, through_pr.index(("W", 1)) % 2, :], pr[:, through_pr.index(("W", 2)) % 2, :],
                        o_ps[:, 0, :])[t]
                dve.tensor_tensor(so[:, n % 2, :], bank[:, 0:E], bout[:, :], ALU.add).then_inc(m.so_ok, 1)

            def gate_output(i, n):
                t = W_ORDER[n]
                dve.wait_ge(m.so_ok, TT * i + n + 1)
                dve.scalar_tensor_tensor(so[:, n % 2, :], so[:, n % 2, :], 0.5, q2[:, t, :], op0=ALU.mult,
                                         op1=ALU.mult).then_inc(m.sg_ok, 1)
                dve.wait_ge(m.sg_ok, TT * i + n + 1)
                if n == 0:
                    dve.wait_ge(m.xr_load, 16 * (i + 1))
                dve.tensor_tensor(so[:, n % 2, :], so[:, n % 2, :], xr[:, t, :], ALU.add).then_inc(m.x2_ok, 1)

            def low_weights(n, part):
                dve.wait_ge(m.w_high, n + 1)
                cols = slice(part * H1 * D1, (part + 1) * H1 * D1)
                dve.tensor_tensor(win_l[:, :, cols], w_in[:, :, cols], win_h[:, :, cols].bitcast(F32),
                                  ALU.subtract).then_inc(m.w_low, 1)

            dve.wait_ge(m.b_load, 16 * BLOADS)
            for hp in range(HP):
                dve.tensor_scalar(kdb[:, hp, :], kdx[:, :, :].rearrange("p a b -> p (a b)"), bqkv[:, hp:hp + 1], None,
                                  ALU.mult).then_inc(m.kdb_ok, 1)
            low_weights(0, 2)
            norm_stats(0)
            low_weights(1, 0)
            normalise(0)
            for kc in range(KC):
                low_parts(0, kc, (misc, fin)[kc])
            low_weights(2, 1)
            dve.wait_ge(m.cs_high, 1)
            dve.tensor_tensor(cs_l[:, :, :], cs, cs_h[:, :, :].bitcast(F32), ALU.subtract).then_inc(m.cs_low, 1)
            dve.wait_ge(m.g_ok, 2)
            dve.wait_ge(m.bout_load, 16)

            def body(i):
                last = isinstance(i, int) and i >= NT1 - 1
                key_distances(i)
                for half in range(2):
                    for s in range(NREL):
                        own_keys(i, half, s)
                for k in range(HP):
                    if k >= 1:
                        key_sums(i, k - 1)
                    scores(i, k)
                    if k >= 1:
                        transposed_blocks(i, k - 1)
                    if k == 1 and not last:
                        norm_stats(i + 1)
                    if k == 3 and not last:
                        normalise(i + 1)
                    if k >= 4:
                        by_distance(i, 0, ((0, 1, 2), (3, 4, 5), (6,), (7,))[k - 4])
                key_sums(i, HP - 1)
                transposed_blocks(i, HP - 1)
                if not last:
                    low_parts(i + 1, 0)
                by_distance(i, 1, range(NREL))
                distances(i)
                if not last:
                    low_parts(i + 1, 1)
                dve.wait_ge(m.tanh_ok, i + 1)
                dve.scalar_tensor_tensor(q2[:, :, :], th[:, :, :], 1.0, q2[:, :, :], op0=ALU.add,
                                         op1=ALU.mult).then_inc(m.gate_ok, 1)
                dve.wait_ge(m.gate_ok, i + 1)
                for n in (0, 2):
                    read_output(i, n)
                    read_output(i, n + 1)
                    gate_output(i, n)
                    gate_output(i, n + 1)

            over_batches(dve, body)

        @block.gpsimd
        def _(pool):
            for i in range(2):
                pool.memset(pt[i][:, :, :, :], 0.0).then_inc(m.zero_pt, 1)
                pool.wait_ge(m.zero_pt, i + 1)
            pool.wait_ge(m.consts_ok, 2)
            pool.wait_ge(m.x_load, 16)

            def rstd_of(i):
                pool.wait_ge(m.aggr, TT * (i + 1))
                wait(pool, m.xn_ok, i)
                stand_alone(pool, m.pool_passed)
                pool.tensor_scalar(veps[:, :], mv[:, :, 1], LN_EPS, None, ALU.add).then_inc(m.veps_ok, 1)
                pool.wait_ge(m.veps_ok, i + 1)
                pool.tensor_tensor(rstd[:, :], veps[:, :], mhalf[:, :], ALU.pow).then_inc(m.rstd_ok, 1)

            def less_maximum(i, k):
                pool.wait_ge(m.mx_ok, HP * i + k + 1)
                pool.tensor_tensor(sc[:, k % 2, :, :, :], sc[:, k % 2, :, :, :],
                                   mx[:, k % 2, :, :].unsqueeze(3).to_broadcast([P, 2, TT, BLK]),
                                   ALU.subtract).then_inc(m.sub_ok, 1)

            def weigh(i, k):
                pool.wait_ge(m.rc_ok, HP * i + k + 1)
                pool.tensor_tensor(ex[:, k % 2, :, :, :], ex[:, k % 2, :, :, :],
                                   rc[:, k % 2, :, :].unsqueeze(3).to_broadcast([P, 2, TT, BLK]),
                                   ALU.mult).then_inc(m.p_ok, 1)

            rstd_of(0)
            pool.wait_ge(m.b_load, 16 * BLOADS)
            pool.wait_ge(m.w_low, 3)

            def body(i):
                last = isinstance(i, int) and i >= NT1 - 1
                wait(pool, m.sc_ok, HP * i)
                for g in range(4):
                    if g % 2 == 0:
                        pool.wait_ge(m.r_sum, NREL * (2 * i + g // 2 + 1))
                    heads = slice(4 * g, 4 * (g + 1))
                    pool.tensor_tensor(
                        rm[:, heads, :, :].rearrange("p h t (n s) -> p (h t) n s", n=4),
                        rt[:, heads, :, :].rearrange("p h t s -> p (h t) s").unsqueeze(2).to_broadcast([P, 4 * TT, 4, NREL]),
                        apart[:, :].rearrange("p (n s) -> p n s", n=4).unsqueeze(1).to_broadcast([P, 4 * TT, 4, NREL]),
                        ALU.add).then_inc(m.rm_ok, 1)
                wait(pool, m.pd_ok, 2 * i)
                stand_alone(pool, m.pool_passed)
                pool.memset(p15[:, :, :, :], 0.0).then_inc(m.p15_zero, 1)
                for k in range(HP):
                    if k >= 1:
                        weigh(i, k - 1)
                    less_maximum(i, k)
                    if k == 2 and not last:
                        rstd_of(i + 1)
                weigh(i, HP - 1)
                for t in range(TT):
                    pool.wait_ge(m.sq_ok, TT * i + t + 1)
                    if t == 0:
                        wait(pool, m.x2_ok, TT * i)
                    pool.tensor_tensor(q2[:, t, :], sq[:, t % 2, 0:E], sq[:, t % 2, E:2 * E], ALU.add).then_inc(m.q2_ok, 1)

            over_batches(pool, body)


def layout1(a):
    kd, vd = a["L1_attn_k_dist_emb"][:NREL], a["L1_attn_v_dist_emb"][:NREL]
    kdx = np.zeros((2, D1, 2, NREL), np.float32)
    vdx = np.zeros((2, D1, HP, H1, NREL), np.float32)
    for h in range(2):
        kdx[h, :, h, :] = kd.T
        for hp in range(HP):
            vdx[h, :, hp, 2 * hp + h, :] = vd.T
    p = np.arange(P)
    key = np.arange(BLK)
    out = {
        "win": a["L1_attn_W_in"].T,
        "wqn": a["L1_attn_W_in"][:H1 * D1],
        "bqkv": a["L1_attn_b_in"].reshape(3 * HP, P).T,
        "kdx": kdx.reshape(P, 2, NREL),
        "vdx": vdx.reshape(P, HP, H1 * NREL),
        "wout": a["L1_attn_W_out"].T,
        "bout": a["L1_attn_b_out"],
        "theta": a["L1_ffn_theta"], "phi": a["L1_ffn_phi"],
        "theta_noise": a["L1_ffn_theta_noise"], "phi_noise": a["L1_ffn_phi_noise"],
        "apart": np.where((p[:, None] % BLK) // NREL == key[None, :] // NREL, 0.0, NEG).astype(np.float32),
        "own": (p[:, None] % NREL == np.arange(NREL)[None, :]).astype(np.float32),
        "ones": np.ones((P, P), np.float32),
    }
    return {k: np.ascontiguousarray(v) for k, v in out.items()}


def layout0(a):
    def halves(w):
        return w.reshape(2, HG, 2, F0, E).transpose(4, 0, 2, 1, 3).reshape(E, HALF, HG * F0)

    pick = np.zeros((P, HALF, BLK), np.float32)
    which = np.zeros((2, HG, HG, S), np.float32)
    for i in range(HALF):
        pick[:, i, i] = 1.0
        which[:, i, i, :] = 1.0
    out = {
        "x": a["L0_attn_x"],
        "wqk": np.concatenate([halves(a["L0_attn_Wq"]), halves(a["L0_attn_Wk"])], axis=2),
        "wcat": np.concatenate([a["L0_attn_Wv"].T, a["L0_ffn_w_route"].T, a["L0_ffn_compress"].T], axis=1),
        "wo": a["L0_attn_Wo"].T,
        "normw": a["L0_attn_norm_w"].reshape(KC, P).T,
        "bo": a["L0_attn_bo"],
        "dw": a["L0_attn_diff_weight"].reshape(1),
        "routed": a["L0_ffn_routed"].transpose(0, 2, 1).reshape(NE * R, E),
        "ident": np.eye(P, dtype=np.float32),
        "rank8": np.arange(NE, 0, -1, dtype=np.float32),
        "pick": pick,
        "which": which.reshape(MROWS, HG, S),
    }
    return {k: np.ascontiguousarray(v) for k, v in out.items()}


def build(nc, io0, io1, out):
    x1 = nc.dram_tensor("x1", [S, B, E], F32).ap()
    with ExitStack() as ctx:
        shared = Shared(nc, ctx)
        layer0(nc, io0, io1, shared, x1)
        layer1(nc, io1, shared, x1, out)


def kernel(**inputs):
    import concourse.bacc as bacc
    from concourse.bass_utils import run_bass_kernel_spmd as run

    nc = bacc.Bacc("TRN2", target_bir_lowering=False, num_devices=1)
    a = {k: np.asarray(v) for k, v in inputs.items()}
    arrays, io = {}, []
    for layer, layout in enumerate((layout0, layout1)):
        io.append({})
        for k, v in layout(a).items():
            arrays[f"in{layer}_{k}"] = v
            io[-1][k] = nc.dram_tensor(f"in{layer}_{k}", v.shape, mybir.dt.from_np(v.dtype), kind="ExternalInput").ap()
    out = nc.dram_tensor("out", [S, B, E], F32, kind="ExternalOutput").ap()
    build(nc, *io, out)
    r = run(nc, [arrays], core_ids=[0])
    return np.ascontiguousarray(r.results[0]["out"].transpose(1, 0, 2))
```
